# Optimizing a Trainium2 kernel written in Bass

```python
import numpy as np
import jax
import jax.numpy as jnp

def _softmax(x, axis=-1):
    return jax.nn.softmax(x, axis=axis)

def _gelu(x):
    return jax.nn.gelu(x, approximate=True)

def _silu(x):
    return jax.nn.silu(x)

def _sigmoid(x):
    return jax.nn.sigmoid(x)

def _layernorm(x, axis=-1, eps=1e-05):
    m = jnp.mean(x, axis=axis, keepdims=True)
    v = jnp.var(x, axis=axis, keepdims=True)
    return (x - m) / jnp.sqrt(v + eps)

def _scatter_add(tgt, idx, src, axis=0):
    return tgt.at[idx].add(src)

def _segment_sum(src, seg, n):
    return jax.ops.segment_sum(src, seg, n)
kernel_name = 'mk_adaln_d1_jaxref_r4_24379b'

def setup_inputs(seed: int=0):
    np.random.seed(seed)
    _w = jnp.asarray

    def _L0_attn_setup():
        import jax, jax.numpy as jnp
        import numpy as np
        H = 1024
        D = H // 4
        key = jax.random.key(seed)
        k1, k2, k3, k4, k5 = jax.random.split(key, 5)
        x = jax.random.normal(k1, (4, 1024, H), dtype=jnp.float32)
        s_in = 1.0 / np.sqrt(H)
        Wqkv = jax.random.normal(k2, (H, 3 * D), dtype=jnp.float32) * s_in
        bqkv = jax.random.normal(k3, (3 * D,), dtype=jnp.float32) * 0.01
        Wo = jax.random.normal(k4, (D, H), dtype=jnp.float32) * (1.0 / np.sqrt(D))
        bo = jax.random.normal(k5, (H,), dtype=jnp.float32) * 0.01
        return {'x': x, 'Wqkv': Wqkv, 'bqkv': bqkv, 'Wo': Wo, 'bo': bo}
    _L0_attn_in = _L0_attn_setup()

    def _L0_ffn_setup():
        import jax, jax.numpy as jnp
        import numpy as np
        LORA_RANK = 16
        LORA_ALPHA = 16
        LORA_SCALE = LORA_ALPHA / LORA_RANK
        key = jax.random.key(seed)
        k1, k2, k3, k4, k5 = jax.random.split(key, 5)
        B, S, D_IN, D_OUT, N_LORA, R = (8, 512, 1024, 1024, 3, LORA_RANK)
        std = 1.0 / np.sqrt(D_IN)
        x = jax.random.normal(k1, (B, S, D_IN), dtype=jnp.float32)
        weight = jax.random.truncated_normal(k2, -3.0, 3.0, (D_OUT, D_IN), dtype=jnp.float32) * std
        bias = jax.random.normal(k3, (D_OUT,), dtype=jnp.float32) * 0.01
        lora_A = jax.random.normal(k4, (N_LORA, R, D_IN), dtype=jnp.float32) * std
        lora_B = jax.random.normal(k5, (N_LORA, D_OUT, R), dtype=jnp.float32) * 0.02
        lora_start_indices = jnp.arange(4, dtype=jnp.int64) * 2
        return {'x': x, 'weight': weight, 'bias': bias, 'lora_A': lora_A, 'lora_B': lora_B, 'lora_start_indices': lora_start_indices}
    _L0_ffn_in = _L0_ffn_setup()
    _L0_c = _w((lambda *s: np.random.randn(*s).astype(np.float32) * 0.05)(4, 1024))
    _L0_wmod = _w((lambda *s: np.random.randn(*s).astype(np.float32) * 0.05)(1024, 6 * 1024) * 1024 ** (-0.5))
    _d = {'L0_attn_x': _L0_attn_in['x'], 'L0_attn_Wqkv': _L0_attn_in['Wqkv'], 'L0_attn_bqkv': _L0_attn_in['bqkv'], 'L0_attn_Wo': _L0_attn_in['Wo'], 'L0_attn_bo': _L0_attn_in['bo'], 'L0_ffn_weight': _L0_ffn_in['weight'], 'L0_ffn_bias': _L0_ffn_in['bias'], 'L0_ffn_lora_A': _L0_ffn_in['lora_A'], 'L0_ffn_lora_B': _L0_ffn_in['lora_B'], 'L0_ffn_lora_start_indices': _L0_ffn_in['lora_start_indices'], 'L0_c': _L0_c, 'L0_wmod': _L0_wmod}
    _x0 = _d['L0_attn_x']
    _d['L0_attn_x'] = jax.random.normal(jax.random.fold_in(jax.random.key(seed), 1), (4, 1024, 1024), dtype=_x0.dtype)
    del _x0
    return _d

def reference(L0_attn_x, L0_attn_Wqkv, L0_attn_bqkv, L0_attn_Wo, L0_attn_bo, L0_ffn_weight, L0_ffn_bias, L0_ffn_lora_A, L0_ffn_lora_B, L0_ffn_lora_start_indices, L0_c, L0_wmod):

    def _L0_attn_ref(x, Wqkv, bqkv, Wo, bo):
        import jax, jax.numpy as jnp
        import numpy as np
        H = 1024
        D = H // 4
        B, S, C = x.shape
        d = C // 4
        qkv = jnp.einsum('bsc,cf->bsf', x, Wqkv) + bqkv
        qkv = qkv.reshape(B, S, 3, d)
        q, k, v = (qkv[:, :, 0], qkv[:, :, 1], qkv[:, :, 2])
        scale = 1.0 / jnp.sqrt(jnp.float32(d)).astype(x.dtype)
        attn = jnp.einsum('bqd,bkd->bqk', q, k) * scale
        attn = jax.nn.softmax(attn, axis=-1)
        out = jnp.einsum('bqk,bkd->bqd', attn, v)
        return jnp.einsum('bqd,dc->bqc', out, Wo) + bo

    def _L0_ffn_ref(x, weight, bias, lora_A, lora_B, lora_start_indices):
        import jax, jax.numpy as jnp
        import numpy as np
        LORA_RANK = 16
        LORA_ALPHA = 16
        LORA_SCALE = LORA_ALPHA / LORA_RANK
        y = jnp.einsum('bsd,od->bso', x, weight) + bias
        B = x.shape[0]
        seg = jnp.searchsorted(lora_start_indices, jnp.arange(B), side='right') - 1
        adapter_idx = jnp.clip(seg - 1, 0, lora_A.shape[0] - 1)
        A = lora_A[adapter_idx]
        Bw = lora_B[adapter_idx]
        lo = jnp.einsum('bsr,bor->bso', jnp.einsum('bsd,brd->bsr', x, A), Bw) * LORA_SCALE
        use_lora = (seg > 0)[:, None, None]
        return y + jnp.where(use_lora, lo, jnp.zeros((), dtype=y.dtype))
    x = L0_attn_x
    mod = (_silu(L0_c) @ L0_wmod).reshape(L0_c.shape[0], 6, 1, -1)
    sa, ca, ga, sb, cb, gb = (mod[:, 0], mod[:, 1], mod[:, 2], mod[:, 3], mod[:, 4], mod[:, 5])
    ga = (2 * (ga >= 0) - 1) * jnp.maximum(jnp.abs(ga), 0.25)
    gb = (2 * (gb >= 0) - 1) * jnp.maximum(jnp.abs(gb), 0.25)
    h = _layernorm(x, axis=-1) * (1 + ca) + sa
    x = x + ga * _L0_attn_ref(h, L0_attn_Wqkv, L0_attn_bqkv, L0_attn_Wo, L0_attn_bo)
    h = _layernorm(x, axis=-1) * (1 + cb) + sb
    x = x + gb * _L0_ffn_ref(h, L0_ffn_weight, L0_ffn_bias, L0_ffn_lora_A, L0_ffn_lora_B, L0_ffn_lora_start_indices)
    return x

_drawn_inputs = setup_inputs


def setup_inputs(seed=0):
    import zlib

    import numpy as np

    out = dict(_drawn_inputs(seed))
    spreads = {}
    factors = {'L0_attn_Wqkv': 3.772,
     'L0_attn_bqkv': 8.0,
     'L0_attn_Wo': 3.732,
     'L0_attn_bo': 64.0,
     'L0_ffn_bias': 64.0,
     'L0_ffn_lora_A': 4.094,
     'L0_ffn_lora_B': 4.12}
    for name, (base, spread) in spreads.items():
        noise = np.random.default_rng([zlib.crc32(name.encode()), seed]).standard_normal(out[name].shape)
        drawn = base * np.exp(spread * noise) if base else spread * noise
        out[name] = jnp.asarray(drawn.astype(out[name].dtype))
    for name, factor in factors.items():
        out[name] = (out[name] * factor).astype(out[name].dtype)
    return out
```

```python
from contextlib import ExitStack

import numpy as np

import concourse.bass as bass
from concourse import mybir

F32 = mybir.dt.float32
F32R = mybir.dt.float32r
I32 = mybir.dt.int32
ALU = mybir.AluOpType
ACT = mybir.ActivationFunctionType
AX_X = mybir.AxisListType.X

P = 128
B, S, H = 4, 1024, 1024
D = H // 4
CT = H // P
DT = D // P
BANK = 512
CHUNK = 512
QT = S // P
MODS = 6
SA, CA, GA, SB, CB, GB = range(MODS)
NL, RANK = 3, 16
LO_ROW = 64
WM = 7
EPS = 1e-5
SCALE = float(D) ** -0.5
LAST = B - 1


def host_constants():
    sel = np.zeros((P, B), np.float32)
    for q in range(4):
        for b in range(B):
            sel[32 * q + b, b] = 1
    pick = np.zeros((2, P, P), np.float32)
    which = np.full((P, 1), -1, np.float32)
    for part in range(2):
        for n in range(NL):
            for r in range(RANK):
                row = LO_ROW * part + RANK * n + r
                which[row, 0] = n + 2
                for side, order in enumerate([(0, 1, 0), (0, 0, 1)]):
                    for block, want in enumerate(order):
                        if want == part:
                            pick[side, row, 32 * block + r] = 1
    return {"ident": np.eye(P, dtype=np.float32), "sel": sel, "pick": pick, "which": which}


FIRST = [
    ("turn_c", (), "A", None), ("turn_lora", (), "B", None), ("stats", (0, 0)), ("mod", (0, CA), "D", None),
    ("mod_turn", (0, CA), "D", ("mod", (0, CA), 0)), ("mod", (1, SA), "D", ("mod_turn", (0, CA), 0)),
    ("mod_turn", (1, SA), "D", ("mod", (1, SA), 0)), ("norm", (0, 0)),
    ("T", (0, 0, 0), "A", ("turn_c", (), 0)), ("T", (0, 0, 1), "B", ("turn_lora", (), 0)),
    ("stats", (0, 1)), ("w_split", (0,)), ("w_split", (1,)), ("norm", (0, 1)),
    ("T", (0, 1, 0), "A", ("T", (0, 0, 0), 0)), ("T", (0, 1, 1), "B", ("T", (0, 0, 1), 0)),
    ("w_split", (2,)), ("w_split", (3,)), ("stats", (1, 0)), ("Q", (0,), "C", None), ("norm", (1, 0)),
    ("T", (1, 0, 0), "A", ("T", (0, 1, 0), 0)), ("T", (1, 0, 1), "B", ("T", (0, 1, 1), 0)),
    ("stats", (1, 1)), ("mod", (2, GA), "D", ("mod_turn", (1, SA), 0)),
    ("K", (0,), "A", ("T", (1, 0, 0), 0)), ("norm", (1, 1)),
    ("mod_turn", (2, GA), "D", ("mod", (2, GA), 0)), ("T", (1, 1, 0), "B", ("T", (1, 0, 1), 0)),
    ("T", (1, 1, 1), "C", ("Q", (0,), 0)), ("mod", (3, SB), "D", ("mod_turn", (2, GA), 0)),
    ("V", (0,), "B", ("T", (1, 1, 0), 0)), ("mod_turn", (3, SB), "D", ("mod", (3, SB), 0)),
    ("mod", (4, CB), "D", ("mod_turn", (3, SB), 0)), ("Q", (1,), "A", ("K", (0,), 0)),
    ("mod_turn", (4, CB), "D", ("mod", (4, CB), 0)), ("mod", (5, GB), "D", ("mod_turn", (4, CB), 0)),
    ("K", (1,), "B", ("V", (0,), 0)), ("mod_turn", (5, GB), "D", ("mod", (5, GB), 0)),
    ("turn_wo", (), "D", ("mod_turn", (5, GB), 0)), ("gates", ()), ("gate", (), "D", ("turn_wo", (), 0)),
    ("V", (1,), "C", ("T", (1, 1, 1), 0)), ("wo_lo", ()), ("row", (), "D", ("gate", (), 0)),
]

ATTENTION = [
    ("S", (0,), "A", ("Q", (1,), -1)), ("S", (1,), "B", ("K", (1,), -1)), ("stats", (0, 0)), ("radd", (0,)),
    ("radd", (1,)), ("S", (2,), "A", ("S", (0,), 0)), ("PT", (0,), "C", ("V", (1,), -1)), ("norm", (0, 0)),
    ("S", (3,), "B", ("S", (1,), 0)), ("PT", (1,), "C", ("PT", (0,), 0)),
    ("T", (0, 0, 0), "D", ("row", (), -1)), ("S", (4,), "A", ("S", (2,), 0)),
    ("PT", (2,), "C", ("PT", (1,), 0)), ("T", (0, 0, 1), "D", ("T", (0, 0, 0), 0)),
    ("PT", (3,), "C", ("PT", (2,), 0)), ("S", (5,), "B", ("S", (3,), 0)), ("PV", (0,), "A", ("S", (4,), 0)),
    ("stats", (0, 1)), ("S", (6,), "B", ("S", (5,), 0)), ("PT", (4,), "C", ("PT", (3,), 0)),
    ("norm", (0, 1)), ("S", (7,), "A", ("PV", (0,), 0)), ("PT", (5,), "C", ("PT", (4,), 0)),
    ("O", (0,), "D", ("T", (0, 0, 1), 0)), ("store", (0,)), ("radd", (2,)),
    ("PT", (6,), "C", ("PT", (5,), 0)), ("O", (1,), "B", ("S", (6,), 0)), ("store", (1,)), ("radd", (3,)),
    ("O", (2,), "D", ("O", (0,), 0)), ("store", (2,)), ("radd", (4,)), ("PT", (7,), "C", ("PT", (6,), 0)),
    ("O", (3,), "B", ("O", (1,), 0)), ("store", (3,)), ("radd", (5,)),
    ("T", (0, 1, 0), "D", ("O", (2,), 0)), ("T", (0, 1, 1), "B", ("O", (3,), 0)), ("stats", (1, 0)),
    ("PV", (1,), "A", ("S", (7,), 0)), ("norm", (1, 0)), ("T", (1, 0, 0), "D", ("T", (0, 1, 0), 0)),
    ("T", (1, 0, 1), "C", ("PT", (7,), 0)), ("stats", (1, 1)), ("Q", (0,), "B", ("T", (0, 1, 1), 0)),
    ("O", (4,), "D", ("T", (1, 0, 0), 0)), ("store", (4,)), ("radd", (6,)),
    ("O", (5,), "C", ("T", (1, 0, 1), 0)), ("store", (5,)), ("radd", (7,)), ("norm", (1, 1)),
    ("K", (0,), "A", ("PV", (1,), 0)), ("T", (1, 1, 0), "D", ("O", (4,), 0)),
    ("T", (1, 1, 1), "C", ("O", (5,), 0)), ("O", (6,), "D", ("T", (1, 1, 0), 0)), ("store", (6,)),
    ("O", (7,), "C", ("T", (1, 1, 1), 0)), ("store", (7,)), ("gates", ()), ("V", (0,), "B", ("Q", (0,), 0)),
    ("Q", (1,), "A", ("K", (0,), 0)), ("gate", (), "D", ("O", (6,), 0)), ("K", (1,), "B", ("V", (0,), 0)),
    ("wo_lo", ()), ("row", (), "D", ("gate", (), 0)), ("V", (1,), "C", ("O", (7,), 0)),
]

ENTER_SECOND = [
    ("enter", ()), ("picks", ()), ("gates2", ()), ("pick_a", (), "D", ("O", (6,), LAST)),
    ("pick_b", (), "D", ("pick_a", (), 0)), ("gate2", (), "D", ("pick_b", (), 0)),
    ("row2", (), "D", ("gate2", (), 0)), ("turn_w", (0,), "A", ("PV", (1,), LAST)),
    ("W", (0,), "D", ("row2", (), 0)), ("turn_w", (1,), "B", ("T", (0, 1, 1), LAST)),
    ("W", (1,), "D", ("W", (0,), 0)), ("W_lo", (0,)), ("turn_w", (2,), "A", ("turn_w", (0,), 0)),
    ("W", (2,), "D", ("W", (1,), 0)), ("W_lo", (1,)), ("turn_w", (3,), "B", ("turn_w", (1,), 0)),
    ("W", (3,), "D", ("W", (2,), 0)), ("W_lo", (2,)), ("turn_w", (4,), "A", ("turn_w", (2,), 0)),
    ("W", (4,), "D", ("W", (3,), 0)), ("W_lo", (3,)), ("turn_w", (5,), "B", ("turn_w", (3,), 0)),
    ("W", (5,), "D", ("W", (4,), 0)), ("W_lo", (4,)), ("turn_w", (6,), "A", ("turn_w", (4,), 0)),
    ("W", (6,), "D", ("W", (5,), 0)), ("W_lo", (5,)), ("turn_w", (7,), "B", ("turn_w", (5,), 0)),
    ("W", (7,), "D", ("W", (6,), 0)), ("W_lo", (6,)), ("W_lo", (7,)), ("radd2", (0, 0, 0)),
    ("F", (0, 0, 0, 0), "A", ("turn_w", (6,), 0)), ("F", (0, 0, 0, 1), "A", None),
    ("F", (0, 0, 0, 2), "A", None), ("F", (0, 0, 0, 3), "A", None), ("y_store", (0, 0, 0)),
    ("radd2", (0, 0, 1)), ("F", (0, 0, 1, 0), "B", ("turn_w", (7,), 0)), ("F", (0, 0, 1, 1), "B", None),
    ("F", (0, 0, 1, 2), "B", None), ("F", (0, 0, 1, 3), "B", None), ("y_store", (0, 0, 1)),
    ("radd2", (0, 1, 0)), ("F", (0, 1, 0, 0), "A", ("F", (0, 0, 0), 0)), ("F", (0, 1, 0, 1), "A", None),
    ("F", (0, 1, 0, 2), "A", None), ("F", (0, 1, 0, 3), "A", None), ("y_store", (0, 1, 0)),
    ("radd2", (0, 1, 1)), ("F", (0, 1, 1, 0), "B", ("F", (0, 0, 1), 0)), ("F", (0, 1, 1, 1), "B", None),
    ("F", (0, 1, 1, 2), "B", None), ("F", (0, 1, 1, 3), "B", None), ("y_store", (0, 1, 1)),
]

SECOND = [
    ("stats", (0, 0)), ("picks", ()), ("radd2", (1, 0, 0)), ("F", (1, 0, 0, 0), "A", ("F", (0, 1, 0), -1)),
    ("pick_a", (), "D", ("W", (7,), -1)), ("norm", (0, 0)), ("F", (1, 0, 0, 1), "A", None),
    ("T", (0, 0, 0), "C", ("T", (1, 1, 1), -1)), ("F", (1, 0, 0, 2), "A", None),
    ("pick_b", (), "D", ("pick_a", (), 0)), ("F", (1, 0, 0, 3), "A", None), ("y_store", (1, 0, 0)),
    ("radd2", (1, 0, 1)), ("F", (1, 0, 1, 0), "B", ("F", (0, 1, 1), -1)),
    ("T", (0, 0, 1), "C", ("T", (0, 0, 0), 0)), ("F", (1, 0, 1, 1), "B", None),
    ("F", (1, 0, 1, 2), "B", None), ("F", (1, 0, 1, 3), "B", None), ("stats", (0, 1)),
    ("y_store", (1, 0, 1)), ("radd2", (1, 1, 0)), ("F", (1, 1, 0, 0), "A", ("F", (1, 0, 0), 0)),
    ("W", (0,), "D", ("pick_b", (), 0)), ("F", (1, 1, 0, 1), "A", None), ("W", (1,), "D", ("W", (0,), 0)),
    ("W_lo", (0,)), ("F", (1, 1, 0, 2), "A", None), ("W", (2,), "D", ("W", (1,), 0)), ("W_lo", (1,)),
    ("F", (1, 1, 0, 3), "A", None), ("W", (3,), "D", ("W", (2,), 0)), ("W_lo", (2,)), ("norm", (0, 1)),
    ("y_store", (1, 1, 0)), ("radd2", (1, 1, 1)), ("F", (1, 1, 1, 0), "B", ("F", (1, 0, 1), 0)),
    ("W_lo", (3,)), ("T", (0, 1, 0), "C", ("T", (0, 0, 1), 0)), ("F", (1, 1, 1, 1), "B", None),
    ("T", (0, 1, 1), "C", ("T", (0, 1, 0), 0)), ("gates2", ()), ("F", (1, 1, 1, 2), "B", None),
    ("F", (1, 1, 1, 3), "B", None), ("y_store", (1, 1, 1)), ("stats", (1, 0)),
    ("F", (0, 0, 0, 0), "A", ("F", (1, 1, 0), 0)), ("gate2", (), "D", ("W", (3,), 0)),
    ("F", (0, 0, 0, 1), "A", None), ("row2", (), "D", ("gate2", (), 0)), ("radd2", (0, 0, 0)),
    ("F", (0, 0, 0, 2), "A", None), ("W", (4,), "D", ("row2", (), 0)), ("F", (0, 0, 0, 3), "A", None),
    ("y_store", (0, 0, 0)), ("radd2", (0, 0, 1)), ("F", (0, 0, 1, 0), "B", ("F", (1, 1, 1), 0)),
    ("W", (5,), "D", ("W", (4,), 0)), ("W_lo", (4,)), ("F", (0, 0, 1, 1), "B", None),
    ("W", (6,), "D", ("W", (5,), 0)), ("W_lo", (5,)), ("F", (0, 0, 1, 2), "B", None),
    ("W", (7,), "D", ("W", (6,), 0)), ("W_lo", (6,)), ("F", (0, 0, 1, 3), "B", None), ("W_lo", (7,)),
    ("norm", (1, 0)), ("y_store", (0, 0, 1)), ("radd2", (0, 1, 0)),
    ("F", (0, 1, 0, 0), "A", ("F", (0, 0, 0), 0)), ("T", (1, 0, 0), "C", ("T", (0, 1, 1), 0)),
    ("F", (0, 1, 0, 1), "A", None), ("T", (1, 0, 1), "C", ("T", (1, 0, 0), 0)),
    ("F", (0, 1, 0, 2), "A", None), ("F", (0, 1, 0, 3), "A", None), ("stats", (1, 1)),
    ("y_store", (0, 1, 0)), ("radd2", (0, 1, 1)), ("F", (0, 1, 1, 0), "B", ("F", (0, 0, 1), 0)),
    ("norm", (1, 1)), ("T", (1, 1, 0), "C", ("T", (1, 0, 1), 0)), ("F", (0, 1, 1, 1), "B", None),
    ("T", (1, 1, 1), "C", ("T", (1, 1, 0), 0)), ("F", (0, 1, 1, 2), "B", None),
    ("F", (0, 1, 1, 3), "B", None), ("y_store", (0, 1, 1)),
]

END = [
    ("radd2", (1, 0, 0)), ("F", (1, 0, 0, 0), "A", ("F", (0, 1, 0), -1)), ("F", (1, 0, 0, 1), "A", None),
    ("F", (1, 0, 0, 2), "A", None), ("F", (1, 0, 0, 3), "A", None), ("y_store", (1, 0, 0)),
    ("radd2", (1, 0, 1)), ("F", (1, 0, 1, 0), "B", ("F", (0, 1, 1), -1)), ("F", (1, 0, 1, 1), "B", None),
    ("F", (1, 0, 1, 2), "B", None), ("F", (1, 0, 1, 3), "B", None), ("y_store", (1, 0, 1)),
    ("radd2", (1, 1, 0)), ("F", (1, 1, 0, 0), "A", ("F", (1, 0, 0), 0)), ("F", (1, 1, 0, 1), "A", None),
    ("F", (1, 1, 0, 2), "A", None), ("F", (1, 1, 0, 3), "A", None), ("y_store", (1, 1, 0)),
    ("radd2", (1, 1, 1)), ("F", (1, 1, 1, 0), "B", ("F", (1, 0, 1), 0)), ("F", (1, 1, 1, 1), "B", None),
    ("F", (1, 1, 1, 2), "B", None), ("F", (1, 1, 1, 3), "B", None), ("y_store", (1, 1, 1)),
]

PROJECTIONS = ("Q", "K", "V", "gates", "gate", "row", "wo_lo")
LAST_ATTENTION = [entry for entry in ATTENTION if entry[0] not in PROJECTIONS]


def build_block(nc, x, wqkv, bqkv, wo, bo, w2, bias, lora_a, lora_b, starts, c, wmod,
                k_ident, k_sel, k_pick, k_which, y):
    with ExitStack() as ctx:
        def sb(name, shape, dt=F32, at=ctx):
            return at.enter_context(nc.sbuf_tensor(name, shape, dt))

        def sem(name):
            return ctx.enter_context(nc.semaphore(name))

        x1_dram = nc.dram_tensor("x1_dram", [B * S, H], F32, kind="Internal").ap()
        w2t_dram = nc.dram_tensor("w2t_dram", [2 * CT // 2, P, 2 * BANK], F32, kind="Internal").ap()
        lora_dram = nc.dram_tensor("lora_dram", [2, P, H], F32, kind="Internal").ap()

        pair = {n: ctx.enter_context(nc.psum_tensor(f"pair{n}", [P, 2 * BANK], F32)) for n in "ABCD"}

        ident = sb("ident", [P, P])
        modT = sb("modT", [P, MODS, CT, B])
        boT = sb("boT", [P, CT])
        biasT = sb("biasT", [P, CT])
        bqkvT = sb("bqkvT", [P, 3 * DT])
        picked = sb("picked", [P, B])
        cur = sb("cur", [P, 2, CT])
        gate_col = sb("gate_col", [P, CT])
        row_col = sb("row_col", [P, CT])
        bn = sb("bn", [P, 2, 2, 6])
        mv = sb("mv", [P, 2, 2])
        rstd = sb("rstd", [P, 2, 2])
        power = sb("power", [P, 2])
        eps = sb("eps", [P, 2])
        fence = sb("fence", [P, 1])
        neg_max = sb("neg_max", [P, QT])
        total = sb("total", [P, QT])
        r_total = sb("r_total", [P, QT])
        xs = sb("xs", [P, 2, H])
        affine = sb("affine", [P, 2, 2 * P])
        h_hi, h_lo = [sb("h0_hi", [P, CT, CHUNK], F32R)], [sb("h0_lo", [P, CT, CHUNK], F32R)]
        with ExitStack() as early:
            c_rows = sb("c_rows", [32, H], at=early)
            c_exp = sb("c_exp", [32, H], at=early)
            a_raw = sb("a_raw", [P, H], at=early)
            a_both = sb("a_both", [P, H], F32R, at=early)
            b_raw = sb("b_raw", [P, CT, P], at=early)
            b_both = sb("b_both", [P, H], F32R, at=early)
            start_i = sb("start_i", [P, B], I32, at=early)
            start_f = sb("start_f", [P, B], at=early)
            which = sb("which", [P, 1], at=early)
            le = sb("le", [P, B, B], at=early)
            s1 = sb("s1", [P, B], at=early)
            s2 = sb("s2", [P, B], at=early)
            s3 = sb("s3", [P, B], at=early)
        h_hi.append(sb("h1_hi", [P, CT, CHUNK], F32R))
        h_lo.append(sb("h1_lo", [P, CT, CHUNK], F32R))
        pt_hi, pt_lo = h_hi[1], h_lo[1]
        with ExitStack() as first:
            w_hi = sb("w_hi", [P, CT, 3 * D], F32R, at=first)
            w_lo = sb("w_lo", [P, CT, 3 * D], F32R, at=first)
            with ExitStack() as early:
                wm = sb("wm", [P, WM, H], at=early)
                scT = sb("scT", [P, CT, 32], at=early)
                sel = sb("sel", [P, B], at=early)
                sign = sb("sign", [P, CT * B], at=early)
                size = sb("size", [P, CT * B], at=early)
                mod_rows = sb("mod_rows", [P, H], at=early)
                w_raw = sb("w_raw", [P, CT, 3 * D], at=early)
            wo_hi = sb("wo_hi", [P, DT, H], F32R, at=first)
            wo_lo = sb("wo_lo", [P, DT, H], F32R, at=first)
            probs = sb("probs", [P, 2, S], at=first)
            xr = sb("xr", [P, 2, H], at=first)
            row_bc = sb("row_bc", [P, H], at=first)
            q_hi = sb("q_hi", [P, DT, S], F32R, at=first)
            q_lo = sb("q_lo", [P, DT, S], F32R, at=first)
            k_hi = sb("k_hi", [P, DT, S], F32R, at=first)
            k_lo = sb("k_lo", [P, DT, S], F32R, at=first)
            v_hi = sb("v_hi", [P, QT, D], F32R, at=first)
            v_lo = sb("v_lo", [P, QT, D], F32R, at=first)
        w2_hi = sb("w2_hi", [P, CT, H], F32R)
        w2_lo = sb("w2_lo", [P, CT, H], F32R)
        gate_bc = sb("gate_bc", [P, H])
        row2_bc = sb("row2_bc", [P, H])
        a_stack = sb("a_stack", [P, H], F32R)
        b_stack = sb("b_stack", [P, H], F32R)
        a_used = sb("a_used", [P, H], F32R)
        b_used = sb("b_used", [P, H], F32R)
        pick = sb("pick", [P, 2, P])
        pick_b = sb("pick_b", [P, 2, P], F32R)
        w2t = sb("w2t", [P, 2, 2 * BANK])
        w_sum = sb("w_sum", [P, 2, 2 * BANK])
        res = sb("res", [P, 4, 2 * BANK])
        gated = sb("gated", [P, 2 * BANK])
        w2_rows = gated_alias = None
        w2_rows = res

        ld_const = sem("ld_const")
        ld_c = sem("ld_c")
        ld_lora = sem("ld_lora")
        ld_wm = [sem(f"ld_wm{i}") for i in range(WM)]
        ld_w = [sem(f"ld_w{i}") for i in range(4)]
        ld_xs = [sem(f"ld_xs{i}") for i in range(2)]
        ld_xr = [sem(f"ld_xr{i}") for i in range(2)]
        ld_wo = sem("ld_wo")
        st_x1 = [sem(f"st_x1_{i}") for i in range(2)]
        st_lora = sem("st_lora")
        ld_stack = sem("ld_stack")
        ld_rows = [sem(f"ld_rows{i}") for i in range(2)]
        st_w2t = [sem(f"st_w2t{i}") for i in range(2)]
        ld_w2t = [sem(f"ld_w2t{i}") for i in range(2)]
        ld_res = [sem(f"ld_res{i}") for i in range(4)]
        st_y = [sem(f"st_y{i}") for i in range(4)]
        v_step = sem("v_step")
        g_step = sem("g_step")
        zeroed = sem("zeroed")
        c_expd = sem("c_expd")
        c_silu = sem("c_silu")
        c_turned = sem("c_turned")
        c_ready = sem("c_ready")
        lora_turned = sem("lora_turned")
        lora_hi = sem("lora_hi")
        lora_lo = sem("lora_lo")
        mod_used = sem("mod_used")
        mod_copied = sem("mod_copied")
        mod_turned = sem("mod_turned")
        mod_made = sem("mod_made")
        w_hi_made = sem("w_hi_made")
        w_lo_made = sem("w_lo_made")
        wo_turned = sem("wo_turned")
        wo_row_made = sem("wo_row_made")
        bn_made = sem("bn_made")
        mv_made = sem("mv_made")
        var_eps = sem("var_eps")
        rstd_made = sem("rstd_made")
        x_normed = sem("x_normed")
        h_turned = sem("h_turned")
        h_affine = sem("h_affine")
        h_hi_made = sem("h_hi_made")
        h_lo_made = sem("h_lo_made")
        q_done, k_done, v_done = sem("q_done"), sem("k_done"), sem("v_done")
        q_hi_made, k_hi_made, v_hi_made = sem("q_hi_made"), sem("k_hi_made"), sem("v_hi_made")
        q_lo_made, k_lo_made, v_lo_made = sem("q_lo_made"), sem("k_lo_made"), sem("v_lo_made")
        gates_made = sem("gates_made")
        gate_done = sem("gate_done")
        wo_gated = sem("wo_gated")
        wo_hi_made = sem("wo_hi_made")
        wo_lo_made = sem("wo_lo_made")
        row_done = sem("row_done")
        row_made = sem("row_made")
        s_done = sem("s_done")
        max_made = sem("max_made")
        exp_made = sem("exp_made")
        r_total_made = sem("r_total_made")
        pt_done = sem("pt_done")
        pt_hi_made = sem("pt_hi_made")
        pt_lo_made = sem("pt_lo_made")
        pv_done = sem("pv_done")
        o_hi_made = sem("o_hi_made")
        o_lo_made = sem("o_lo_made")
        o_done = sem("o_done")
        residual_made = sem("residual_made")
        x1_made = sem("x1_made")
        picks_made = sem("picks_made")
        pick_done = sem("pick_done")
        picked_made = sem("picked_made")
        gates2_made = sem("gates2_made")
        gate2_done = sem("gate2_done")
        gate2_made = sem("gate2_made")
        row2_done = sem("row2_done")
        row2_made = sem("row2_made")
        w2_turned = sem("w2_turned")
        w2t_made = sem("w2t_made")
        lora_done = sem("lora_done")
        w_sum_made = sem("w_sum_made")
        w2_hi_made = sem("w2_hi_made")
        w2_lo_made = sem("w2_lo_made")
        f_done = sem("f_done")
        residual2_made = sem("residual2_made")
        y_gated = sem("y_gated")
        y_made = sem("y_made")

        def round_no(stage, b, j, r):
            return 4 * (b + 1) + 2 * j + r + stage * 2 * 2 * B

        def turn_no(stage, b, j, r, half):
            return 2 * round_no(stage, b, j, r) + half

        def f_no(b, j, h, p):
            return QT * (b if j else b + 1) + 4 * j + 2 * h + p

        def wait(eng, s, value):
            if not isinstance(value, int) or value > 0:
                eng.wait_ge(s, value)

        def wait_emptied(eng, before, b, stage):
            if before is None:
                return
            what, i, turn = before
            if turn == LAST:
                b, stage = LAST, 0
            else:
                b = b + turn
            s, value = {
                "turn_c": lambda: (c_ready, 1),
                "turn_lora": lambda: (lora_lo, 2),
                "mod": lambda: (mod_copied, i[0] + 1),
                "mod_turn": lambda: (mod_made, i[0] + 1),
                "turn_wo": lambda: (wo_row_made, 1),
                "T": lambda: (h_affine, 4 * turn_no(stage, b, *i) + 4),
                "Q": lambda: (q_lo_made, 2 * (2 * (b + 1) + i[0]) + 2),
                "K": lambda: (k_lo_made, 2 * (2 * (b + 1) + i[0]) + 2),
                "V": lambda: (v_lo_made, 2 * (b + 1) + i[0] + 1),
                "gate": lambda: (wo_gated, DT * (b + 1) + DT),
                "row": lambda: (row_made, b + 2),
                "S": lambda: (exp_made, QT * b + i[0] + 1),
                "PT": lambda: (pt_lo_made, QT * b + i[0] + 1),
                "PV": lambda: (o_lo_made, 2 * b + i[0] + 1),
                "O": lambda: (x1_made, QT * b + i[0] + 1),
                "pick_a": lambda: (picked_made, 2 * (b + 1) + 1),
                "pick_b": lambda: (picked_made, 2 * (b + 1) + 2),
                "gate2": lambda: (gate2_made, b + 2),
                "row2": lambda: (row2_made, b + 2),
                "turn_w": lambda: (w2t_made, i[0] + 1),
                "W": lambda: (w_sum_made, 8 * (b + 1) + i[0] + 1),
                "F": lambda: (y_gated, f_no(b, *i) + 1),
            }[what]()
            wait(eng, s, value)

        block = ctx.enter_context(nc.Block())

        @block.sync
        def _(sp):
            def load_xs(stage, b, j, r):
                wait(sp, h_turned, turn_no(stage, b, j, r, 0))
                src = x if stage == 0 else x1_dram
                if stage == 1:
                    for i in range(2):
                        wait(sp, st_x1[i], 16 * QT // 2 * (b + 2))
                for i in range(2):
                    row = (b + 1) * S + j * CHUNK + (2 * r + i) * P
                    sp.dma_start(xs[:, i, :], src[bass.ds(row, P), :]).then_inc(ld_xs[i], 16)

            def load_wm(n, q):
                slot, k = n % WM, n % CT
                wait(sp, mod_used, n - WM + 1)
                sp.dma_start(wm[:, slot, :], wmod[k * P:(k + 1) * P, q * H:(q + 1) * H]).then_inc(ld_wm[slot], 16)

            def load_residual(b, t):
                wait(sp, st_x1[t % 2], 16 * (QT // 2 * b + t // 2))
                sp.dma_start(xr[:, t % 2, :], x[bass.ds(b * S + t * P, P), :]).then_inc(ld_xr[t % 2], 16)

            def load_wo(b):
                wait(sp, pt_done, QT * (b + 1))
                sp.dma_start(probs[:, :, :], wo.rearrange("(d p) n -> p d n", p=P)).then_inc(ld_wo, 16)

            sp.dma_start(ident[:, :], k_ident).then_inc(ld_const, 16)
            sp.dma_start(sel[:, :], k_sel).then_inc(ld_const, 16)
            for k in range(WM):
                load_wm(k, CA)
            load_xs(0, -1, 0, 0)
            load_wm(WM, CA)
            for k in range(4):
                load_wm(CT + k, SA)
            for n in range(2):
                sp.dma_start(w_raw[:, 2 * n:2 * n + 2, :], wqkv[2 * n * P:(2 * n + 2) * P, :].rearrange(
                    "(c p) n -> p c n", p=P)).then_inc(ld_w[n], 16)
            for k in range(4, CT):
                load_wm(CT + k, SA)
            for n in range(2, 4):
                sp.dma_start(w_raw[:, 2 * n:2 * n + 2, :], wqkv[2 * n * P:(2 * n + 2) * P, :].rearrange(
                    "(c p) n -> p c n", p=P)).then_inc(ld_w[n], 16)
            load_xs(0, -1, 0, 1)
            load_xs(0, -1, 1, 0)
            for k in range(CT):
                load_wm(2 * CT + k, GA)
                if k == 3:
                    load_xs(0, -1, 1, 1)
            for s, q in ((3, SB), (4, CB), (5, GB)):
                for k in range(CT):
                    load_wm(s * CT + k, q)
            sp.wait_ge(mod_used, MODS * CT)
            load_wo(-1)

            def attention_loads(b, last):
                load_xs(*((1, -1) if last else (0, b)), 0, 0)
                load_xs(*((1, -1) if last else (0, b)), 0, 1)
                load_residual(b, 2)
                load_residual(b, 3)
                load_xs(*((1, -1) if last else (0, b)), 1, 0)
                load_residual(b, 4)
                load_residual(b, 5)
                load_xs(*((1, -1) if last else (0, b)), 1, 1)
                load_residual(b, 6)
                if not last:
                    load_wo(b)
                load_residual(b, 7)
                if not last:
                    load_residual(b + 1, 0)
                    load_residual(b + 1, 1)

            sp.wait_ge(mod_made, MODS)
            load_residual(0, 0)
            load_residual(0, 1)
            with sp.Fori(0, B - 1) as b:
                attention_loads(b, False)
            attention_loads(LAST, True)

            sp.wait_ge(o_done, QT * B)
            for i in range(2):
                sp.wait_ge(st_x1[i], 16 * QT // 2 * B)
            sp.dma_start(pick[:, :, :], k_pick.rearrange("s p n -> p s n")).then_inc(ld_stack, 16)
            sp.dma_start(a_stack[:, :].bitcast(F32), lora_dram[0]).then_inc(ld_stack, 16)
            sp.dma_start(b_stack[:, :].bitcast(F32), lora_dram[1]).then_inc(ld_stack, 16)

            def load_rows(n):
                h, cp = n // 4, n % 4
                wait(sp, w2_turned, n - 1)
                src = w2[h * BANK:(h + 1) * BANK, cp * 2 * P:(cp + 1) * 2 * P]
                sp.dma_start(w2_rows[:, n % 2, :].rearrange("p (o c) -> p o c", o=4),
                             src.rearrange("(o p) c -> p o c", p=P)).then_inc(ld_rows[n % 2], 16)

            def store_w2t(n):
                sp.wait_ge(w2t_made, n + 1)
                sp.dma_start(w2t_dram[n], w2t[:, n % 2, :]).then_inc(st_w2t[n % 2], 16)

            load_rows(0)
            load_rows(1)
            for n in range(8):
                if n + 2 < 8:
                    load_rows(n + 2)
                store_w2t(n)

            def load_w2t(b, n):
                wait(sp, w_sum_made, 8 * (b + 1) + n - 1)
                sp.wait_ge(st_w2t[n % 2], 16 * 4)
                sp.dma_start(w2t[:, n % 2, :], w2t_dram[n]).then_inc(ld_w2t[n % 2], 16)

            def load_res(b, j, h, p):
                n = f_no(b, j, h, p)
                slot = 2 * h + p
                batch = b if j else b + 1
                if j == 0 and isinstance(b, int) and b < 0:
                    if slot < 2:
                        sp.wait_ge(w2_turned, 8)
                else:
                    sp.wait_ge(st_y[slot], 16 * (2 * batch + j))
                row = batch * S + j * CHUNK + p * 2 * P
                src = x1_dram[bass.ds(row, 2 * P), h * BANK:(h + 1) * BANK].rearrange("(t p) n -> p t n", p=P)
                sp.dma_start(res[:, slot, :].rearrange("p (t n) -> p t n", t=2), src).then_inc(ld_res[slot], 16)

            for slot in (2, 3, 0, 1):
                load_res(-1, 0, slot // 2, slot % 2)

            with sp.Fori(0, B - 1) as b:
                load_xs(1, b, 0, 0)
                load_res(b, 1, 0, 0)
                load_res(b, 1, 0, 1)
                load_w2t(b, 0)
                load_w2t(b, 1)
                load_xs(1, b, 0, 1)
                load_res(b, 1, 1, 0)
                load_res(b, 1, 1, 1)
                load_w2t(b, 2)
                load_w2t(b, 3)
                load_res(b, 0, 0, 0)
                load_w2t(b, 4)
                load_xs(1, b, 1, 0)
                load_w2t(b, 5)
                load_res(b, 0, 0, 1)
                load_w2t(b, 6)
                load_w2t(b, 7)
                load_res(b, 0, 1, 0)
                load_res(b, 0, 1, 1)
                load_xs(1, b, 1, 1)
            for h in range(2):
                for p in range(2):
                    load_res(LAST, 1, h, p)

        @block.gpsimd
        def _(pool):
            nc.gpsimd.memset(power[:, :], -0.5).then_inc(g_step, 1)
            nc.gpsimd.memset(eps[:, :], EPS).then_inc(g_step, 1)
            pool.wait_ge(zeroed, 3)
            pool.dma_start(c_rows[0:B, :], c).then_inc(ld_c, 16)
            for at in (0, LO_ROW):
                pool.dma_start(a_raw[at:at + NL * RANK, :], lora_a.rearrange("n r d -> (n r) d")).then_inc(ld_lora, 16)
                for n in range(NL):
                    pool.dma_start(b_raw[:, :, at + n * RANK:at + (n + 1) * RANK],
                                   lora_b[n].rearrange("(t p) r -> p t r", p=P)).then_inc(ld_lora, 16)
            pool.dma_start(start_i[:, :], starts.partition_broadcast(P)).then_inc(ld_lora, 16)
            pool.dma_start(which[:, :], k_which).then_inc(ld_lora, 16)
            pool.dma_start(bqkvT[:, :], bqkv.rearrange("(f p) -> p f", p=P),
                               allow_slow_non_contiguous=True).then_inc(ld_lora, 16)
            pool.dma_start(boT[:, :], bo.rearrange("(f p) -> p f", p=P),
                               allow_slow_non_contiguous=True).then_inc(ld_lora, 16)
            pool.dma_start(biasT[:, :], bias.rearrange("(f p) -> p f", p=P),
                               allow_slow_non_contiguous=True).then_inc(ld_lora, 16)
            pool.wait_ge(lora_lo, 2)
            pool.dma_start(lora_dram[0], a_both[:, :].bitcast(F32)).then_inc(st_lora, 16)
            pool.dma_start(lora_dram[1], b_both[:, :].bitcast(F32)).then_inc(st_lora, 16)

            def step(entry, b, stage, prep):
                what, i = entry[0], entry[1]
                if what == "stats":
                    n = round_no(*prep, *i)
                    pool.wait_ge(mv_made, 2 * n + 2)
                    nc.gpsimd.tensor_tensor(rstd[:, 0, :], mv[:, :, 1], eps[:, :], ALU.add).then_inc(var_eps, 1)
                    pool.wait_ge(var_eps, n + 1)
                    nc.gpsimd.tensor_tensor(rstd[:, 1, :], rstd[:, 0, :], power[:, :], ALU.pow).then_inc(rstd_made, 1)
                elif what == "radd":
                    t = i[0]
                    pool.wait_ge(ld_xr[t % 2], 16 * (QT // 2 * b + t // 2 + 1))
                    pool.wait_ge(row_made, b + 1)
                    xt = xr[:, t % 2, :]
                    nc.gpsimd.tensor_tensor(xt, xt, row_bc[:, :], ALU.add).then_inc(residual_made, 1)
                elif what == "store":
                    t = i[0]
                    pool.wait_ge(x1_made, QT * b + t + 1)
                    pool.dma_start(x1_dram[bass.ds(b * S + t * P, P), :], xr[:, t % 2, :]).then_inc(st_x1[t % 2], 16)
                elif what == "radd2":
                    j, h, p = i
                    n = f_no(b, j, h, p)
                    slot, batch = 2 * h + p, (b if j else b + 1)
                    pool.wait_ge(ld_res[slot], 16 * (2 * batch + j + 1))
                    pool.wait_ge(row2_made, batch + 1)
                    rt = res[:, slot, :].rearrange("p (t n) -> p t n", t=2)
                    row = row2_bc[:, h * BANK:(h + 1) * BANK].unsqueeze(1).to_broadcast([P, 2, BANK])
                    nc.gpsimd.tensor_tensor(rt, rt, row, ALU.add).then_inc(residual2_made, 1)
                elif what == "y_store":
                    j, h, p = i
                    n = f_no(b, j, h, p)
                    slot, batch = 2 * h + p, (b if j else b + 1)
                    pool.wait_ge(y_made, n + 1)
                    dst = y[bass.ds(batch * S + j * CHUNK + p * 2 * P, 2 * P), h * BANK:(h + 1) * BANK]
                    pool.dma_start(dst.rearrange("(t p) n -> p t n", p=P),
                                   res[:, slot, :].rearrange("p (t n) -> p t n", t=2)).then_inc(st_y[slot], 16)

            pool.wait_ge(g_step, 2)
            for entry in FIRST:
                step(entry, -1, 0, (0, -1))
            with pool.Fori(0, B - 1) as b:
                for entry in ATTENTION:
                    step(entry, b, 0, (0, b))
            for entry in LAST_ATTENTION:
                step(entry, LAST, 0, (1, -1))
            for entry in ENTER_SECOND:
                step(entry, -1, 1, (1, -1))
            with pool.Fori(0, B - 1) as b:
                for entry in SECOND:
                    step(entry, b, 1, (1, b))
            for entry in END:
                step(entry, LAST, 1, (1, LAST))
            for slot in range(4):
                pool.wait_ge(st_y[slot], 16 * 2 * B)
            pool.wait_ge(st_lora, 32)

        @block.scalar
        def _(act):
            def emptied_copy(dst, src, made):
                nc.scalar.activation(dst, src, ACT.Copy).then_inc(made, 1)

            def step(entry, b, stage, prep):
                what, i = entry[0], entry[1]
                ps = pair[entry[2]] if len(entry) > 2 else None
                if what == "turn_lora":
                    act.wait_ge(ld_lora, 16 * 13)
                    nc.scalar.activation(a_both[:, :], a_raw[:, :], ACT.Copy).then_inc(lora_hi, 1)
                    act.wait_ge(lora_turned, 1)
                    nc.scalar.activation(b_both[:, :], ps[:, :], ACT.Copy).then_inc(lora_hi, 1)
                elif what == "mod":
                    act.wait_ge(mod_used, CT * (i[0] + 1))
                    wait(act, mod_turned, i[0])
                    emptied_copy(mod_rows[:, :], ps[:, :], mod_copied)
                elif what == "w_split":
                    n = i[0]
                    act.wait_ge(ld_w[n], 16)
                    c2 = slice(2 * n, 2 * n + 2)
                    nc.scalar.activation(w_hi[:, c2, 0:D], w_raw[:, c2, 0:D], ACT.Copy, scale=SCALE).then_inc(w_hi_made, 1)
                    nc.scalar.activation(w_hi[:, c2, D:], w_raw[:, c2, D:], ACT.Copy).then_inc(w_hi_made, 1)
                elif what == "T":
                    j, r, half = i
                    n = turn_no(*prep, *i)
                    act.wait_ge(h_turned, n + 1)
                    if stage == 0 and entry in FIRST and i == (1, 0, 0):
                        act.wait_ge(st_lora, 32)
                    for sub in range(2):
                        wait(act, h_lo_made, 2 * n + sub)
                        for cc in range(2):
                            ct = 4 * half + 2 * sub + cc
                            nc.scalar.activation(affine[:, cc, :], ps[:, (2 * sub + cc) * 2 * P:(2 * sub + cc + 1) * 2 * P],
                                                 ACT.Identity, bias=cur[:, 1, ct:ct + 1],
                                                 scale=cur[:, 0, ct:ct + 1]).then_inc(h_affine, 1)
                        act.wait_ge(h_affine, 4 * n + 2 * sub + 2)
                        ct = 4 * half + 2 * sub
                        nc.scalar.activation(h_hi[j][:, ct:ct + 2, 2 * r * P:2 * (r + 1) * P], affine[:, :, :],
                                             ACT.Copy).then_inc(h_hi_made, 1)
                elif what in ("Q", "K"):
                    n = 2 * (b + 1) + i[0]
                    done, made, dst, col = (q_done, q_hi_made, q_hi, 0) if what == "Q" else (k_done, k_hi_made, k_hi, DT)
                    act.wait_ge(done, n + 1)
                    for m in range(DT):
                        nc.scalar.activation(dst[:, m, i[0] * CHUNK:(i[0] + 1) * CHUNK], ps[:, m * BANK:(m + 1) * BANK],
                                             ACT.Identity, bias=bqkvT[:, col + m:col + m + 1]).then_inc(made, 1)
                elif what == "V":
                    act.wait_ge(v_done, 2 * (b + 1) + i[0] + 1)
                    emptied_copy(v_hi[:, 4 * i[0]:4 * i[0] + 4, :], ps[:, :], v_hi_made)
                elif what == "gate":
                    for d in range(DT):
                        act.wait_ge(wo_gated, DT * (b + 1) + d + 1)
                        nc.scalar.activation(wo_hi[:, d, :], probs[:, d, :], ACT.Copy).then_inc(wo_hi_made, 1)
                elif what == "row":
                    act.wait_ge(row_done, b + 2)
                    wait(act, residual_made, QT * (b + 1))
                    emptied_copy(row_bc[:, :], ps[:, :], row_made)
                elif what == "S":
                    t = i[0]
                    act.wait_ge(max_made, QT * b + t + 1)
                    if t >= 2:
                        act.wait_ge(pt_done, QT * b + t - 1)
                    else:
                        act.wait_ge(wo_lo_made, DT * (b + 1))
                    nc.scalar.activation(probs[:, t % 2, :], ps[:, :], ACT.Exp, bias=neg_max[:, t:t + 1],
                                         accum_out=total[:, t:t + 1]).then_inc(exp_made, 1)
                elif what == "PT":
                    t = i[0]
                    act.wait_ge(pt_done, QT * b + t + 1)
                    nc.scalar.activation(pt_hi[:, :, (t % 4) * P:(t % 4 + 1) * P],
                                         ps[:, :].rearrange("p (k q) -> p k q", q=P), ACT.Copy).then_inc(pt_hi_made, 1)
                elif what == "PV":
                    act.wait_ge(pv_done, 2 * b + i[0] + 1)
                    nc.scalar.activation(q_hi[:, :, i[0] * CHUNK:(i[0] + 1) * CHUNK],
                                         ps[:, :].rearrange("p (d q) -> p d q", d=DT), ACT.Copy).then_inc(o_hi_made, 1)
                elif what in ("pick_a", "pick_b"):
                    side = 0 if what == "pick_a" else 1
                    act.wait_ge(pick_done, 2 * (b + 1) + side + 1)
                    emptied_copy((a_used, b_used)[side][:, :], ps[:, :], picked_made)
                elif what == "gate2":
                    act.wait_ge(gate2_done, b + 2)
                    wait(act, y_gated, QT * (b + 1))
                    emptied_copy(gate_bc[:, :], ps[:, :], gate2_made)
                elif what == "row2":
                    act.wait_ge(row2_done, b + 2)
                    wait(act, residual2_made, QT * (b + 1))
                    emptied_copy(row2_bc[:, :], ps[:, :], row2_made)
                elif what == "turn_w":
                    n = i[0]
                    act.wait_ge(w2_turned, n + 1)
                    if n >= 2:
                        act.wait_ge(st_w2t[n % 2], 16 * (n // 2))
                        act.wait_ge(w_sum_made, n - 1)
                    emptied_copy(w2t[:, n % 2, :], ps[:, :], w2t_made)
                elif what == "W":
                    n = 8 * (b + 1) + i[0]
                    h, cp = i[0] // 4, i[0] % 4
                    act.wait_ge(w_sum_made, n + 1)
                    nc.scalar.activation(w2_hi[:, 2 * cp:2 * cp + 2, h * BANK:(h + 1) * BANK],
                                         w_sum[:, n_slot(i), :].rearrange("p (c n) -> p c n", c=2),
                                         ACT.Copy).then_inc(w2_hi_made, 1)
                elif what == "turn_c":
                    act.wait_ge(ld_c, 16)
                    nc.scalar.activation(c_exp[0:B, :], c_rows[0:B, :], ACT.Exp, scale=-1.0).then_inc(c_expd, 1)

            def n_slot(i):
                return i[0] % 2

            for entry in FIRST:
                step(entry, -1, 0, (0, -1))
            with act.Fori(0, B - 1) as b:
                for entry in ATTENTION:
                    step(entry, b, 0, (0, b))
            for entry in LAST_ATTENTION:
                step(entry, LAST, 0, (1, -1))
            for entry in ENTER_SECOND:
                step(entry, -1, 1, (1, -1))
            with act.Fori(0, B - 1) as b:
                for entry in SECOND:
                    step(entry, b, 1, (1, b))

        @block.vector
        def _(dve):
            chain = [0]

            def link(ins):
                chain[0] += 1
                ins.then_inc(v_step, 1)
                dve.wait_ge(v_step, chain[0])

            def step(entry, b, stage, prep):
                what, i = entry[0], entry[1]
                ps = pair[entry[2]] if len(entry) > 2 else None
                if what == "turn_c":
                    dve.wait_ge(c_expd, 1)
                    link(nc.vector.tensor_scalar(c_exp[0:B, :], c_exp[0:B, :], 1.0, None, ALU.add))
                    link(nc.vector.reciprocal(c_exp[0:B, :], c_exp[0:B, :]))
                    nc.vector.tensor_tensor(c_rows[0:B, :], c_rows[0:B, :], c_exp[0:B, :], ALU.mult).then_inc(c_silu, 1)
                    dve.wait_ge(c_turned, 1)
                    nc.vector.tensor_copy(scT[:, :, :], ps[:, 0:CT * 32]).then_inc(c_ready, 1)
                elif what == "turn_lora":
                    dve.wait_ge(ld_lora, 16 * 13)
                    link(nc.vector.tensor_copy(start_f[:, :], start_i[:, :]))
                    for b0 in range(B):
                        ins = nc.vector.tensor_scalar(le[:, :, b0], start_f[:, :], float(b0), None, ALU.is_le)
                    link(ins)
                    link(nc.vector.tensor_tensor(s1[:, :], le[:, 0, :], le[:, 1, :], ALU.mult))
                    link(nc.vector.tensor_tensor(s1[:, :], le[:, 0, :], s1[:, :], ALU.subtract))
                    link(nc.vector.scalar_tensor_tensor(s1[:, :], le[:, 1, :], 2.0, s1[:, :], ALU.mult, ALU.add))
                    link(nc.vector.scalar_tensor_tensor(s2[:, :], le[:, 3, :], 3.0, s1[:, :], ALU.add, ALU.subtract))
                    link(nc.vector.tensor_tensor(s3[:, :], le[:, 2, :], s2[:, :], ALU.mult))
                    link(nc.vector.tensor_tensor(s3[:, :], s3[:, :], s1[:, :], ALU.add))
                    link(nc.vector.tensor_scalar(picked[:, :], s3[:, :], which[:, 0:1], None, ALU.is_equal))
                    link(nc.vector.tensor_scalar(bqkvT[:, 0:DT], bqkvT[:, 0:DT], SCALE, None, ALU.mult))
                    dve.wait_ge(lora_hi, 1)
                    nc.vector.tensor_tensor(a_both[LO_ROW:, :], a_raw[LO_ROW:, :], a_both[LO_ROW:, :].bitcast(F32),
                                            ALU.subtract).then_inc(lora_lo, 1)
                    dve.wait_ge(lora_hi, 2)
                    nc.vector.tensor_tensor(b_both[LO_ROW:, :], ps[LO_ROW:, :], b_both[LO_ROW:, :].bitcast(F32),
                                            ALU.subtract).then_inc(lora_lo, 1)
                elif what == "mod_turn":
                    s, q = i
                    dve.wait_ge(mod_turned, s + 1)
                    src, dst = ps[:, 0:CT * B], modT[:, q, :, :].rearrange("p c b -> p (c b)")
                    if q in (CA, CB):
                        nc.vector.tensor_scalar(dst, src, 1.0, None, ALU.add).then_inc(mod_made, 1)
                    elif q in (SA, SB):
                        nc.vector.tensor_copy(dst, src).then_inc(mod_made, 1)
                    else:
                        link(nc.vector.tensor_copy(dst, src))
                        link(nc.vector.tensor_scalar(sign[:, :], dst, 0.0, 2.0, ALU.is_ge, ALU.mult))
                        link(nc.vector.scalar_tensor_tensor(size[:, :], dst, -1.0, dst, ALU.mult, ALU.max))
                        link(nc.vector.tensor_scalar(size[:, :], size[:, :], 0.25, None, ALU.max))
                        nc.vector.scalar_tensor_tensor(dst, sign[:, :], -1.0, size[:, :], ALU.add,
                                                       ALU.mult).then_inc(mod_made, 1)
                elif what == "w_split":
                    n = i[0]
                    dve.wait_ge(w_hi_made, 2 * n + 2)
                    c2 = slice(2 * n, 2 * n + 2)
                    nc.vector.scalar_tensor_tensor(w_lo[:, c2, 0:D], w_raw[:, c2, 0:D], SCALE,
                                                   w_hi[:, c2, 0:D].bitcast(F32), ALU.mult, ALU.subtract).then_inc(w_lo_made, 1)
                    nc.vector.tensor_tensor(w_lo[:, c2, D:], w_raw[:, c2, D:], w_hi[:, c2, D:].bitcast(F32),
                                            ALU.subtract).then_inc(w_lo_made, 1)
                elif what == "turn_wo":
                    dve.wait_ge(wo_turned, 1)
                    nc.vector.tensor_tensor(boT[:, :], boT[:, :], ps[:, 0:CT], ALU.add).then_inc(wo_row_made, 1)
                elif what == "stats":
                    n = round_no(*prep, *i)
                    for k in range(2):
                        dve.wait_ge(ld_xs[k], 16 * (n + 1))
                        for half in range(2):
                            nc.vector.bn_stats(bn[:, k, half, :], xs[:, k, half * BANK:(half + 1) * BANK]).then_inc(bn_made, 1)
                    dve.wait_ge(bn_made, 4 * n + 4)
                    nc.vector.memset(fence[:, :], 0.0)
                    for k in range(2):
                        nc.vector.bn_aggr(mv[:, k, :], bn[:, k, :, :].rearrange("p h n -> p (h n)")).then_inc(mv_made, 1)
                elif what == "norm":
                    n = round_no(*prep, *i)
                    if i == (0, 0):
                        pst, pb = prep
                        wait(dve, h_affine, 4 * turn_no(pst, pb, 0, 0, 0))
                        if stage == 0 and isinstance(b, int) and b < 0:
                            dve.wait_ge(mod_made, 2)
                        for k, q in enumerate((CA, SA) if pst == 0 else (CB, SB)):
                            src = modT[:, q, :, bass.ds(pb + 1, 1)].rearrange("p c b -> p (c b)")
                            nc.vector.tensor_copy(cur[:, k, :], src)
                    dve.wait_ge(rstd_made, n + 1)
                    for k in range(2):
                        nc.vector.tensor_scalar(xs[:, k, :], xs[:, k, :], mv[:, k, 0:1], rstd[:, 1, k:k + 1],
                                                ALU.subtract, ALU.mult).then_inc(x_normed, 1)
                elif what == "T":
                    j, r, half = i
                    n = turn_no(*prep, *i)
                    for sub in range(2):
                        ct = 4 * half + 2 * sub
                        where = (slice(None), slice(ct, ct + 2), slice(2 * r * P, 2 * (r + 1) * P))
                        dve.wait_ge(h_hi_made, 2 * n + sub + 1)
                        nc.vector.tensor_tensor(h_lo[j][where], affine[:, :, :], h_hi[j][where].bitcast(F32),
                                                ALU.subtract).then_inc(h_lo_made, 1)
                elif what in ("Q", "K"):
                    n = 2 * (b + 1) + i[0]
                    hi_made, made, hi, lo, col = ((q_hi_made, q_lo_made, q_hi, q_lo, 0) if what == "Q"
                                                  else (k_hi_made, k_lo_made, k_hi, k_lo, DT))
                    for m in range(DT):
                        where = (slice(None), m, slice(i[0] * CHUNK, (i[0] + 1) * CHUNK))
                        dve.wait_ge(hi_made, 2 * n + m + 1)
                        nc.vector.scalar_tensor_tensor(lo[where], ps[:, m * BANK:(m + 1) * BANK],
                                                       bqkvT[:, col + m:col + m + 1], hi[where].bitcast(F32),
                                                       ALU.add, ALU.subtract).then_inc(made, 1)
                elif what == "V":
                    dve.wait_ge(v_hi_made, 2 * (b + 1) + i[0] + 1)
                    where = (slice(None), slice(4 * i[0], 4 * i[0] + 4), slice(None))
                    nc.vector.tensor_tensor(v_lo[where], ps[:, :].rearrange("p (t n) -> p t n", t=4),
                                            v_hi[where].bitcast(F32), ALU.subtract).then_inc(v_lo_made, 1)
                elif what == "gates":
                    wait(dve, row_done, b + 1)
                    src = modT[:, GA, :, bass.ds(b + 1, 1)].rearrange("p c b -> p (c b)")
                    nc.vector.tensor_copy(gate_col[:, :], src).then_inc(gates_made, 1)
                    dve.wait_ge(wo_row_made, 1)
                    nc.vector.tensor_tensor(row_col[:, :], src, boT[:, :], ALU.mult).then_inc(gates_made, 1)
                elif what == "gate":
                    dve.wait_ge(gate_done, b + 2)
                    dve.wait_ge(ld_wo, 16 * (b + 2))
                    for d in range(DT):
                        nc.vector.tensor_tensor(probs[:, d, :], probs[:, d, :], ps[:, :], ALU.mult).then_inc(wo_gated, 1)
                elif what == "wo_lo":
                    for d in range(DT):
                        dve.wait_ge(wo_hi_made, DT * (b + 1) + d + 1)
                        nc.vector.tensor_tensor(wo_lo[:, d, :], probs[:, d, :], wo_hi[:, d, :].bitcast(F32),
                                                ALU.subtract).then_inc(wo_lo_made, 1)
                elif what == "S":
                    t = i[0]
                    dve.wait_ge(s_done, QT * b + t + 1)
                    nc.vector.tensor_reduce(neg_max[:, t:t + 1], ps[:, :], AX_X, ALU.max, negate=True).then_inc(max_made, 1)
                elif what == "PT":
                    t = i[0]
                    dve.wait_ge(exp_made, QT * b + t + 1)
                    nc.vector.reciprocal(r_total[:, t:t + 1], total[:, t:t + 1]).then_inc(r_total_made, 1)
                    where = (slice(None), slice(None), slice((t % 4) * P, (t % 4 + 1) * P))
                    dve.wait_ge(pt_hi_made, QT * b + t + 1)
                    nc.vector.tensor_tensor(pt_lo[where], ps[:, :].rearrange("p (k q) -> p k q", q=P),
                                            pt_hi[where].bitcast(F32), ALU.subtract).then_inc(pt_lo_made, 1)
                elif what == "PV":
                    dve.wait_ge(o_hi_made, 2 * b + i[0] + 1)
                    where = (slice(None), slice(None), slice(i[0] * CHUNK, (i[0] + 1) * CHUNK))
                    nc.vector.tensor_tensor(q_lo[where], ps[:, :].rearrange("p (d q) -> p d q", d=DT),
                                            q_hi[where].bitcast(F32), ALU.subtract).then_inc(o_lo_made, 1)
                elif what == "O":
                    t = i[0]
                    dve.wait_ge(o_done, QT * b + t + 1)
                    dve.wait_ge(residual_made, QT * b + t + 1)
                    dve.wait_ge(r_total_made, QT * b + t + 1)
                    xt = xr[:, t % 2, :]
                    nc.vector.scalar_tensor_tensor(xt, ps[:, :], r_total[:, t:t + 1], xt, ALU.mult,
                                                   ALU.add).then_inc(x1_made, 1)
                elif what == "enter":
                    dve.wait_ge(ld_stack, 48)
                elif what == "picks":
                    wait(dve, pick_done, 2 * (b + 1))
                    for side in range(2):
                        nc.vector.tensor_scalar(pick_b[:, side, :], pick[:, side, :], picked[:, bass.ds(b + 1, 1)], None,
                                                ALU.mult).then_inc(picks_made, 1)
                elif what == "gates2":
                    wait(dve, row2_done, b + 1)
                    src = modT[:, GB, :, bass.ds(b + 1, 1)].rearrange("p c b -> p (c b)")
                    nc.vector.tensor_copy(gate_col[:, :], src).then_inc(gates2_made, 1)
                    nc.vector.tensor_tensor(row_col[:, :], src, biasT[:, :], ALU.mult).then_inc(gates2_made, 1)
                elif what == "W":
                    n = 8 * (b + 1) + i[0]
                    slot = i[0] % 2
                    dve.wait_ge(lora_done, n + 1)
                    wait(dve, w2_lo_made, n - 1)
                    if isinstance(b, int) and b < 0:
                        dve.wait_ge(w2t_made, n + 1)
                    else:
                        dve.wait_ge(ld_w2t[slot], 16 * (4 * b + i[0] // 2 + 1))
                    nc.vector.tensor_tensor(w_sum[:, slot, :], w2t[:, slot, :], ps[:, :], ALU.add).then_inc(w_sum_made, 1)
                elif what == "W_lo":
                    n = 8 * (b + 1) + i[0]
                    h, cp = i[0] // 4, i[0] % 4
                    where = (slice(None), slice(2 * cp, 2 * cp + 2), slice(h * BANK, (h + 1) * BANK))
                    dve.wait_ge(w2_hi_made, n + 1)
                    nc.vector.tensor_tensor(w2_lo[where], w_sum[:, i[0] % 2, :].rearrange("p (c n) -> p c n", c=2),
                                            w2_hi[where].bitcast(F32), ALU.subtract).then_inc(w2_lo_made, 1)
                elif what == "F" and i[3] == 3:
                    j, h, p = i[:3]
                    n = f_no(b, j, h, p)
                    slot, batch = 2 * h + p, (b if j else b + 1)
                    dve.wait_ge(f_done, n + 1)
                    dve.wait_ge(gate2_made, batch + 1)
                    wait(dve, y_made, n)
                    gate = gate_bc[:, h * BANK:(h + 1) * BANK].unsqueeze(1).to_broadcast([P, 2, BANK])
                    nc.vector.tensor_tensor(gated[:, :].rearrange("p (t n) -> p t n", t=2),
                                            ps[:, :].rearrange("p (t n) -> p t n", t=2), gate, ALU.mult).then_inc(y_gated, 1)
                    dve.wait_ge(y_gated, n + 1)
                    dve.wait_ge(residual2_made, n + 1)
                    nc.vector.tensor_tensor(res[:, slot, :], res[:, slot, :], gated[:, :], ALU.add).then_inc(y_made, 1)

            nc.vector.memset(c_rows[:, :], 0.0).then_inc(zeroed, 1)
            nc.vector.memset(a_raw[:, :], 0.0).then_inc(zeroed, 1)
            nc.vector.memset(b_raw[:, :, :], 0.0).then_inc(zeroed, 1)
            for entry in FIRST:
                step(entry, -1, 0, (0, -1))
            with dve.Fori(0, B - 1) as b:
                for entry in ATTENTION:
                    step(entry, b, 0, (0, b))
            for entry in LAST_ATTENTION:
                step(entry, LAST, 0, (1, -1))
            for entry in ENTER_SECOND:
                step(entry, -1, 1, (1, -1))
            with dve.Fori(0, B - 1) as b:
                for entry in SECOND:
                    step(entry, b, 1, (1, b))
            for entry in END:
                step(entry, LAST, 1, (1, LAST))

        @block.tensor
        def _(pe):
            def product3(out, left, right, first, last):
                nc.tensor.matmul(out, left[0], right[0], start=first, stop=False)
                nc.tensor.matmul(out, left[0], right[1], start=False, stop=False)
                return nc.tensor.matmul(out, left[1], right[0], start=False, stop=last)

            def both(hi, lo, *where):
                return hi[(slice(None),) + where], lo[(slice(None),) + where]

            def spread(ps, col, done):
                for ct in range(CT):
                    last = nc.tensor.transpose(ps[:, ct * P:(ct + 1) * P], col[:, ct:ct + 1].to_broadcast([P, P]), ident[:, :])
                last.then_inc(done, 1)

            def step(entry, b, stage, prep):
                if len(entry) < 3:
                    return
                what, i, _, before = entry
                ps = pair[entry[2]]
                if before and before[0] == "T":
                    wait_emptied(pe, before, prep[1], prep[0])
                else:
                    wait_emptied(pe, before, b, stage)
                if what == "turn_c":
                    pe.wait_ge(ld_const, 32)
                    pe.wait_ge(zeroed, 1)
                    pe.wait_ge(c_silu, 1)
                    for k in range(CT):
                        last = nc.tensor.transpose(ps[:, 32 * k:32 * k + 32], c_rows[:, k * P:(k + 1) * P], ident[0:32, 0:32])
                    last.then_inc(c_turned, 1)
                elif what == "turn_lora":
                    pe.wait_ge(ld_lora, 16 * 13)
                    pe.wait_ge(zeroed, 3)
                    for k in range(CT):
                        last = nc.tensor.transpose(ps[:, k * P:(k + 1) * P], b_raw[:, k, :], ident[:, :])
                    last.then_inc(lora_turned, 1)
                elif what == "mod":
                    if i[0] == 0:
                        pe.wait_ge(c_ready, 1)
                    for k in range(CT):
                        n = CT * i[0] + k
                        q = 32 * (k % 4)
                        pe.wait_ge(ld_wm[n % WM], 16 * (n // WM + 1))
                        for half in range(2):
                            cols = slice(half * BANK, (half + 1) * BANK)
                            last = nc.tensor.matmul(ps[q:q + 32, cols], scT[:, k, :], wm[:, n % WM, cols],
                                                    start=(k < 4), stop=(k >= 4))
                        last.then_inc(mod_used, 1)
                elif what == "mod_turn":
                    pe.wait_ge(mod_copied, i[0] + 1)
                    for k in range(CT):
                        last = nc.tensor.matmul(ps[:, k * B:(k + 1) * B], mod_rows[:, k * P:(k + 1) * P], sel[:, :],
                                                start=True, stop=True)
                    last.then_inc(mod_turned, 1)
                elif what == "T":
                    j, r, half = i
                    n = turn_no(*prep, *i)
                    pe.wait_ge(x_normed, 2 * round_no(*prep, j, r) + 2)
                    for cc in range(4):
                        for k in range(2):
                            ct = 4 * half + cc
                            last = nc.tensor.transpose(ps[:, (2 * cc + k) * P:(2 * cc + k + 1) * P],
                                                       xs[:, k, ct * P:(ct + 1) * P], ident[:, :])
                    last.then_inc(h_turned, 1)
                elif what in ("Q", "K", "V"):
                    j = i[0]
                    pe.wait_ge(h_lo_made, 2 * turn_no(0, b, j, 1, 1) + 2)
                    if stage == 0 and isinstance(b, int):
                        pe.wait_ge(w_lo_made, 8)
                    if what == "V":
                        for t in range(4):
                            for ct in range(CT):
                                last = product3(ps[:, t * D:(t + 1) * D], both(h_hi[j], h_lo[j], ct, slice(t * P, (t + 1) * P)),
                                                both(w_hi, w_lo, ct, slice(2 * D, 3 * D)), ct == 0, ct == CT - 1)
                        last.then_inc(v_done, 1)
                    else:
                        for m in range(DT):
                            at = (0 if what == "Q" else D) + m * P
                            for ct in range(CT):
                                last = product3(ps[:, m * BANK:(m + 1) * BANK], both(w_hi, w_lo, ct, slice(at, at + P)),
                                                both(h_hi[j], h_lo[j], ct, slice(None)), ct == 0, ct == CT - 1)
                        last.then_inc(q_done if what == "Q" else k_done, 1)
                elif what == "turn_wo":
                    pe.wait_ge(ld_wo, 16)
                    for ct in range(CT):
                        for d in range(DT):
                            last = nc.tensor.matmul(ps[:, ct:ct + 1], probs[:, d, ct * P:(ct + 1) * P],
                                                    bqkvT[:, 2 * DT + d:2 * DT + d + 1], start=(d == 0), stop=(d == DT - 1))
                    last.then_inc(wo_turned, 1)
                elif what == "gate":
                    pe.wait_ge(gates_made, 2 * (b + 1) + 1)
                    spread(ps, gate_col, gate_done)
                elif what == "row":
                    pe.wait_ge(gates_made, 2 * (b + 1) + 2)
                    spread(ps, row_col, row_done)
                elif what == "S":
                    t = i[0]
                    pe.wait_ge(q_lo_made, 4 * (b + 1))
                    pe.wait_ge(k_lo_made, 4 * (b + 1))
                    for half in range(2):
                        for d in range(DT):
                            last = product3(ps[:, half * BANK:(half + 1) * BANK], both(q_hi, q_lo, d, slice(t * P, (t + 1) * P)),
                                            both(k_hi, k_lo, d, slice(half * BANK, (half + 1) * BANK)), d == 0, d == DT - 1)
                    last.then_inc(s_done, 1)
                elif what == "PT":
                    t = i[0]
                    pe.wait_ge(exp_made, QT * b + t + 1)
                    for k in range(QT):
                        last = nc.tensor.transpose(ps[:, k * P:(k + 1) * P], probs[:, t % 2, k * P:(k + 1) * P], ident[:, :])
                    last.then_inc(pt_done, 1)
                elif what == "PV":
                    pe.wait_ge(v_lo_made, 2 * (b + 1))
                    pe.wait_ge(pt_lo_made, QT * b + 4 * i[0] + 4)
                    for m in range(DT):
                        for k in range(QT):
                            last = product3(ps[:, m * BANK:(m + 1) * BANK], both(v_hi, v_lo, k, slice(m * P, (m + 1) * P)),
                                            both(pt_hi, pt_lo, k, slice(None)), k == 0, k == QT - 1)
                    last.then_inc(pv_done, 1)
                elif what == "O":
                    t = i[0]
                    pe.wait_ge(o_lo_made, 2 * b + t // 4 + 1)
                    pe.wait_ge(wo_lo_made, DT * (b + 1))
                    for half in range(2):
                        cols = slice(half * BANK, (half + 1) * BANK)
                        for d in range(DT):
                            last = product3(ps[:, cols], both(q_hi, q_lo, d, slice(t * P, (t + 1) * P)),
                                            both(wo_hi, wo_lo, d, cols), d == 0, d == DT - 1)
                    last.then_inc(o_done, 1)
                elif what in ("pick_a", "pick_b"):
                    side = 0 if what == "pick_a" else 1
                    pe.wait_ge(picks_made, 2 * (b + 1) + side + 1)
                    for half in range(2):
                        cols = slice(half * BANK, (half + 1) * BANK)
                        last = nc.tensor.matmul(ps[:, cols], pick_b[:, side, :], (a_stack, b_stack)[side][:, cols],
                                                start=True, stop=True)
                    last.then_inc(pick_done, 1)
                elif what == "gate2":
                    pe.wait_ge(gates2_made, 2 * (b + 1) + 1)
                    spread(ps, gate_col, gate2_done)
                elif what == "row2":
                    pe.wait_ge(gates2_made, 2 * (b + 1) + 2)
                    spread(ps, row_col, row2_done)
                elif what == "turn_w":
                    n = i[0]
                    pe.wait_ge(ld_rows[n % 2], 16 * (n // 2 + 1))
                    for cc in range(2):
                        for o in range(4):
                            last = nc.tensor.transpose(ps[:, (4 * cc + o) * P:(4 * cc + o + 1) * P],
                                                       w2_rows[:, n % 2, (2 * o + cc) * P:(2 * o + cc + 1) * P], ident[:, :])
                    last.then_inc(w2_turned, 1)
                elif what == "W":
                    h, cp = i[0] // 4, i[0] % 4
                    pe.wait_ge(picked_made, 2 * (b + 2))
                    for cc in range(2):
                        ct = 2 * cp + cc
                        last = nc.tensor.matmul(ps[:, cc * BANK:(cc + 1) * BANK], a_used[:, ct * P:(ct + 1) * P],
                                                b_used[:, h * BANK:(h + 1) * BANK], start=True, stop=True)
                    last.then_inc(lora_done, 1)
                elif what == "F":
                    j, h, p, s = i
                    batch = b if j else b + 1
                    if s == 0:
                        pe.wait_ge(w2_lo_made, 8 * batch + 4 * h + 4)
                        pe.wait_ge(h_lo_made, 2 * turn_no(1, batch - 1, j, 1, 1) + 2)
                    t = s // 2
                    for ct in range(4 * (s % 2), 4 * (s % 2) + 4):
                        last = product3(ps[:, t * BANK:(t + 1) * BANK],
                                        both(h_hi[j], h_lo[j], ct, slice((2 * p + t) * P, (2 * p + t + 1) * P)),
                                        both(w2_hi, w2_lo, ct, slice(h * BANK, (h + 1) * BANK)), ct == 0, ct == CT - 1)
                    if s == 3:
                        last.then_inc(f_done, 1)

            for entry in FIRST:
                step(entry, -1, 0, (0, -1))
            with pe.Fori(0, B - 1) as b:
                for entry in ATTENTION:
                    step(entry, b, 0, (0, b))
            for entry in LAST_ATTENTION:
                step(entry, LAST, 0, (1, -1))
            for entry in ENTER_SECOND:
                step(entry, -1, 1, (1, -1))
            with pe.Fori(0, B - 1) as b:
                for entry in SECOND:
                    step(entry, b, 1, (1, b))
            for entry in END:
                step(entry, LAST, 1, (1, LAST))


_INS = [
    "L0_attn_x", "L0_attn_Wqkv", "L0_attn_bqkv", "L0_attn_Wo", "L0_attn_bo", "L0_ffn_weight", "L0_ffn_bias",
    "L0_ffn_lora_A", "L0_ffn_lora_B", "L0_ffn_lora_start_indices", "L0_c", "L0_wmod",
]


def kernel(**inputs):
    import concourse.bacc as bacc
    from concourse.bass_utils import run_bass_kernel_spmd

    nc = bacc.Bacc("TRN2", target_bir_lowering=False, num_devices=1)
    arrays, args = {}, []

    def give(name, a):
        arrays[f"in_{name}"] = a
        args.append(nc.dram_tensor(f"in_{name}", a.shape, mybir.dt.from_np(a.dtype), kind="ExternalInput").ap())

    for name in _INS:
        a = np.ascontiguousarray(inputs[name])
        if name == "L0_attn_x":
            a = a.reshape(B * S, H)
        elif name == "L0_ffn_lora_start_indices":
            a = a.reshape(1, B)
        give(name, a)
    for name, a in host_constants().items():
        give(name, a)
    out = nc.dram_tensor("out_y", (B * S, H), F32, kind="ExternalOutput").ap()
    build_block(nc, *args, out)
    r = run_bass_kernel_spmd(nc, [arrays], core_ids=[0])
    return r.results[0]["out_y"].reshape(B, S, H)
```

```python
from contextlib import ExitStack

import numpy as np

import concourse.bass as bass
from concourse import mybir

F32 = mybir.dt.float32
F32R = mybir.dt.float32r
I32 = mybir.dt.int32
ALU = mybir.AluOpType
ACT = mybir.ActivationFunctionType
AX_X = mybir.AxisListType.X

P = 128
B, S, H = 4, 1024, 1024
D = H // 4
CT = H // P
DT = D // P
BANK = 512
CHUNK = 512
QT = S // P
MODS = 6
SA, CA, GA, SB, CB, GB = range(MODS)
NL, RANK = 3, 16
LO_ROW = 64
WM = 7
EPS = 1e-5
SCALE = float(D) ** -0.5
LAST = B - 1


def host_constants():
    sel = np.zeros((P, B), np.float32)
    for q in range(4):
        for b in range(B):
            sel[32 * q + b, b] = 1
    pick = np.zeros((2, P, P), np.float32)
    which = np.full((P, 1), -1, np.float32)
    for part in range(2):
        for n in range(NL):
            for r in range(RANK):
                row = LO_ROW * part + RANK * n + r
                which[row, 0] = n + 2
                for side, order in enumerate([(0, 1, 0), (0, 0, 1)]):
                    for block, want in enumerate(order):
                        if want == part:
                            pick[side, row, 32 * block + r] = 1
    return {"ident": np.eye(P, dtype=np.float32), "sel": sel, "pick": pick, "which": which}


FIRST = [
    ("turn_c", (), "C", None), ("mod", (0, CA, 0), "B", None), ("mod", (0, CA, 1), "B", None),
    ("mod", (1, SA, 0), "D", None), ("mod_turn", (0, CA), "B", ("mod", (0, CA), 0)), ("stats", (0, 0)),
    ("mod", (1, SA, 1), "D", None), ("mod_turn", (1, SA), "C", ("turn_c", (), 0)), ("norm", (0, 0)),
    ("turn_lora", (), "C", ("mod_turn", (1, SA), 0)), ("T", (0, 0, 0), "B", ("mod_turn", (0, CA), 0)),
    ("T", (0, 0, 1), "D", ("mod", (1, SA), 0)), ("w_split", (0,)), ("stats", (0, 1)), ("norm", (0, 1)),
    ("w_split", (1,)), ("w_split", (2,)), ("T", (0, 1, 0), "C", ("turn_lora", (), 0)),
    ("T", (0, 1, 1), "A", None), ("stats", (1, 0)), ("norm", (1, 0)), ("w_split", (3,)),
    ("T", (1, 0, 0), "D", ("T", (0, 0, 1), 0)), ("T", (1, 0, 1), "B", ("T", (0, 0, 0), 0)),
    ("mod", (2, GA, 0), "C", ("T", (0, 1, 0), 0)), ("stats", (1, 1)),
    ("Q", (0, 0), "A", ("T", (0, 1, 1), 0)), ("norm", (1, 1)), ("Q", (0, 1), "A", None),
    ("mod", (2, GA, 1), "C", None), ("T", (1, 1, 0), "B", ("T", (1, 0, 1), 0)),
    ("K", (0, 0), "C", ("mod", (2, GA), 0)), ("mod", (3, SB, 0), "A", ("Q", (0,), 0)),
    ("T", (1, 1, 1), "B", ("T", (1, 1, 0), 0)), ("mod_turn", (2, GA), "D", ("T", (1, 0, 0), 0)),
    ("mod", (3, SB, 1), "A", None), ("K", (0, 1), "C", None),
    ("mod", (4, CB, 0), "D", ("mod_turn", (2, GA), 0)), ("K", (1, 0), "A", ("mod", (3, SB), 0)),
    ("mod_turn", (3, SB), "C", ("K", (0,), 0)), ("mod", (4, CB, 1), "D", None),
    ("Q", (1, 0), "B", ("T", (1, 1, 1), 0)), ("mod", (5, GB, 0), "C", ("mod_turn", (3, SB), 0)),
    ("mod_turn", (4, CB), "D", ("mod", (4, CB), 0)), ("Q", (1, 1), "B", None),
    ("mod", (5, GB, 1), "C", None), ("K", (1, 1), "A", None),
    ("mod_turn", (5, GB), "D", ("mod_turn", (4, CB), 0)), ("V", (1, 0), "C", ("mod", (5, GB), 0)),
    ("turn_wo", (), "D", ("mod_turn", (5, GB), 0)), ("gates", ()), ("gate", (), "D", ("turn_wo", (), 0)),
    ("wo_lo", ()), ("V", (1, 1), "C", None), ("row", (), "D", ("gate", (), 0)),
]

ATTENTION = [
    ("S", (0,), "B", ("Q", (1,), -1)), ("load_x", (0, 0)), ("gates", ()), ("stats", (0, 0)),
    ("V", (0, 0), "D", ("row", (), -1)), ("S", (1,), "A", ("K", (1,), -1)), ("norm", (0, 0)),
    ("PT", (0,), "B", ("S", (0,), 0)), ("S", (2,), "C", ("V", (1,), -1)), ("load_x", (0, 1)),
    ("S", (3,), "A", ("S", (1,), 0)), ("PT", (1,), "B", ("PT", (0,), 0)), ("radd", (0,)),
    ("PT", (2,), "C", ("S", (2,), 0)), ("V", (0, 1), "D", None), ("load_r", (2,)),
    ("T", (0, 0, 0), "C", ("PT", (2,), 0)), ("PT", (3,), "B", ("PT", (1,), 0)),
    ("T", (0, 0, 1), "D", ("V", (0,), 0)), ("S", (4,), "A", ("S", (3,), 0)),
    ("S", (5,), "C", ("T", (0, 0, 0), 0)), ("PV", (0, 0), "B", ("PT", (3,), 0)), ("stats", (0, 1)),
    ("load_x", (1, 0)), ("norm", (0, 1)), ("S", (6,), "D", ("T", (0, 0, 1), 0)), ("load_wo", ()),
    ("PT", (4,), "C", ("S", (5,), 0)), ("PV", (0, 1), "B", None), ("load_r", (3,)),
    ("PT", (5,), "A", ("S", (4,), 0)), ("T", (0, 1, 0), "D", ("S", (6,), 0)),
    ("O", (0,), "C", ("PT", (4,), 0)), ("radd", (1,)), ("store", (0,)), ("load_r", (4,)),
    ("PT", (6,), "B", ("PV", (0,), 0)), ("T", (0, 1, 1), "D", ("T", (0, 1, 0), 0)),
    ("S", (7,), "A", ("PT", (5,), 0)), ("O", (1,), "B", ("PT", (6,), 0)), ("store", (1,)),
    ("K", (0, 0), "C", ("O", (0,), 0)), ("radd", (2,)), ("PT", (7,), "D", ("T", (0, 1, 1), 0)),
    ("stats", (1, 0)), ("norm", (1, 0)), ("O", (2,), "A", ("S", (7,), 0)), ("O", (3,), "B", ("O", (1,), 0)),
    ("load_r", (5,)), ("PV", (1, 0), "D", ("PT", (7,), 0)), ("PV", (1, 1), "D", None), ("store", (2,)),
    ("T", (1, 0, 0), "B", ("O", (3,), 0)), ("T", (1, 0, 1), "A", ("O", (2,), 0)), ("K", (0, 1), "C", None),
    ("radd", (3,)), ("store", (3,)), ("stats", (1, 1)), ("radd", (4,)),
    ("O", (4,), "B", ("T", (1, 0, 0), 0)), ("norm", (1, 1)), ("Q", (0, 0), "C", ("K", (0,), 0)),
    ("load_x", (1, 1)), ("store", (4,)), ("Q", (0, 1), "C", None), ("O", (5,), "A", ("T", (1, 0, 1), 0)),
    ("T", (1, 1, 0), "D", ("PV", (1,), 0)), ("radd", (5,)), ("T", (1, 1, 1), "C", ("Q", (0,), 0)),
    ("O", (6,), "A", ("O", (5,), 0)), ("O", (7,), "B", ("O", (4,), 0)), ("load_r", (6,)), ("load_r", (7,)),
    ("gate", (), "D", ("T", (1, 1, 0), 0)), ("store", (5,)), ("load_next", (0,)), ("radd", (6,)),
    ("V", (1, 0), "C", ("T", (1, 1, 1), 0)), ("wo_lo", ()), ("K", (1, 0), "A", ("O", (6,), 0)),
    ("Q", (1, 0), "B", ("O", (7,), 0)), ("load_next", (1,)), ("Q", (1, 1), "B", None),
    ("K", (1, 1), "A", None), ("radd", (7,)), ("V", (1, 1), "C", None), ("store", (6,)),
    ("row", (), "D", ("gate", (), 0)), ("store", (7,)),
]

LAST_ATTENTION = [
    ("load_x", (0, 0)), ("S", (0,), "A", ("K", (1,), -1)), ("S", (1,), "D", ("row", (), -1)),
    ("stats", (0, 0)), ("PT", (0,), "A", ("S", (0,), 0)), ("S", (2,), "C", ("V", (1,), -1)),
    ("V", (0, 0), "D", ("S", (1,), 0)), ("norm", (0, 0)), ("PT", (1,), "B", ("Q", (1,), -1)),
    ("radd", (0,)), ("V", (0, 1), "D", None), ("S", (3,), "B", ("PT", (1,), 0)),
    ("S", (4,), "A", ("PT", (0,), 0)), ("load_x", (0, 1)), ("T", (0, 0, 0), "C", ("S", (2,), 0)),
    ("PT", (2,), "D", ("V", (0,), 0)), ("PT", (3,), "B", ("S", (3,), 0)),
    ("T", (0, 0, 1), "C", ("T", (0, 0, 0), 0)), ("S", (5,), "A", ("S", (4,), 0)), ("load_rows", (0,)),
    ("stats", (0, 1)), ("PV", (0, 0), "D", ("PT", (2,), 0)), ("norm", (0, 1)), ("radd", (1,)),
    ("load_rows", (1,)), ("PV", (0, 1), "D", None), ("PT", (4,), "C", ("T", (0, 0, 1), 0)),
    ("S", (6,), "A", ("S", (5,), 0)), ("turn_w", (0,), "D", ("PV", (0,), 0)), ("load_stack", ()),
    ("load_rows", (2,)), ("turn_w", (1,), "C", ("PT", (4,), 0)), ("store_w2t", (0,)), ("store_w2t", (1,)),
    ("PT", (5,), "B", ("PT", (3,), 0)), ("load_rows", (3,)), ("T", (0, 1, 0), "A", ("S", (6,), 0)),
    ("O", (0,), "C", ("turn_w", (1,), 0)), ("load_x", (1, 0)), ("load_rows", (4,)),
    ("T", (0, 1, 1), "D", ("turn_w", (0,), 0)), ("S", (7,), "A", ("T", (0, 1, 0), 0)),
    ("O", (1,), "D", ("T", (0, 1, 1), 0)), ("load_r", (2,)), ("load_r", (3,)),
    ("PT", (6,), "B", ("PT", (5,), 0)), ("store", (0,)), ("store_w2t", (2,)),
    ("PT", (7,), "C", ("O", (0,), 0)), ("store", (1,)), ("store_w2t", (3,)),
    ("turn_w", (2,), "A", ("S", (7,), 0)), ("stats", (1, 0)), ("turn_w", (3,), "A", ("turn_w", (2,), 0)),
    ("O", (2,), "C", ("PT", (7,), 0)), ("PV", (1, 0), "D", ("O", (1,), 0)),
    ("O", (3,), "B", ("PT", (6,), 0)), ("load_rows", (5,)), ("radd", (2,)), ("load_r", (4,)),
    ("PV", (1, 1), "D", None), ("radd", (3,)), ("load_rows", (6,)), ("store_w2t", (4,)), ("store", (2,)),
    ("store_w2t", (5,)), ("norm", (1, 0)), ("turn_w", (4,), "B", ("O", (3,), 0)), ("store", (3,)),
    ("turn_w", (5,), "D", ("PV", (1,), 0)), ("load_r", (5,)), ("radd", (4,)),
    ("O", (4,), "A", ("turn_w", (3,), 0)), ("T", (1, 0, 0), "C", ("O", (2,), 0)), ("load_rows", (7,)),
    ("T", (1, 0, 1), "D", ("turn_w", (5,), 0)), ("turn_w", (6,), "C", ("T", (1, 0, 0), 0)),
    ("pick_a", (), "B", ("turn_w", (4,), 0)), ("store_w2t", (6,)),
    ("turn_w", (7,), "C", ("turn_w", (6,), 0)), ("picks", ()), ("store", (4,)), ("load_x", (1, 1)),
    ("O", (5,), "B", ("pick_a", (), 0)), ("radd", (5,)), ("stats", (1, 1)),
    ("pick_b", (), "D", ("T", (1, 0, 1), 0)), ("W", (0,), "C", ("turn_w", (7,), 0)), ("store_w2t", (7,)),
    ("load_r", (6,)), ("load_w2t", (0,)), ("load_w2t", (1,)), ("norm", (1, 1)), ("gates2", ()),
    ("W", (1,), "B", ("O", (5,), 0)), ("load_r", (7,)), ("O", (6,), "A", ("O", (4,), 0)), ("W_lo", (0,)),
    ("store", (5,)), ("W_lo", (1,)), ("load_w2t", (2,)), ("radd", (6,)),
    ("T", (1, 1, 0), "B", ("W", (1,), 0)), ("W", (2,), "C", ("W", (0,), 0)),
    ("O", (7,), "D", ("pick_b", (), 0)), ("radd", (7,)), ("gate2", (), "A", ("O", (6,), 0)),
    ("W", (3,), "D", ("O", (7,), 0)), ("load_w2t", (3,)), ("store", (6,)), ("W_lo", (2,)), ("W_lo", (3,)),
    ("row2", (), "B", ("T", (1, 1, 0), 0)), ("store", (7,)), ("load_w2t", (4,)), ("load_w2t", (5,)),
    ("T", (1, 1, 1), "C", ("W", (2,), 0)),
]

ENTER_SECOND = [
    ("W", (4,), "D", ("W", (3,), LAST)), ("W_lo", (4,)), ("load_w2t", (6,)),
    ("W", (5,), "B", ("row2", (), LAST)), ("F", (0, 0, 0, 0), "A", ("gate2", (), LAST)), ("W_lo", (5,)),
    ("radd2", (0, 0, 0)), ("F", (0, 0, 0, 1), "A", None), ("W", (6,), "D", ("W", (4,), 0)),
    ("load_res", (0, 0, 0)), ("F", (0, 0, 0, 2), "A", None), ("F", (0, 0, 0, 3), "A", None),
    ("W", (7,), "D", ("W", (6,), 0)), ("F", (0, 0, 1, 0), "B", ("W", (5,), 0)),
    ("F", (0, 0, 1, 1), "B", None), ("W_lo", (6,)), ("load_res", (0, 0, 1)), ("radd2", (0, 0, 1)),
    ("F", (0, 0, 1, 2), "B", None), ("y_store", (0, 0, 0)), ("W_lo", (7,)), ("load_res", (0, 1, 0)),
    ("load_res", (0, 1, 1)), ("radd2", (0, 1, 0)), ("F", (0, 0, 1, 3), "B", None), ("load_w2t", (7,)),
    ("F", (0, 1, 0, 0), "A", ("F", (0, 0, 0), 0)), ("F", (0, 1, 0, 1), "A", None),
    ("F", (0, 1, 0, 2), "A", None), ("radd2", (0, 1, 1)), ("F", (0, 1, 0, 3), "A", None),
    ("y_store", (0, 0, 1)), ("F", (0, 1, 1, 0), "B", ("F", (0, 0, 1), 0)), ("F", (0, 1, 1, 1), "B", None),
    ("y_store", (0, 1, 0)), ("F", (0, 1, 1, 2), "B", None), ("F", (0, 1, 1, 3), "B", None),
    ("y_store", (0, 1, 1)),
]

SECOND = [
    ("picks", ()), ("load_res", (1, 0, 0)), ("F", (1, 0, 0, 0), "A", ("F", (0, 1, 0), -1)),
    ("F", (1, 0, 0, 1), "A", None), ("load_res", (1, 0, 1)), ("pick_a", (), "C", ("T", (1, 1, 1), -1)),
    ("F", (1, 0, 0, 2), "A", None), ("load_w2t", (0,)), ("load_w2t", (1,)), ("load_x", (0, 0)),
    ("pick_b", (), "C", ("pick_a", (), 0)), ("radd2", (1, 0, 0)), ("stats", (0, 0)), ("norm", (0, 0)),
    ("F", (1, 0, 0, 3), "A", None), ("F", (1, 0, 1, 0), "D", ("W", (7,), -1)), ("load_res", (1, 1, 0)),
    ("radd2", (1, 0, 1)), ("T", (0, 0, 0), "C", ("pick_b", (), 0)), ("load_x", (0, 1)),
    ("F", (1, 0, 1, 1), "D", None), ("T", (0, 0, 1), "A", ("F", (1, 0, 0), 0)), ("load_res", (1, 1, 1)),
    ("F", (1, 0, 1, 2), "D", None), ("load_w2t", (2,)), ("F", (1, 0, 1, 3), "D", None),
    ("radd2", (1, 1, 0)), ("W", (0,), "B", ("F", (0, 1, 1), -1)),
    ("F", (1, 1, 0, 0), "A", ("T", (0, 0, 1), 0)), ("load_w2t", (3,)),
    ("W", (1,), "D", ("F", (1, 0, 1), 0)), ("load_w2t", (4,)), ("load_res", (0, 0, 0)),
    ("load_res", (0, 0, 1)), ("F", (1, 1, 0, 1), "A", None), ("stats", (0, 1)), ("y_store", (1, 0, 0)),
    ("radd2", (1, 1, 1)), ("W_lo", (0,)), ("F", (1, 1, 0, 2), "A", None), ("norm", (0, 1)),
    ("W", (2,), "B", ("W", (0,), 0)), ("load_x", (1, 0)), ("W_lo", (1,)), ("F", (1, 1, 0, 3), "A", None),
    ("y_store", (1, 0, 1)), ("W_lo", (2,)), ("W", (3,), "C", ("T", (0, 0, 0), 0)),
    ("F", (1, 1, 1, 0), "D", ("W", (1,), 0)), ("W_lo", (3,)), ("gates2", ()), ("load_w2t", (5,)),
    ("T", (0, 1, 0), "B", ("W", (2,), 0)), ("y_store", (1, 1, 0)), ("F", (1, 1, 1, 1), "D", None),
    ("T", (0, 1, 1), "A", ("F", (1, 1, 0), 0)), ("F", (1, 1, 1, 2), "D", None),
    ("F", (1, 1, 1, 3), "D", None), ("y_store", (1, 1, 1)), ("stats", (1, 0)), ("load_res", (0, 1, 0)),
    ("gate2", (), "B", ("T", (0, 1, 0), 0)), ("F", (0, 0, 0, 0), "C", ("W", (3,), 0)), ("norm", (1, 0)),
    ("F", (0, 0, 0, 1), "C", None), ("load_w2t", (6,)), ("W", (4,), "B", ("gate2", (), 0)),
    ("row2", (), "D", ("F", (1, 1, 1), 0)), ("F", (0, 0, 0, 2), "C", None), ("radd2", (0, 0, 0)),
    ("W", (5,), "A", ("T", (0, 1, 1), 0)), ("radd2", (0, 0, 1)), ("W_lo", (4,)),
    ("F", (0, 0, 0, 3), "C", None), ("W_lo", (5,)), ("load_res", (0, 1, 1)),
    ("W", (6,), "A", ("W", (5,), 0)), ("F", (0, 0, 1, 0), "B", ("W", (4,), 0)), ("W_lo", (6,)),
    ("y_store", (0, 0, 0)), ("load_w2t", (7,)), ("radd2", (0, 1, 0)), ("F", (0, 0, 1, 1), "B", None),
    ("W", (7,), "D", ("row2", (), 0)), ("W_lo", (7,)), ("F", (0, 0, 1, 2), "B", None),
    ("T", (1, 0, 0), "C", ("F", (0, 0, 0), 0)), ("F", (0, 0, 1, 3), "B", None), ("load_x", (1, 1)),
    ("F", (0, 1, 0, 0), "A", ("W", (6,), 0)), ("T", (1, 0, 1), "B", ("F", (0, 0, 1), 0)),
    ("F", (0, 1, 0, 1), "A", None), ("radd2", (0, 1, 1)), ("stats", (1, 1)), ("norm", (1, 1)),
    ("F", (0, 1, 0, 2), "A", None), ("y_store", (0, 0, 1)), ("F", (0, 1, 0, 3), "A", None),
    ("F", (0, 1, 1, 0), "B", ("T", (1, 0, 1), 0)), ("y_store", (0, 1, 0)), ("F", (0, 1, 1, 1), "B", None),
    ("T", (1, 1, 0), "C", ("T", (1, 0, 0), 0)), ("F", (0, 1, 1, 2), "B", None),
    ("T", (1, 1, 1), "C", ("T", (1, 1, 0), 0)), ("F", (0, 1, 1, 3), "B", None), ("y_store", (0, 1, 1)),
]

END = [
    ("load_res", (1, 0, 0)), ("load_res", (1, 0, 1)), ("load_res", (1, 1, 0)), ("load_res", (1, 1, 1)),
    ("radd2", (1, 0, 0)), ("F", (1, 0, 0, 0), "A", ("F", (0, 1, 0), -1)), ("F", (1, 0, 0, 1), "A", None),
    ("F", (1, 0, 0, 2), "A", None), ("F", (1, 0, 0, 3), "A", None), ("y_store", (1, 0, 0)),
    ("radd2", (1, 0, 1)), ("F", (1, 0, 1, 0), "B", ("F", (0, 1, 1), -1)), ("F", (1, 0, 1, 1), "B", None),
    ("F", (1, 0, 1, 2), "B", None), ("F", (1, 0, 1, 3), "B", None), ("y_store", (1, 0, 1)),
    ("radd2", (1, 1, 0)), ("F", (1, 1, 0, 0), "A", ("F", (1, 0, 0), 0)), ("F", (1, 1, 0, 1), "A", None),
    ("F", (1, 1, 0, 2), "A", None), ("F", (1, 1, 0, 3), "A", None), ("y_store", (1, 1, 0)),
    ("radd2", (1, 1, 1)), ("F", (1, 1, 1, 0), "B", ("F", (1, 0, 1), 0)), ("F", (1, 1, 1, 1), "B", None),
    ("F", (1, 1, 1, 2), "B", None), ("F", (1, 1, 1, 3), "B", None), ("y_store", (1, 1, 1)),
]

OF_SECOND = ("picks", "pick_a", "pick_b", "gates2", "gate2", "row2", "turn_w", "W", "W_lo", "F",
             "radd2", "y_store", "load_rows", "store_w2t", "load_w2t", "load_res", "load_stack")


def build_block(nc, x, wqkv, bqkv, wo, bo, w2, bias, lora_a, lora_b, starts, c, wmod,
                k_ident, k_sel, k_pick, k_which, y):
    with ExitStack() as ctx:
        def sb(name, shape, dt=F32, at=ctx):
            return at.enter_context(nc.sbuf_tensor(name, shape, dt))

        def sem(name):
            return ctx.enter_context(nc.semaphore(name))

        x1_dram = nc.dram_tensor("x1_dram", [B * S, H], F32, kind="Internal").ap()
        w2t_dram = nc.dram_tensor("w2t_dram", [2 * CT // 2, P, 2 * BANK], F32, kind="Internal").ap()
        lora_dram = nc.dram_tensor("lora_dram", [2, P, H], F32, kind="Internal").ap()

        pair = {n: ctx.enter_context(nc.psum_tensor(f"pair{n}", [P, 2 * BANK], F32)) for n in "ABCD"}

        ident = sb("ident", [P, P])
        modT = sb("modT", [P, MODS, CT, B])
        boT = sb("boT", [P, CT])
        biasT = sb("biasT", [P, CT])
        bqkvT = sb("bqkvT", [P, 3 * DT])
        picked = sb("picked", [P, B])
        cur = sb("cur", [P, 2, CT])
        gate_col = sb("gate_col", [P, CT])
        row_col = sb("row_col", [P, CT])
        bn = sb("bn", [P, 2, 2, 6])
        mv = sb("mv", [P, 2, 2])
        rstd = sb("rstd", [P, 2, 2])
        power = sb("power", [P, 2])
        eps = sb("eps", [P, 2])
        fence = sb("fence", [P, 1])
        neg_max = sb("neg_max", [P, QT])
        total = sb("total", [P, QT])
        r_total = sb("r_total", [P, QT])
        xs = sb("xs", [P, 2, H])
        h_hi, h_lo = [sb("h0_hi", [P, CT, CHUNK], F32R)], [sb("h0_lo", [P, CT, CHUNK], F32R)]
        with ExitStack() as early:
            c_rows = sb("c_rows", [B * CT, P], at=early)
            c_exp = sb("c_exp", [B * CT, P], at=early)
            a_raw = sb("a_raw", [P, H], at=early)
            a_both = sb("a_both", [P, H], F32R, at=early)
            b_raw = sb("b_raw", [P, CT, P], at=early)
            b_both = sb("b_both", [P, H], F32R, at=early)
            start_i = sb("start_i", [P, B], I32, at=early)
            start_f = sb("start_f", [P, B], at=early)
            which = sb("which", [P, 1], at=early)
            le = sb("le", [P, B, B], at=early)
            s1 = sb("s1", [P, B], at=early)
            s2 = sb("s2", [P, B], at=early)
            s3 = sb("s3", [P, B], at=early)
        h_hi.append(sb("h1_hi", [P, CT, CHUNK], F32R))
        h_lo.append(sb("h1_lo", [P, CT, CHUNK], F32R))
        pt_hi, pt_lo = h_hi[1], h_lo[1]
        with ExitStack() as first:
            w_hi = sb("w_hi", [P, CT, 3 * D], F32R, at=first)
            w_lo = sb("w_lo", [P, CT, 3 * D], F32R, at=first)
            with ExitStack() as early:
                wm = sb("wm", [P, WM, H], at=early)
                scT = sb("scT", [P, CT, 32], at=early)
                sel = sb("sel", [P, B], at=early)
                sign = sb("sign", [P, CT * B], at=early)
                size = sb("size", [P, CT * B], at=early)
                mod_rows = sb("mod_rows", [P, H], at=early)
                w_raw = sb("w_raw", [P, CT, 3 * D], at=early)
            wo_hi = sb("wo_hi", [P, DT, H], F32R, at=first)
            wo_lo = sb("wo_lo", [P, DT, H], F32R, at=first)
            probs = sb("probs", [P, 2, S], at=first)
            xr = sb("xr", [P, 2, H], at=first)
            row_bc = sb("row_bc", [P, H], at=first)
            q_hi = sb("q_hi", [P, DT, S], F32R, at=first)
            q_lo = sb("q_lo", [P, DT, S], F32R, at=first)
            k_hi = sb("k_hi", [P, DT, S], F32R, at=first)
            k_lo = sb("k_lo", [P, DT, S], F32R, at=first)
            v_hi = sb("v_hi", [P, QT, D], F32R, at=first)
            v_lo = sb("v_lo", [P, QT, D], F32R, at=first)
        w2t = sb("w2t", [P, 2, 2 * BANK])
        w_sum = sb("w_sum", [P, 2, 2 * BANK])
        w2_rows = w_sum
        a_stack = sb("a_stack", [P, H], F32R)
        b_stack = sb("b_stack", [P, H], F32R)
        a_used = sb("a_used", [P, H], F32R)
        b_used = sb("b_used", [P, H], F32R)
        pick = sb("pick", [P, 2, P])
        pick_b = sb("pick_b", [P, 2, P], F32R)
        gate_bc = sb("gate_bc", [P, H])
        row2_bc = sb("row2_bc", [P, H])
        res = sb("res", [P, 4, 2 * BANK])
        later_hi = sb("w2_hi1", [P, CT, BANK], F32R)
        later_lo = sb("w2_lo1", [P, CT, BANK], F32R)
        gated = sb("gated", [P, 2 * BANK])
        sb("spacer", [P, 6 * 256])
        w2_hi = [sb("w2_hi0", [P, CT, BANK], F32R), later_hi]
        w2_lo = [sb("w2_lo0", [P, CT, BANK], F32R), later_lo]

        ld_const = sem("ld_const")
        ld_c = sem("ld_c")
        ld_lora = sem("ld_lora")
        ld_wm = [sem(f"ld_wm{i}") for i in range(WM)]
        ld_w = [sem(f"ld_w{i}") for i in range(4)]
        ld_xs = [sem(f"ld_xs{i}") for i in range(2)]
        ld_xr = [sem(f"ld_xr{i}") for i in range(2)]
        ld_wo = sem("ld_wo")
        st_x1 = [sem(f"st_x1_{i}") for i in range(2)]
        st_lora = sem("st_lora")
        ld_stack = sem("ld_stack")
        ld_rows = [sem(f"ld_rows{i}") for i in range(2)]
        st_w2t = [sem(f"st_w2t{i}") for i in range(2)]
        ld_w2t = [sem(f"ld_w2t{i}") for i in range(2)]
        ld_res = [sem(f"ld_res{i}") for i in range(4)]
        st_y = [sem(f"st_y{i}") for i in range(4)]
        v_step = sem("v_step")
        g_step = sem("g_step")
        zeroed = sem("zeroed")
        c_expd = sem("c_expd")
        c_silu = sem("c_silu")
        c_turned = sem("c_turned")
        c_ready = sem("c_ready")
        lora_turned = sem("lora_turned")
        lora_hi = sem("lora_hi")
        lora_lo = sem("lora_lo")
        mod_used = sem("mod_used")
        mod_copied = sem("mod_copied")
        mod_turned = sem("mod_turned")
        mod_made = sem("mod_made")
        w_hi_made = sem("w_hi_made")
        w_lo_made = sem("w_lo_made")
        wo_turned = sem("wo_turned")
        wo_row_made = sem("wo_row_made")
        bn_made = sem("bn_made")
        mv_made = sem("mv_made")
        var_eps = sem("var_eps")
        rstd_made = sem("rstd_made")
        x_normed = sem("x_normed")
        h_turned = sem("h_turned")
        h_affine = sem("h_affine")
        h_hi_made = sem("h_hi_made")
        h_lo_made = sem("h_lo_made")
        q_done, k_done, v_done = sem("q_done"), sem("k_done"), sem("v_done")
        q_hi_made, k_hi_made, v_hi_made = sem("q_hi_made"), sem("k_hi_made"), sem("v_hi_made")
        q_lo_made, k_lo_made, v_lo_made = sem("q_lo_made"), sem("k_lo_made"), sem("v_lo_made")
        gates_made = sem("gates_made")
        gate_done = sem("gate_done")
        wo_gated = sem("wo_gated")
        wo_hi_made = sem("wo_hi_made")
        wo_lo_made = sem("wo_lo_made")
        row_done = sem("row_done")
        row_made = sem("row_made")
        s_done = sem("s_done")
        max_made = sem("max_made")
        exp_made = sem("exp_made")
        r_total_made = sem("r_total_made")
        pt_done = sem("pt_done")
        pt_hi_made = sem("pt_hi_made")
        pt_lo_made = sem("pt_lo_made")
        pv_done = sem("pv_done")
        o_hi_made = sem("o_hi_made")
        o_lo_made = sem("o_lo_made")
        o_done = sem("o_done")
        residual_made = sem("residual_made")
        x1_made = sem("x1_made")
        picks_made = sem("picks_made")
        pick_done = sem("pick_done")
        picked_made = sem("picked_made")
        gates2_made = sem("gates2_made")
        gate2_done = sem("gate2_done")
        gate2_made = sem("gate2_made")
        row2_done = sem("row2_done")
        row2_made = sem("row2_made")
        w2_turned = sem("w2_turned")
        w2t_made = sem("w2t_made")
        lora_done = sem("lora_done")
        w_sum_made = sem("w_sum_made")
        w2_hi_made = sem("w2_hi_made")
        w2_lo_made = sem("w2_lo_made")
        f_done = sem("f_done")
        residual2_made = sem("residual2_made")
        y_gated = sem("y_gated")
        y_made = sem("y_made")

        def round_no(stage, b, j, r):
            return 4 * (b + 1) + 2 * j + r + stage * 2 * 2 * B

        def turn_no(stage, b, j, r, half):
            return 2 * round_no(stage, b, j, r) + half

        def f_no(b, j, h, p):
            return QT * (b if j else b + 1) + 4 * j + 2 * h + p

        def v_no(b, j, p):
            return 4 * (b + 1) + p if j else 4 * b + 2 + p

        def wait(eng, s, value):
            if not isinstance(value, int) or value > 0:
                eng.wait_ge(s, value)

        def wait_emptied(eng, before, b, prep):
            if before is None:
                return
            what, i, turn = before
            stage, pb = prep
            if turn == LAST:
                b, stage, pb = LAST, 1, -1
            else:
                b, pb = b + turn, pb + turn
            if what in OF_SECOND or what == "T":
                b = pb
            s, value = {
                "turn_c": lambda: (c_ready, 1),
                "turn_lora": lambda: (lora_lo, 2),
                "mod": lambda: (mod_copied, i[0] + 1),
                "mod_turn": lambda: (mod_made, i[0] + 1),
                "turn_wo": lambda: (wo_row_made, 1),
                "T": lambda: (h_affine, 4 * turn_no(stage, b, *i) + 4),
                "Q": lambda: (q_lo_made, 2 * (2 * (b + 1) + i[0]) + 2),
                "K": lambda: (k_lo_made, 2 * (2 * (b + 1) + i[0]) + 2),
                "V": lambda: (v_lo_made, v_no(b, i[0], 1) + 1),
                "gate": lambda: (wo_gated, DT * (b + 1) + DT),
                "row": lambda: (row_made, b + 2),
                "S": lambda: (exp_made, QT * b + i[0] + 1),
                "PT": lambda: (pt_lo_made, QT * b + i[0] + 1),
                "PV": lambda: (o_lo_made, 4 * b + 2 * i[0] + 2),
                "O": lambda: (x1_made, QT * b + i[0] + 1),
                "pick_a": lambda: (picked_made, 2 * (b + 1) + 1),
                "pick_b": lambda: (picked_made, 2 * (b + 1) + 2),
                "gate2": lambda: (gate2_made, b + 2),
                "row2": lambda: (row2_made, b + 2),
                "turn_w": lambda: (w2t_made, i[0] + 1),
                "W": lambda: (w_sum_made, 8 * (b + 1) + i[0] + 1),
                "F": lambda: (y_gated, f_no(b, *i) + 1),
            }[what]()
            wait(eng, s, value)

        def h_parts(j, r, ct):
            where = (slice(None), slice(ct, ct + 2), slice(2 * r * P, 2 * (r + 1) * P))
            return (xs[:, :, ct * P:(ct + 2) * P].rearrange("p k (c n) -> p c k n", c=2),
                    h_hi[j][where].rearrange("p c (k n) -> p c k n", k=2),
                    h_lo[j][where].rearrange("p c (k n) -> p c k n", k=2))

        block = ctx.enter_context(nc.Block())

        @block.sync
        def _(sp):
            def load_xs(stage, b, j, r):
                wait(sp, h_lo_made, 2 * turn_no(stage, b, j, r, 0))
                src = x if stage == 0 else x1_dram
                if stage == 1:
                    for i in range(2):
                        wait(sp, st_x1[i], 16 * QT // 2 * (b + 2))
                for i in range(2):
                    row = (b + 1) * S + j * CHUNK + (2 * r + i) * P
                    sp.dma_start(xs[:, i, :], src[bass.ds(row, P), :]).then_inc(ld_xs[i], 16)

            def load_wm(n, q):
                slot, k = n % WM, n % CT
                wait(sp, mod_used, n - WM + 1)
                sp.dma_start(wm[:, slot, :], wmod[k * P:(k + 1) * P, q * H:(q + 1) * H]).then_inc(ld_wm[slot], 16)

            def load_residual(b, t):
                wait(sp, st_x1[t % 2], 16 * (QT // 2 * b + t // 2))
                sp.dma_start(xr[:, t % 2, :], x[bass.ds(b * S + t * P, P), :]).then_inc(ld_xr[t % 2], 16)

            def load_wo(b):
                wait(sp, pt_done, QT * (b + 1))
                sp.dma_start(probs[:, :, :], wo.rearrange("(d p) n -> p d n", p=P)).then_inc(ld_wo, 16)

            def load_rows(n):
                h, cp = n // 4, n % 4
                if n < 2:
                    sp.wait_ge(v_done, 4 * B)
                wait(sp, w2_turned, n - 1)
                src = w2[h * BANK:(h + 1) * BANK, cp * 2 * P:(cp + 1) * 2 * P]
                sp.dma_start(w2_rows[:, n % 2, :].rearrange("p (o c) -> p o c", o=4),
                             src.rearrange("(o p) c -> p o c", p=P)).then_inc(ld_rows[n % 2], 16)

            def store_w2t(n):
                sp.wait_ge(w2t_made, n + 1)
                sp.dma_start(w2t_dram[n], w2t[:, n % 2, :]).then_inc(st_w2t[n % 2], 16)

            def load_stack():
                sp.wait_ge(v_done, 4 * B)
                sp.dma_start(pick[:, :, :], k_pick.rearrange("s p n -> p s n")).then_inc(ld_stack, 16)
                sp.dma_start(a_stack[:, :].bitcast(F32), lora_dram[0]).then_inc(ld_stack, 16)
                sp.dma_start(b_stack[:, :].bitcast(F32), lora_dram[1]).then_inc(ld_stack, 16)

            def load_w2t(b, n):
                wait(sp, w_sum_made, 8 * (b + 1) + n - 1)
                sp.wait_ge(st_w2t[n % 2], 16 * 4)
                sp.dma_start(w2t[:, n % 2, :], w2t_dram[n]).then_inc(ld_w2t[n % 2], 16)

            def load_res(b, j, h, p):
                slot = 2 * h + p
                batch = b if j else b + 1
                if j == 0 and isinstance(b, int) and b < 0:
                    sp.wait_ge(o_done, QT * B)
                    for i in range(2):
                        sp.wait_ge(st_x1[i], 16 * QT // 2 * B)
                else:
                    sp.wait_ge(st_y[slot], 16 * (2 * batch + j))
                row = batch * S + j * CHUNK + p * 2 * P
                src = x1_dram[bass.ds(row, 2 * P), h * BANK:(h + 1) * BANK].rearrange("(t p) n -> p t n", p=P)
                sp.dma_start(res[:, slot, :].rearrange("p (t n) -> p t n", t=2), src).then_inc(ld_res[slot], 16)

            def step(entry, b, prep):
                what, i = entry[0], entry[1]
                if what in OF_SECOND:
                    b = prep[1]
                if what == "load_x":
                    load_xs(*prep, *i)
                elif what == "load_r":
                    load_residual(b, *i)
                elif what == "load_next":
                    load_residual(b + 1, *i)
                elif what == "load_wo":
                    load_wo(b)
                elif what == "load_rows":
                    load_rows(*i)
                elif what == "store_w2t":
                    store_w2t(*i)
                elif what == "load_stack":
                    load_stack()
                elif what == "load_w2t":
                    load_w2t(b, *i)
                elif what == "load_res":
                    load_res(b, *i)

            sp.dma_start(c_rows[:, :], c.rearrange("b (k n) -> (b k) n", n=P)).then_inc(ld_c, 16)
            sp.dma_start(ident[:, :], k_ident).then_inc(ld_const, 16)
            sp.dma_start(sel[:, :], k_sel).then_inc(ld_const, 16)
            for k in range(CT):
                if k == WM:
                    load_xs(0, -1, 0, 0)
                load_wm(k, CA)
            for k in range(CT):
                load_wm(CT + k, SA)
            for n in range(4):
                sp.dma_start(w_raw[:, 2 * n:2 * n + 2, :], wqkv[2 * n * P:(2 * n + 2) * P, :].rearrange(
                    "(c p) n -> p c n", p=P)).then_inc(ld_w[n], 16)
                if n == 1:
                    load_xs(0, -1, 0, 1)
            load_xs(0, -1, 1, 0)
            for s, q in ((2, GA), (3, SB), (4, CB), (5, GB)):
                for k in range(CT):
                    load_wm(s * CT + k, q)
                if s == 2:
                    load_xs(0, -1, 1, 1)
            sp.wait_ge(mod_used, MODS * CT)
            load_wo(-1)
            sp.wait_ge(mod_made, MODS)
            load_residual(0, 0)
            load_residual(0, 1)
            with sp.Fori(0, B - 1) as b:
                for entry in ATTENTION:
                    step(entry, b, (0, b))
            for entry in LAST_ATTENTION:
                step(entry, LAST, (1, -1))
            for entry in ENTER_SECOND:
                step(entry, -1, (1, -1))
            with sp.Fori(0, B - 1) as b:
                for entry in SECOND:
                    step(entry, b, (1, b))
            for entry in END:
                step(entry, LAST, (1, LAST))

        @block.gpsimd
        def _(pool):
            nc.gpsimd.memset(power[:, :], -0.5).then_inc(g_step, 1)
            nc.gpsimd.memset(eps[:, :], EPS).then_inc(g_step, 1)
            pool.wait_ge(zeroed, 3)
            for at in (0, LO_ROW):
                pool.dma_start(a_raw[at:at + NL * RANK, :], lora_a.rearrange("n r d -> (n r) d")).then_inc(ld_lora, 16)
                for n in range(NL):
                    pool.dma_start(b_raw[:, :, at + n * RANK:at + (n + 1) * RANK],
                                   lora_b[n].rearrange("(t p) r -> p t r", p=P)).then_inc(ld_lora, 16)
            pool.dma_start(start_i[:, :], starts.partition_broadcast(P)).then_inc(ld_lora, 16)
            pool.dma_start(which[:, :], k_which).then_inc(ld_lora, 16)
            pool.dma_start(bqkvT[:, :], bqkv.rearrange("(f p) -> p f", p=P),
                               allow_slow_non_contiguous=True).then_inc(ld_lora, 16)
            pool.dma_start(boT[:, :], bo.rearrange("(f p) -> p f", p=P),
                               allow_slow_non_contiguous=True).then_inc(ld_lora, 16)
            pool.dma_start(biasT[:, :], bias.rearrange("(f p) -> p f", p=P),
                               allow_slow_non_contiguous=True).then_inc(ld_lora, 16)

            def step(entry, b, stage, prep):
                what, i = entry[0], entry[1]
                if what in OF_SECOND:
                    b = prep[1]
                if what == "turn_lora":
                    pool.wait_ge(lora_lo, 2)
                    pool.dma_start(lora_dram[0], a_both[:, :].bitcast(F32)).then_inc(st_lora, 16)
                    pool.dma_start(lora_dram[1], b_both[:, :].bitcast(F32)).then_inc(st_lora, 16)
                elif what == "stats":
                    n = round_no(*prep, *i)
                    pool.wait_ge(mv_made, 2 * n + 2)
                    nc.gpsimd.tensor_tensor(rstd[:, 0, :], mv[:, :, 1], eps[:, :], ALU.add).then_inc(var_eps, 1)
                    pool.wait_ge(var_eps, n + 1)
                    nc.gpsimd.tensor_tensor(rstd[:, 1, :], rstd[:, 0, :], power[:, :], ALU.pow).then_inc(rstd_made, 1)
                elif what == "radd":
                    t = i[0]
                    pool.wait_ge(ld_xr[t % 2], 16 * (QT // 2 * b + t // 2 + 1))
                    pool.wait_ge(row_made, b + 1)
                    xt = xr[:, t % 2, :]
                    nc.gpsimd.tensor_tensor(xt, xt, row_bc[:, :], ALU.add).then_inc(residual_made, 1)
                elif what == "store":
                    t = i[0]
                    pool.wait_ge(x1_made, QT * b + t + 1)
                    pool.dma_start(x1_dram[bass.ds(b * S + t * P, P), :], xr[:, t % 2, :]).then_inc(st_x1[t % 2], 16)
                elif what == "radd2":
                    j, h, p = i
                    n = f_no(b, j, h, p)
                    slot, batch = 2 * h + p, (b if j else b + 1)
                    pool.wait_ge(ld_res[slot], 16 * (2 * batch + j + 1))
                    pool.wait_ge(row2_made, batch + 1)
                    rt = res[:, slot, :].rearrange("p (t n) -> p t n", t=2)
                    row = row2_bc[:, h * BANK:(h + 1) * BANK].unsqueeze(1).to_broadcast([P, 2, BANK])
                    nc.gpsimd.tensor_tensor(rt, rt, row, ALU.add).then_inc(residual2_made, 1)
                elif what == "y_store":
                    j, h, p = i
                    n = f_no(b, j, h, p)
                    slot, batch = 2 * h + p, (b if j else b + 1)
                    pool.wait_ge(y_made, n + 1)
                    dst = y[bass.ds(batch * S + j * CHUNK + p * 2 * P, 2 * P), h * BANK:(h + 1) * BANK]
                    pool.dma_start(dst.rearrange("(t p) n -> p t n", p=P),
                                   res[:, slot, :].rearrange("p (t n) -> p t n", t=2)).then_inc(st_y[slot], 16)

            pool.wait_ge(g_step, 2)
            for entry in FIRST:
                step(entry, -1, 0, (0, -1))
            with pool.Fori(0, B - 1) as b:
                for entry in ATTENTION:
                    step(entry, b, 0, (0, b))
            for entry in LAST_ATTENTION:
                step(entry, LAST, 0, (1, -1))
            for entry in ENTER_SECOND:
                step(entry, -1, 1, (1, -1))
            with pool.Fori(0, B - 1) as b:
                for entry in SECOND:
                    step(entry, b, 1, (1, b))
            for entry in END:
                step(entry, LAST, 1, (1, LAST))
            for slot in range(4):
                pool.wait_ge(st_y[slot], 16 * 2 * B)
            pool.wait_ge(st_lora, 32)

        @block.scalar
        def _(act):
            def emptied_copy(dst, src, made):
                nc.scalar.activation(dst, src, ACT.Copy).then_inc(made, 1)

            def step(entry, b, stage, prep):
                what, i = entry[0], entry[1]
                if what in OF_SECOND:
                    b = prep[1]
                ps = pair[entry[2]] if len(entry) > 2 else None
                if what == "turn_lora":
                    act.wait_ge(ld_lora, 16 * 13)
                    nc.scalar.activation(a_both[:, :], a_raw[:, :], ACT.Copy).then_inc(lora_hi, 1)
                    act.wait_ge(lora_turned, 1)
                    nc.scalar.activation(b_both[:, :], ps[:, :], ACT.Copy).then_inc(lora_hi, 1)
                elif what == "mod":
                    if i[2] == 0:
                        return
                    act.wait_ge(mod_used, CT * (i[0] + 1))
                    wait(act, mod_turned, i[0])
                    emptied_copy(mod_rows[:, :], ps[:, :], mod_copied)
                elif what == "w_split":
                    n = i[0]
                    act.wait_ge(ld_w[n], 16)
                    c2 = slice(2 * n, 2 * n + 2)
                    nc.scalar.activation(w_hi[:, c2, 0:D], w_raw[:, c2, 0:D], ACT.Copy, scale=SCALE).then_inc(w_hi_made, 1)
                    nc.scalar.activation(w_hi[:, c2, D:], w_raw[:, c2, D:], ACT.Copy).then_inc(w_hi_made, 1)
                elif what == "T":
                    j, r, half = i
                    n = turn_no(*prep, *i)
                    act.wait_ge(h_turned, n + 1)
                    if stage == 0 and entry in FIRST and i == (1, 0, 0):
                        act.wait_ge(st_lora, 32)
                    if stage == 0 and i == (1, 0, 0) and not (isinstance(b, int) and b < 0):
                        act.wait_ge(pv_done, 4 * (b + 1))
                    for sub in range(2):
                        for cc in range(2):
                            ct = 4 * half + 2 * sub + cc
                            nc.scalar.activation(xs[:, :, ct * P:(ct + 1) * P],
                                                 ps[:, (2 * sub + cc) * 2 * P:(2 * sub + cc + 1) * 2 * P].rearrange(
                                                     "p (k n) -> p k n", k=2),
                                                 ACT.Identity, bias=cur[:, 1, ct:ct + 1],
                                                 scale=cur[:, 0, ct:ct + 1]).then_inc(h_affine, 1)
                    for sub in range(2):
                        act.wait_ge(h_affine, 4 * n + 2 * sub + 2)
                        h, hi, _ = h_parts(j, r, 4 * half + 2 * sub)
                        nc.scalar.activation(hi, h, ACT.Copy).then_inc(h_hi_made, 1)
                elif what in ("Q", "K"):
                    n = 2 * (b + 1) + i[0]
                    done, made, dst, col = (q_done, q_hi_made, q_hi, 0) if what == "Q" else (k_done, k_hi_made, k_hi, DT)
                    m = i[1]
                    act.wait_ge(done, 2 * n + m + 1)
                    nc.scalar.activation(dst[:, m, i[0] * CHUNK:(i[0] + 1) * CHUNK], ps[:, m * BANK:(m + 1) * BANK],
                                         ACT.Identity, bias=bqkvT[:, col + m:col + m + 1]).then_inc(made, 1)
                elif what == "V":
                    p = i[1]
                    act.wait_ge(v_done, v_no(b, i[0], p) + 1)
                    emptied_copy(v_hi[:, 4 * i[0] + 2 * p:4 * i[0] + 2 * p + 2, :],
                                 ps[:, p * BANK:(p + 1) * BANK].rearrange("p (t n) -> p t n", t=2), v_hi_made)
                elif what == "gate":
                    for d in range(DT):
                        act.wait_ge(wo_gated, DT * (b + 1) + d + 1)
                        nc.scalar.activation(wo_hi[:, d, :], probs[:, d, :], ACT.Copy).then_inc(wo_hi_made, 1)
                elif what == "row":
                    act.wait_ge(row_done, b + 2)
                    wait(act, residual_made, QT * (b + 1))
                    emptied_copy(row_bc[:, :], ps[:, :], row_made)
                elif what == "S":
                    t = i[0]
                    act.wait_ge(max_made, QT * b + t + 1)
                    if t >= 2:
                        act.wait_ge(pt_done, QT * b + t - 1)
                    else:
                        act.wait_ge(wo_lo_made, DT * (b + 1))
                    nc.scalar.activation(probs[:, t % 2, :], ps[:, :], ACT.Exp, bias=neg_max[:, t:t + 1],
                                         accum_out=total[:, t:t + 1]).then_inc(exp_made, 1)
                elif what == "PT":
                    t = i[0]
                    act.wait_ge(pt_done, QT * b + t + 1)
                    if t == 4:
                        act.wait_ge(pv_done, 4 * b + 2)
                    nc.scalar.activation(pt_hi[:, :, (t % 4) * P:(t % 4 + 1) * P],
                                         ps[:, :].rearrange("p (k q) -> p k q", q=P), ACT.Copy).then_inc(pt_hi_made, 1)
                elif what == "PV":
                    m = i[1]
                    act.wait_ge(pv_done, 4 * b + 2 * i[0] + m + 1)
                    nc.scalar.activation(q_hi[:, m, i[0] * CHUNK:(i[0] + 1) * CHUNK], ps[:, m * BANK:(m + 1) * BANK],
                                         ACT.Copy).then_inc(o_hi_made, 1)
                elif what in ("pick_a", "pick_b"):
                    side = 0 if what == "pick_a" else 1
                    act.wait_ge(pick_done, 2 * (b + 1) + side + 1)
                    emptied_copy((a_used, b_used)[side][:, :], ps[:, :], picked_made)
                elif what == "gate2":
                    act.wait_ge(gate2_done, b + 2)
                    wait(act, y_gated, QT * (b + 1))
                    emptied_copy(gate_bc[:, :], ps[:, :], gate2_made)
                elif what == "row2":
                    act.wait_ge(row2_done, b + 2)
                    wait(act, residual2_made, QT * (b + 1))
                    emptied_copy(row2_bc[:, :], ps[:, :], row2_made)
                elif what == "turn_w":
                    n = i[0]
                    act.wait_ge(w2_turned, n + 1)
                    if n >= 2:
                        act.wait_ge(st_w2t[n % 2], 16 * (n // 2))
                    emptied_copy(w2t[:, n % 2, :], ps[:, :], w2t_made)
                elif what == "W":
                    n = 8 * (b + 1) + i[0]
                    h, cp = i[0] // 4, i[0] % 4
                    act.wait_ge(w_sum_made, n + 1)
                    if h == 1 and isinstance(b, int) and b < 0:
                        for k in range(2):
                            act.wait_ge(st_x1[k], 16 * QT // 2 * B)
                    nc.scalar.activation(w2_hi[h][:, 2 * cp:2 * cp + 2, :],
                                         w_sum[:, n_slot(i), :].rearrange("p (c n) -> p c n", c=2),
                                         ACT.Copy).then_inc(w2_hi_made, 1)
                elif what == "turn_c":
                    act.wait_ge(ld_c, 16)
                    nc.scalar.activation(c_exp[:, :], c_rows[:, :], ACT.Exp, scale=-1.0).then_inc(c_expd, 1)

            def n_slot(i):
                return i[0] % 2

            for entry in FIRST:
                step(entry, -1, 0, (0, -1))
            with act.Fori(0, B - 1) as b:
                for entry in ATTENTION:
                    step(entry, b, 0, (0, b))
            for entry in LAST_ATTENTION:
                step(entry, LAST, 0, (1, -1))
            for entry in ENTER_SECOND:
                step(entry, -1, 1, (1, -1))
            with act.Fori(0, B - 1) as b:
                for entry in SECOND:
                    step(entry, b, 1, (1, b))

        @block.vector
        def _(dve):
            chain = [0]

            def link(ins):
                chain[0] += 1
                ins.then_inc(v_step, 1)
                dve.wait_ge(v_step, chain[0])

            def step(entry, b, stage, prep):
                what, i = entry[0], entry[1]
                if what in OF_SECOND:
                    b = prep[1]
                ps = pair[entry[2]] if len(entry) > 2 else None
                if what == "turn_c":
                    dve.wait_ge(c_expd, 1)
                    link(nc.vector.tensor_scalar(c_exp[:, :], c_exp[:, :], 1.0, None, ALU.add))
                    link(nc.vector.reciprocal(c_exp[:, :], c_exp[:, :]))
                    nc.vector.tensor_tensor(c_rows[:, :], c_rows[:, :], c_exp[:, :], ALU.mult).then_inc(c_silu, 1)
                    dve.wait_ge(c_turned, 1)
                    dve.wait_ge(zeroed, 1)
                    nc.vector.tensor_copy(scT[:, :, 0:B], ps[:, 0:B * CT].rearrange("p (b k) -> p k b", b=B)).then_inc(c_ready, 1)
                    nc.vector.memset(a_raw[:, :], 0.0).then_inc(zeroed, 1)
                    nc.vector.memset(b_raw[:, :, :], 0.0).then_inc(zeroed, 1)
                elif what == "turn_lora":
                    dve.wait_ge(ld_lora, 16 * 13)
                    link(nc.vector.tensor_copy(start_f[:, :], start_i[:, :]))
                    for b0 in range(B):
                        ins = nc.vector.tensor_scalar(le[:, :, b0], start_f[:, :], float(b0), None, ALU.is_le)
                    link(ins)
                    link(nc.vector.tensor_tensor(s1[:, :], le[:, 0, :], le[:, 1, :], ALU.mult))
                    link(nc.vector.tensor_tensor(s1[:, :], le[:, 0, :], s1[:, :], ALU.subtract))
                    link(nc.vector.scalar_tensor_tensor(s1[:, :], le[:, 1, :], 2.0, s1[:, :], ALU.mult, ALU.add))
                    link(nc.vector.scalar_tensor_tensor(s2[:, :], le[:, 3, :], 3.0, s1[:, :], ALU.add, ALU.subtract))
                    link(nc.vector.tensor_tensor(s3[:, :], le[:, 2, :], s2[:, :], ALU.mult))
                    link(nc.vector.tensor_tensor(s3[:, :], s3[:, :], s1[:, :], ALU.add))
                    link(nc.vector.tensor_scalar(picked[:, :], s3[:, :], which[:, 0:1], None, ALU.is_equal))
                    link(nc.vector.tensor_scalar(bqkvT[:, 0:DT], bqkvT[:, 0:DT], SCALE, None, ALU.mult))
                    dve.wait_ge(lora_hi, 1)
                    nc.vector.tensor_tensor(a_both[LO_ROW:, :], a_raw[LO_ROW:, :], a_both[LO_ROW:, :].bitcast(F32),
                                            ALU.subtract).then_inc(lora_lo, 1)
                    dve.wait_ge(lora_hi, 2)
                    nc.vector.tensor_tensor(b_both[LO_ROW:, :], ps[LO_ROW:, :], b_both[LO_ROW:, :].bitcast(F32),
                                            ALU.subtract).then_inc(lora_lo, 1)
                elif what == "mod_turn":
                    s, q = i
                    dve.wait_ge(mod_turned, s + 1)
                    src, dst = ps[:, 0:CT * B], modT[:, q, :, :].rearrange("p c b -> p (c b)")
                    if q in (CA, CB):
                        nc.vector.tensor_scalar(dst, src, 1.0, None, ALU.add).then_inc(mod_made, 1)
                    elif q in (SA, SB):
                        nc.vector.tensor_copy(dst, src).then_inc(mod_made, 1)
                    else:
                        link(nc.vector.tensor_copy(dst, src))
                        link(nc.vector.tensor_scalar(sign[:, :], dst, 0.0, 2.0, ALU.is_ge, ALU.mult))
                        link(nc.vector.scalar_tensor_tensor(size[:, :], dst, -1.0, dst, ALU.mult, ALU.max))
                        link(nc.vector.tensor_scalar(size[:, :], size[:, :], 0.25, None, ALU.max))
                        nc.vector.scalar_tensor_tensor(dst, sign[:, :], -1.0, size[:, :], ALU.add,
                                                       ALU.mult).then_inc(mod_made, 1)
                elif what == "w_split":
                    n = i[0]
                    dve.wait_ge(w_hi_made, 2 * n + 2)
                    c2 = slice(2 * n, 2 * n + 2)
                    nc.vector.scalar_tensor_tensor(w_lo[:, c2, 0:D], w_raw[:, c2, 0:D], SCALE,
                                                   w_hi[:, c2, 0:D].bitcast(F32), ALU.mult, ALU.subtract).then_inc(w_lo_made, 1)
                    nc.vector.tensor_tensor(w_lo[:, c2, D:], w_raw[:, c2, D:], w_hi[:, c2, D:].bitcast(F32),
                                            ALU.subtract).then_inc(w_lo_made, 1)
                elif what == "turn_wo":
                    dve.wait_ge(wo_turned, 1)
                    nc.vector.tensor_tensor(boT[:, :], boT[:, :], ps[:, 0:CT], ALU.add).then_inc(wo_row_made, 1)
                elif what == "stats":
                    n = round_no(*prep, *i)
                    for k in range(2):
                        dve.wait_ge(ld_xs[k], 16 * (n + 1))
                        for half in range(2):
                            nc.vector.bn_stats(bn[:, k, half, :], xs[:, k, half * BANK:(half + 1) * BANK]).then_inc(bn_made, 1)
                    dve.wait_ge(bn_made, 4 * n + 4)
                    nc.vector.memset(fence[:, :], 0.0)
                    for k in range(2):
                        nc.vector.bn_aggr(mv[:, k, :], bn[:, k, :, :].rearrange("p h n -> p (h n)")).then_inc(mv_made, 1)
                elif what == "norm":
                    n = round_no(*prep, *i)
                    if i == (0, 0):
                        pst, pb = prep
                        wait(dve, h_affine, 4 * turn_no(pst, pb, 0, 0, 0))
                        if stage == 0 and isinstance(b, int) and b < 0:
                            dve.wait_ge(mod_made, 2)
                        for k, q in enumerate((CA, SA) if pst == 0 else (CB, SB)):
                            src = modT[:, q, :, bass.ds(pb + 1, 1)].rearrange("p c b -> p (c b)")
                            nc.vector.tensor_copy(cur[:, k, :], src)
                    dve.wait_ge(rstd_made, n + 1)
                    for k in range(2):
                        nc.vector.tensor_scalar(xs[:, k, :], xs[:, k, :], mv[:, k, 0:1], rstd[:, 1, k:k + 1],
                                                ALU.subtract, ALU.mult).then_inc(x_normed, 1)
                elif what == "T":
                    j, r, half = i
                    n = turn_no(*prep, *i)
                    for sub in range(2):
                        h, hi, lo = h_parts(j, r, 4 * half + 2 * sub)
                        dve.wait_ge(h_hi_made, 2 * n + sub + 1)
                        nc.vector.tensor_tensor(lo, h, hi.bitcast(F32), ALU.subtract).then_inc(h_lo_made, 1)
                elif what in ("Q", "K"):
                    n = 2 * (b + 1) + i[0]
                    hi_made, made, hi, lo, col = ((q_hi_made, q_lo_made, q_hi, q_lo, 0) if what == "Q"
                                                  else (k_hi_made, k_lo_made, k_hi, k_lo, DT))
                    m = i[1]
                    where = (slice(None), m, slice(i[0] * CHUNK, (i[0] + 1) * CHUNK))
                    dve.wait_ge(hi_made, 2 * n + m + 1)
                    nc.vector.scalar_tensor_tensor(lo[where], ps[:, m * BANK:(m + 1) * BANK],
                                                   bqkvT[:, col + m:col + m + 1], hi[where].bitcast(F32),
                                                   ALU.add, ALU.subtract).then_inc(made, 1)
                elif what == "V":
                    p = i[1]
                    dve.wait_ge(v_hi_made, v_no(b, i[0], p) + 1)
                    where = (slice(None), slice(4 * i[0] + 2 * p, 4 * i[0] + 2 * p + 2), slice(None))
                    nc.vector.tensor_tensor(v_lo[where], ps[:, p * BANK:(p + 1) * BANK].rearrange("p (t n) -> p t n", t=2),
                                            v_hi[where].bitcast(F32), ALU.subtract).then_inc(v_lo_made, 1)
                elif what == "gates":
                    wait(dve, row_done, b + 1)
                    src = modT[:, GA, :, bass.ds(b + 1, 1)].rearrange("p c b -> p (c b)")
                    nc.vector.tensor_copy(gate_col[:, :], src).then_inc(gates_made, 1)
                    dve.wait_ge(wo_row_made, 1)
                    nc.vector.tensor_tensor(row_col[:, :], src, boT[:, :], ALU.mult).then_inc(gates_made, 1)
                elif what == "gate":
                    dve.wait_ge(gate_done, b + 2)
                    dve.wait_ge(ld_wo, 16 * (b + 2))
                    for d in range(DT):
                        nc.vector.tensor_tensor(probs[:, d, :], probs[:, d, :], ps[:, :], ALU.mult).then_inc(wo_gated, 1)
                elif what == "wo_lo":
                    for d in range(DT):
                        dve.wait_ge(wo_hi_made, DT * (b + 1) + d + 1)
                        nc.vector.tensor_tensor(wo_lo[:, d, :], probs[:, d, :], wo_hi[:, d, :].bitcast(F32),
                                                ALU.subtract).then_inc(wo_lo_made, 1)
                elif what == "S":
                    t = i[0]
                    dve.wait_ge(s_done, QT * b + t + 1)
                    nc.vector.tensor_reduce(neg_max[:, t:t + 1], ps[:, :], AX_X, ALU.max, negate=True).then_inc(max_made, 1)
                elif what == "PT":
                    t = i[0]
                    dve.wait_ge(exp_made, QT * b + t + 1)
                    nc.vector.reciprocal(r_total[:, t:t + 1], total[:, t:t + 1]).then_inc(r_total_made, 1)
                    where = (slice(None), slice(None), slice((t % 4) * P, (t % 4 + 1) * P))
                    dve.wait_ge(pt_hi_made, QT * b + t + 1)
                    nc.vector.tensor_tensor(pt_lo[where], ps[:, :].rearrange("p (k q) -> p k q", q=P),
                                            pt_hi[where].bitcast(F32), ALU.subtract).then_inc(pt_lo_made, 1)
                elif what == "PV":
                    m = i[1]
                    dve.wait_ge(o_hi_made, 4 * b + 2 * i[0] + m + 1)
                    where = (slice(None), m, slice(i[0] * CHUNK, (i[0] + 1) * CHUNK))
                    nc.vector.tensor_tensor(q_lo[where], ps[:, m * BANK:(m + 1) * BANK],
                                            q_hi[where].bitcast(F32), ALU.subtract).then_inc(o_lo_made, 1)
                elif what == "O":
                    t = i[0]
                    dve.wait_ge(o_done, QT * b + t + 1)
                    dve.wait_ge(residual_made, QT * b + t + 1)
                    dve.wait_ge(r_total_made, QT * b + t + 1)
                    xt = xr[:, t % 2, :]
                    nc.vector.scalar_tensor_tensor(xt, ps[:, :], r_total[:, t:t + 1], xt, ALU.mult,
                                                   ALU.add).then_inc(x1_made, 1)
                elif what == "picks":
                    wait(dve, pick_done, 2 * (b + 1))
                    if isinstance(b, int) and b < 0:
                        dve.wait_ge(ld_stack, 48)
                    for side in range(2):
                        nc.vector.tensor_scalar(pick_b[:, side, :], pick[:, side, :], picked[:, bass.ds(b + 1, 1)], None,
                                                ALU.mult).then_inc(picks_made, 1)
                elif what == "gates2":
                    wait(dve, row2_done, b + 1)
                    src = modT[:, GB, :, bass.ds(b + 1, 1)].rearrange("p c b -> p (c b)")
                    nc.vector.tensor_copy(gate_col[:, :], src).then_inc(gates2_made, 1)
                    nc.vector.tensor_tensor(row_col[:, :], src, biasT[:, :], ALU.mult).then_inc(gates2_made, 1)
                elif what == "W":
                    n = 8 * (b + 1) + i[0]
                    slot = i[0] % 2
                    dve.wait_ge(lora_done, n + 1)
                    wait(dve, w2_lo_made, n - 1)
                    dve.wait_ge(ld_w2t[slot], 16 * (4 * (b + 1) + i[0] // 2 + 1))
                    nc.vector.tensor_tensor(w_sum[:, slot, :], w2t[:, slot, :], ps[:, :], ALU.add).then_inc(w_sum_made, 1)
                elif what == "W_lo":
                    n = 8 * (b + 1) + i[0]
                    h, cp = i[0] // 4, i[0] % 4
                    where = (slice(None), slice(2 * cp, 2 * cp + 2), slice(None))
                    dve.wait_ge(w2_hi_made, n + 1)
                    nc.vector.tensor_tensor(w2_lo[h][where], w_sum[:, i[0] % 2, :].rearrange("p (c n) -> p c n", c=2),
                                            w2_hi[h][where].bitcast(F32), ALU.subtract).then_inc(w2_lo_made, 1)
                elif what == "F" and i[3] == 3:
                    j, h, p = i[:3]
                    n = f_no(b, j, h, p)
                    slot, batch = 2 * h + p, (b if j else b + 1)
                    dve.wait_ge(f_done, n + 1)
                    dve.wait_ge(gate2_made, batch + 1)
                    wait(dve, y_made, n)
                    gate = gate_bc[:, h * BANK:(h + 1) * BANK].unsqueeze(1).to_broadcast([P, 2, BANK])
                    nc.vector.tensor_tensor(gated[:, :].rearrange("p (t n) -> p t n", t=2),
                                            ps[:, :].rearrange("p (t n) -> p t n", t=2), gate, ALU.mult).then_inc(y_gated, 1)
                    dve.wait_ge(y_gated, n + 1)
                    dve.wait_ge(residual2_made, n + 1)
                    nc.vector.tensor_tensor(res[:, slot, :], res[:, slot, :], gated[:, :], ALU.add).then_inc(y_made, 1)

            nc.vector.memset(scT[:, :, :], 0.0).then_inc(zeroed, 1)
            for entry in FIRST:
                step(entry, -1, 0, (0, -1))
            with dve.Fori(0, B - 1) as b:
                for entry in ATTENTION:
                    step(entry, b, 0, (0, b))
            for entry in LAST_ATTENTION:
                step(entry, LAST, 0, (1, -1))
            for entry in ENTER_SECOND:
                step(entry, -1, 1, (1, -1))
            with dve.Fori(0, B - 1) as b:
                for entry in SECOND:
                    step(entry, b, 1, (1, b))
            for entry in END:
                step(entry, LAST, 1, (1, LAST))

        @block.tensor
        def _(pe):
            def product3(out, left, right, first, last):
                nc.tensor.matmul(out, left[0], right[0], start=first, stop=False)
                nc.tensor.matmul(out, left[0], right[1], start=False, stop=False)
                return nc.tensor.matmul(out, left[1], right[0], start=False, stop=last)

            def both(hi, lo, *where):
                return hi[(slice(None),) + where], lo[(slice(None),) + where]

            def spread(ps, col, done):
                for ct in range(CT):
                    last = nc.tensor.transpose(ps[:, ct * P:(ct + 1) * P], col[:, ct:ct + 1].to_broadcast([P, P]), ident[:, :])
                last.then_inc(done, 1)

            def step(entry, b, stage, prep):
                if len(entry) < 3:
                    return
                what, i, _, before = entry
                ps = pair[entry[2]]
                wait_emptied(pe, before, b, prep)
                if what in OF_SECOND:
                    b = prep[1]
                if what == "turn_c":
                    pe.wait_ge(ld_const, 32)
                    pe.wait_ge(c_silu, 1)
                    nc.tensor.transpose(ps[:, 0:B * CT], c_rows[:, :], ident[0:B * CT, 0:B * CT]).then_inc(c_turned, 1)
                elif what == "turn_lora":
                    pe.wait_ge(ld_lora, 16 * 13)
                    pe.wait_ge(zeroed, 3)
                    for k in range(CT):
                        last = nc.tensor.transpose(ps[:, k * P:(k + 1) * P], b_raw[:, k, :], ident[:, :])
                    last.then_inc(lora_turned, 1)
                elif what == "mod":
                    if i[0] == 0:
                        pe.wait_ge(c_ready, 1)
                    for k in range(4 * i[2], 4 * i[2] + 4):
                        n = CT * i[0] + k
                        q = 32 * (k % 4)
                        pe.wait_ge(ld_wm[n % WM], 16 * (n // WM + 1))
                        for half in range(2):
                            cols = slice(half * BANK, (half + 1) * BANK)
                            last = nc.tensor.matmul(ps[q:q + 32, cols], scT[:, k, :], wm[:, n % WM, cols],
                                                    start=(k < 4), stop=(k >= 4))
                        last.then_inc(mod_used, 1)
                elif what == "mod_turn":
                    pe.wait_ge(mod_copied, i[0] + 1)
                    for k in range(CT):
                        last = nc.tensor.matmul(ps[:, k * B:(k + 1) * B], mod_rows[:, k * P:(k + 1) * P], sel[:, :],
                                                start=True, stop=True)
                    last.then_inc(mod_turned, 1)
                elif what == "T":
                    j, r, half = i
                    n = turn_no(*prep, *i)
                    pe.wait_ge(x_normed, 2 * round_no(*prep, j, r) + 2)
                    for cc in range(4):
                        for k in range(2):
                            ct = 4 * half + cc
                            last = nc.tensor.transpose(ps[:, (2 * cc + k) * P:(2 * cc + k + 1) * P],
                                                       xs[:, k, ct * P:(ct + 1) * P], ident[:, :])
                    last.then_inc(h_turned, 1)
                elif what in ("Q", "K", "V"):
                    j = i[0]
                    if what != "V" or j == 1:
                        pe.wait_ge(h_lo_made, 2 * turn_no(0, b, j, 1, 1) + 2)
                    if stage == 0 and isinstance(b, int):
                        pe.wait_ge(w_lo_made, 8)
                    if what == "V":
                        for t in range(2 * i[1], 2 * i[1] + 2):
                            for ct in range(CT):
                                last = product3(ps[:, t * D:(t + 1) * D], both(h_hi[j], h_lo[j], ct, slice(t * P, (t + 1) * P)),
                                                both(w_hi, w_lo, ct, slice(2 * D, 3 * D)), ct == 0, ct == CT - 1)
                        last.then_inc(v_done, 1)
                    else:
                        m = i[1]
                        at = (0 if what == "Q" else D) + m * P
                        for ct in range(CT):
                            last = product3(ps[:, m * BANK:(m + 1) * BANK], both(w_hi, w_lo, ct, slice(at, at + P)),
                                            both(h_hi[j], h_lo[j], ct, slice(None)), ct == 0, ct == CT - 1)
                        last.then_inc(q_done if what == "Q" else k_done, 1)
                elif what == "turn_wo":
                    pe.wait_ge(ld_wo, 16)
                    for ct in range(CT):
                        for d in range(DT):
                            last = nc.tensor.matmul(ps[:, ct:ct + 1], probs[:, d, ct * P:(ct + 1) * P],
                                                    bqkvT[:, 2 * DT + d:2 * DT + d + 1], start=(d == 0), stop=(d == DT - 1))
                    last.then_inc(wo_turned, 1)
                elif what == "gate":
                    pe.wait_ge(gates_made, 2 * (b + 1) + 1)
                    spread(ps, gate_col, gate_done)
                elif what == "row":
                    pe.wait_ge(gates_made, 2 * (b + 1) + 2)
                    spread(ps, row_col, row_done)
                elif what == "S":
                    t = i[0]
                    pe.wait_ge(q_lo_made, 4 * (b + 1))
                    pe.wait_ge(k_lo_made, 4 * (b + 1))
                    for half in range(2):
                        for d in range(DT):
                            last = product3(ps[:, half * BANK:(half + 1) * BANK], both(q_hi, q_lo, d, slice(t * P, (t + 1) * P)),
                                            both(k_hi, k_lo, d, slice(half * BANK, (half + 1) * BANK)), d == 0, d == DT - 1)
                    last.then_inc(s_done, 1)
                elif what == "PT":
                    t = i[0]
                    pe.wait_ge(exp_made, QT * b + t + 1)
                    for k in range(QT):
                        last = nc.tensor.transpose(ps[:, k * P:(k + 1) * P], probs[:, t % 2, k * P:(k + 1) * P], ident[:, :])
                    last.then_inc(pt_done, 1)
                elif what == "PV":
                    pe.wait_ge(v_lo_made, 4 * (b + 1))
                    pe.wait_ge(pt_lo_made, QT * b + 4 * i[0] + 4)
                    m = i[1]
                    for k in range(QT):
                        last = product3(ps[:, m * BANK:(m + 1) * BANK], both(v_hi, v_lo, k, slice(m * P, (m + 1) * P)),
                                        both(pt_hi, pt_lo, k, slice(None)), k == 0, k == QT - 1)
                    last.then_inc(pv_done, 1)
                elif what == "O":
                    t = i[0]
                    pe.wait_ge(o_lo_made, 4 * b + 2 * (t // 4) + 2)
                    pe.wait_ge(wo_lo_made, DT * (b + 1))
                    for half in range(2):
                        cols = slice(half * BANK, (half + 1) * BANK)
                        for d in range(DT):
                            last = product3(ps[:, cols], both(q_hi, q_lo, d, slice(t * P, (t + 1) * P)),
                                            both(wo_hi, wo_lo, d, cols), d == 0, d == DT - 1)
                    last.then_inc(o_done, 1)
                elif what in ("pick_a", "pick_b"):
                    side = 0 if what == "pick_a" else 1
                    pe.wait_ge(picks_made, 2 * (b + 1) + side + 1)
                    for half in range(2):
                        cols = slice(half * BANK, (half + 1) * BANK)
                        last = nc.tensor.matmul(ps[:, cols], pick_b[:, side, :], (a_stack, b_stack)[side][:, cols],
                                                start=True, stop=True)
                    last.then_inc(pick_done, 1)
                elif what == "gate2":
                    pe.wait_ge(gates2_made, 2 * (b + 1) + 1)
                    spread(ps, gate_col, gate2_done)
                elif what == "row2":
                    pe.wait_ge(gates2_made, 2 * (b + 1) + 2)
                    spread(ps, row_col, row2_done)
                elif what == "turn_w":
                    n = i[0]
                    pe.wait_ge(ld_rows[n % 2], 16 * (n // 2 + 1))
                    for cc in range(2):
                        for o in range(4):
                            last = nc.tensor.transpose(ps[:, (4 * cc + o) * P:(4 * cc + o + 1) * P],
                                                       w2_rows[:, n % 2, (2 * o + cc) * P:(2 * o + cc + 1) * P], ident[:, :])
                    last.then_inc(w2_turned, 1)
                elif what == "W":
                    h, cp = i[0] // 4, i[0] % 4
                    pe.wait_ge(picked_made, 2 * (b + 2))
                    for cc in range(2):
                        ct = 2 * cp + cc
                        last = nc.tensor.matmul(ps[:, cc * BANK:(cc + 1) * BANK], a_used[:, ct * P:(ct + 1) * P],
                                                b_used[:, h * BANK:(h + 1) * BANK], start=True, stop=True)
                    last.then_inc(lora_done, 1)
                elif what == "F":
                    j, h, p, s = i
                    batch = b if j else b + 1
                    if s == 0:
                        pe.wait_ge(w2_lo_made, 8 * batch + 4 * h + 4)
                        pe.wait_ge(h_lo_made, 2 * turn_no(1, batch - 1, j, 1, 1) + 2)
                    t = s // 2
                    for ct in range(4 * (s % 2), 4 * (s % 2) + 4):
                        last = product3(ps[:, t * BANK:(t + 1) * BANK],
                                        both(h_hi[j], h_lo[j], ct, slice((2 * p + t) * P, (2 * p + t + 1) * P)),
                                        both(w2_hi[h], w2_lo[h], ct, slice(None)), ct == 0, ct == CT - 1)
                    if s == 3:
                        last.then_inc(f_done, 1)

            for entry in FIRST:
                step(entry, -1, 0, (0, -1))
            with pe.Fori(0, B - 1) as b:
                for entry in ATTENTION:
                    step(entry, b, 0, (0, b))
            for entry in LAST_ATTENTION:
                step(entry, LAST, 0, (1, -1))
            for entry in ENTER_SECOND:
                step(entry, -1, 1, (1, -1))
            with pe.Fori(0, B - 1) as b:
                for entry in SECOND:
                    step(entry, b, 1, (1, b))
            for entry in END:
                step(entry, LAST, 1, (1, LAST))


_INS = [
    "L0_attn_x", "L0_attn_Wqkv", "L0_attn_bqkv", "L0_attn_Wo", "L0_attn_bo", "L0_ffn_weight", "L0_ffn_bias",
    "L0_ffn_lora_A", "L0_ffn_lora_B", "L0_ffn_lora_start_indices", "L0_c", "L0_wmod",
]


def kernel(**inputs):
    import concourse.bacc as bacc
    from concourse.bass_utils import run_bass_kernel_spmd

    nc = bacc.Bacc("TRN2", target_bir_lowering=False, num_devices=1)
    arrays, args = {}, []

    def give(name, a):
        arrays[f"in_{name}"] = a
        args.append(nc.dram_tensor(f"in_{name}", a.shape, mybir.dt.from_np(a.dtype), kind="ExternalInput").ap())

    for name in _INS:
        a = np.ascontiguousarray(inputs[name])
        if name == "L0_attn_x":
            a = a.reshape(B * S, H)
        elif name == "L0_ffn_lora_start_indices":
            a = a.reshape(1, B)
        give(name, a)
    for name, a in host_constants().items():
        give(name, a)
    out = nc.dram_tensor("out_y", (B * S, H), F32, kind="ExternalOutput").ap()
    build_block(nc, *args, out)
    r = run_bass_kernel_spmd(nc, [arrays], core_ids=[0])
    return r.results[0]["out_y"].reshape(B, S, H)
```

```python
from contextlib import ExitStack

import numpy as np

import concourse.bass as bass
from concourse import mybir

F32 = mybir.dt.float32
F32R = mybir.dt.float32r
I32 = mybir.dt.int32
ALU = mybir.AluOpType
ACT = mybir.ActivationFunctionType
AX_X = mybir.AxisListType.X

P = 128
B, S, H = 4, 1024, 1024
D = H // 4
CT = H // P
DT = D // P
BANK = 512
CHUNK = 512
QT = S // P
MODS = 6
SA, CA, GA, SB, CB, GB = range(MODS)
NL, RANK = 3, 16
LO_ROW = 64
WM = 7
EPS = 1e-5
SCALE = float(D) ** -0.5
LAST = B - 1


def host_constants():
    sel = np.zeros((P, B), np.float32)
    for q in range(4):
        for b in range(B):
            sel[32 * q + b, b] = 1
    pick = np.zeros((2, P, P), np.float32)
    which = np.full((P, 1), -1, np.float32)
    for part in range(2):
        for n in range(NL):
            for r in range(RANK):
                row = LO_ROW * part + RANK * n + r
                which[row, 0] = n + 2
                for side, order in enumerate([(0, 1, 0), (0, 0, 1)]):
                    for block, want in enumerate(order):
                        if want == part:
                            pick[side, row, 32 * block + r] = 1
    return {"ident": np.eye(P, dtype=np.float32), "sel": sel, "pick": pick, "which": which}


FIRST = [
    ("turn_c", (), "D", None), ("mod", (0, CA, 0), "D", ("turn_c", (), 0)), ("mod", (0, CA, 1), "D", None),
    ("stats", (0, 0)), ("mod", (1, SA, 0), "C", None), ("mod_turn", (0, CA), "D", ("mod", (0, CA), 0)),
    ("mod", (1, SA, 1), "C", None), ("norm", (0, 0)), ("w_hi", (0,)), ("stats", (0, 1)), ("w_hi", (1,)),
    ("mod_turn", (1, SA), "A", None), ("w_lo", (0,)), ("cur", ()), ("norm", (0, 1)), ("w_lo", (1,)),
    ("T", (0, 0, 0), "C", ("mod", (1, SA), 0)), ("stats", (1, 0)), ("w_hi", (2,)),
    ("T", (0, 0, 1), "B", None), ("norm", (1, 0)), ("T", (0, 1, 0), "C", ("T", (0, 0, 0), 0)),
    ("w_lo", (2,)), ("T", (0, 1, 1), "B", ("T", (0, 0, 1), 0)), ("w_lo", (3,)), ("w_hi", (3,)),
    ("T", (1, 0, 0), "D", ("mod_turn", (0, CA), 0)), ("T", (1, 0, 1), "C", ("T", (0, 1, 0), 0)),
    ("mod", (2, GA, 0), "A", ("mod_turn", (1, SA), 0)), ("stats", (1, 1)),
    ("K", (0, 0), "D", ("T", (1, 0, 0), 0)), ("mod", (2, GA, 1), "A", None),
    ("Q", (0, 0), "B", ("T", (0, 1, 1), 0)), ("mod", (3, SB, 0), "C", ("T", (1, 0, 1), 0)),
    ("norm", (1, 1)), ("Q", (0, 1), "B", None), ("T", (1, 1, 0), "A", ("mod", (2, GA), 0)),
    ("mod", (3, SB, 1), "C", None), ("mod_turn", (2, GA), "B", ("Q", (0,), 0)),
    ("T", (1, 1, 1), "A", ("T", (1, 1, 0), 0)), ("K", (0, 1), "D", None),
    ("mod_turn", (3, SB), "A", ("T", (1, 1, 1), 0)), ("mod", (4, CB, 0), "C", ("mod", (3, SB), 0)),
    ("Q", (1, 0), "B", ("mod_turn", (2, GA), 0)), ("mod", (4, CB, 1), "C", None),
    ("K", (1, 0), "A", ("mod_turn", (3, SB), 0)), ("mod", (5, GB, 0), "C", ("mod", (4, CB), 0)),
    ("mod_turn", (4, CB), "D", ("K", (0,), 0)), ("mod", (5, GB, 1), "C", None), ("Q", (1, 1), "B", None),
    ("mod_turn", (5, GB), "C", ("mod", (5, GB), 0)), ("K", (1, 1), "A", None),
    ("turn_wo", (), "D", ("mod_turn", (4, CB), 0)), ("gates", ()),
    ("V", (1, 0), "C", ("mod_turn", (5, GB), 0)), ("gate", (), "D", ("turn_wo", (), 0)),
    ("V", (1, 1), "C", None), ("row", (), "D", ("gate", (), 0)), ("wo_lo", ()),
]

ATTENTION = [
    ("S", (0,), "B", ("Q", (1,), -1)), ("load_x", (0, 0)), ("gates", ()), ("stats", (0, 0)),
    ("V", (0, 0), "D", ("row", (), -1)), ("S", (1,), "A", ("K", (1,), -1)), ("cur", ()), ("norm", (0, 0)),
    ("PT", (0,), "B", ("S", (0,), 0)), ("S", (2,), "C", ("V", (1,), -1)), ("load_x", (0, 1)),
    ("S", (3,), "A", ("S", (1,), 0)), ("PT", (1,), "B", ("PT", (0,), 0)), ("radd", (0,)),
    ("PT", (2,), "C", ("S", (2,), 0)), ("V", (0, 1), "D", None), ("load_r", (2,)),
    ("T", (0, 0, 0), "C", ("PT", (2,), 0)), ("PT", (3,), "B", ("PT", (1,), 0)),
    ("T", (0, 0, 1), "D", ("V", (0,), 0)), ("S", (4,), "A", ("S", (3,), 0)),
    ("S", (5,), "C", ("T", (0, 0, 0), 0)), ("PV", (0, 0), "B", ("PT", (3,), 0)), ("stats", (0, 1)),
    ("load_x", (1, 0)), ("norm", (0, 1)), ("S", (6,), "D", ("T", (0, 0, 1), 0)), ("load_wo", ()),
    ("PT", (4,), "C", ("S", (5,), 0)), ("PV", (0, 1), "B", None), ("load_r", (3,)),
    ("PT", (5,), "A", ("S", (4,), 0)), ("T", (0, 1, 0), "D", ("S", (6,), 0)),
    ("O", (0,), "C", ("PT", (4,), 0)), ("radd", (1,)), ("store", (0,)), ("load_r", (4,)),
    ("PT", (6,), "B", ("PV", (0,), 0)), ("T", (0, 1, 1), "D", ("T", (0, 1, 0), 0)),
    ("S", (7,), "A", ("PT", (5,), 0)), ("O", (1,), "B", ("PT", (6,), 0)), ("store", (1,)),
    ("K", (0, 0), "C", ("O", (0,), 0)), ("radd", (2,)), ("PT", (7,), "D", ("T", (0, 1, 1), 0)),
    ("stats", (1, 0)), ("norm", (1, 0)), ("O", (2,), "A", ("S", (7,), 0)), ("O", (3,), "B", ("O", (1,), 0)),
    ("load_r", (5,)), ("PV", (1, 0), "D", ("PT", (7,), 0)), ("PV", (1, 1), "D", None), ("store", (2,)),
    ("T", (1, 0, 0), "B", ("O", (3,), 0)), ("T", (1, 0, 1), "A", ("O", (2,), 0)), ("K", (0, 1), "C", None),
    ("radd", (3,)), ("store", (3,)), ("stats", (1, 1)), ("radd", (4,)),
    ("O", (4,), "B", ("T", (1, 0, 0), 0)), ("norm", (1, 1)), ("Q", (0, 0), "C", ("K", (0,), 0)),
    ("load_x", (1, 1)), ("store", (4,)), ("Q", (0, 1), "C", None), ("O", (5,), "A", ("T", (1, 0, 1), 0)),
    ("T", (1, 1, 0), "D", ("PV", (1,), 0)), ("radd", (5,)), ("T", (1, 1, 1), "C", ("Q", (0,), 0)),
    ("O", (6,), "A", ("O", (5,), 0)), ("O", (7,), "B", ("O", (4,), 0)), ("load_r", (6,)), ("load_r", (7,)),
    ("gate", (), "D", ("T", (1, 1, 0), 0)), ("store", (5,)), ("load_next", (0,)), ("radd", (6,)),
    ("V", (1, 0), "C", ("T", (1, 1, 1), 0)), ("wo_lo", ()), ("K", (1, 0), "A", ("O", (6,), 0)),
    ("Q", (1, 0), "B", ("O", (7,), 0)), ("load_next", (1,)), ("Q", (1, 1), "B", None),
    ("K", (1, 1), "A", None), ("radd", (7,)), ("V", (1, 1), "C", None), ("store", (6,)),
    ("row", (), "D", ("gate", (), 0)), ("store", (7,)),
]

LAST_ATTENTION = [
    ("S", (0,), "B", ("Q", (1,), -1)), ("stats", (0, 0)), ("S", (1,), "C", ("V", (1,), -1)),
    ("V", (0, 0), "B", ("S", (0,), 0)), ("norm", (0, 0)), ("load_x", (0, 0)), ("load_rows", (0,)),
    ("load_x", (0, 1)), ("load_rows", (1,)), ("PT", (0,), "C", ("S", (1,), 0)), ("cur", ()),
    ("store_w2t", (0,)), ("PT", (1,), "D", ("row", (), -1)), ("load_rows", (2,)), ("V", (0, 1), "B", None),
    ("load_pick", ()), ("T", (0, 0, 0), "D", ("PT", (1,), 0)), ("S", (2,), "C", ("PT", (0,), 0)),
    ("S", (3,), "B", ("V", (0,), 0)), ("radd", (0,)), ("S", (4,), "A", ("K", (1,), -1)),
    ("PT", (2,), "D", ("T", (0, 0, 0), 0)), ("load_rows", (3,)), ("PT", (3,), "B", ("S", (3,), 0)),
    ("radd", (1,)), ("store_w2t", (1,)), ("T", (0, 0, 1), "C", ("S", (2,), 0)),
    ("S", (5,), "A", ("S", (4,), 0)), ("zero_lora", ()), ("PV", (0, 0), "D", ("PT", (2,), 0)),
    ("stats", (0, 1)), ("PV", (0, 1), "D", None), ("turn_w", (0,), "B", ("PT", (3,), 0)),
    ("PT", (4,), "C", ("T", (0, 0, 1), 0)), ("load_lora", ()), ("S", (6,), "D", ("PV", (0,), 0)),
    ("norm", (0, 1)), ("O", (0,), "C", ("PT", (4,), 0)), ("load_r", (2,)),
    ("turn_w", (1,), "B", ("turn_w", (0,), 0)), ("load_x", (1, 0)), ("store", (0,)),
    ("PT", (5,), "A", ("S", (5,), 0)), ("T", (0, 1, 0), "C", ("O", (0,), 0)),
    ("S", (7,), "B", ("turn_w", (1,), 0)), ("O", (1,), "A", ("PT", (5,), 0)), ("store_w2t", (2,)),
    ("load_rows", (4,)), ("load_rows", (5,)), ("store_w2t", (3,)), ("load_r", (3,)), ("store_w2t", (4,)),
    ("T", (0, 1, 1), "D", ("S", (6,), 0)), ("PT", (6,), "B", ("S", (7,), 0)), ("load_r", (4,)),
    ("turn_w", (2,), "D", ("T", (0, 1, 1), 0)), ("store", (1,)), ("load_rows", (6,)), ("radd", (2,)),
    ("load_rows", (7,)), ("PT", (7,), "A", ("O", (1,), 0)), ("store_w2t", (5,)),
    ("turn_w", (3,), "C", ("T", (0, 1, 0), 0)), ("stats", (1, 0)), ("O", (2,), "D", ("turn_w", (2,), 0)),
    ("load_r", (5,)), ("PV", (1, 0), "A", ("PT", (7,), 0)), ("store", (2,)),
    ("turn_w", (4,), "D", ("O", (2,), 0)), ("norm", (1, 0)), ("PV", (1, 1), "A", None), ("radd", (3,)),
    ("store_w2t", (6,)), ("T", (1, 0, 0), "C", ("turn_w", (3,), 0)), ("radd", (4,)),
    ("turn_w", (5,), "B", ("PT", (6,), 0)), ("gates2", ()), ("load_x", (1, 1)),
    ("O", (3,), "A", ("PV", (1,), 0)), ("O", (4,), "D", ("turn_w", (4,), 0)),
    ("turn_lora", (), "B", ("turn_w", (5,), 0)), ("store_w2t", (7,)), ("turn_w", (6,), "D", ("O", (4,), 0)),
    ("T", (1, 0, 1), "A", ("O", (3,), 0)), ("picks", ()), ("store", (3,)),
    ("O", (5,), "C", ("T", (1, 0, 0), 0)), ("load_w2t", (0,)), ("load_r", (6,)), ("store", (4,)),
    ("radd", (5,)), ("turn_w", (7,), "B", ("turn_lora", (), 0)), ("pick_a", (), "B", ("turn_w", (7,), 0)),
    ("stats", (1, 1)), ("load_w2t", (1,)), ("pick_b", (), "C", ("O", (5,), 0)), ("load_w2t", (2,)),
    ("W", (0,), "D", ("turn_w", (6,), 0)), ("norm", (1, 1)), ("W_lo", (0,)),
    ("W", (1,), "C", ("pick_b", (), 0)), ("load_r", (7,)), ("O", (6,), "A", ("T", (1, 0, 1), 0)),
    ("load_w2t", (3,)), ("W", (2,), "D", ("W", (0,), 0)), ("store", (5,)),
    ("gate2", (), "C", ("W", (1,), 0)), ("W_lo", (1,)), ("radd", (6,)), ("W_lo", (2,)),
    ("W", (3,), "A", ("O", (6,), 0)), ("O", (7,), "D", ("W", (2,), 0)), ("store", (6,)), ("load_w2t", (4,)),
    ("W_lo", (3,)), ("T", (1, 1, 0), "B", ("pick_a", (), 0)), ("load_w2t", (5,)), ("radd", (7,)),
    ("T", (1, 1, 1), "C", ("gate2", (), 0)), ("row2", (), "D", ("O", (7,), 0)),
    ("F", (0, 0, 0, 0), "A", ("W", (3,), 0)), ("store", (7,)), ("load_res", (0, 0, 0)),
    ("W", (4,), "B", ("T", (1, 1, 0), 0)), ("radd2", (0, 0, 0)), ("F", (0, 0, 0, 1), "A", None),
    ("load_w2t", (6,)), ("radd2", (0, 0, 1)), ("W_lo", (4,)), ("F", (0, 0, 0, 2), "A", None),
    ("load_res", (0, 0, 1)), ("W", (5,), "B", ("W", (4,), 0)), ("load_res", (0, 1, 0)),
    ("W", (6,), "D", ("row2", (), 0)), ("F", (0, 0, 0, 3), "A", None), ("load_w2t", (7,)), ("W_lo", (5,)),
    ("W", (7,), "D", ("W", (6,), 0)), ("radd2", (0, 1, 0)), ("F", (0, 0, 1, 0), "B", ("W", (5,), 0)),
    ("W_lo", (6,)), ("F", (0, 0, 1, 1), "B", None), ("y_store", (0, 0, 0)), ("W_lo", (7,)),
    ("F", (0, 0, 1, 2), "B", None), ("F", (0, 0, 1, 3), "B", None),
    ("F", (0, 1, 0, 0), "A", ("F", (0, 0, 0), 0)), ("F", (0, 1, 0, 1), "A", None),
    ("F", (0, 1, 0, 2), "A", None), ("y_store", (0, 0, 1)), ("F", (0, 1, 0, 3), "A", None),
    ("F", (0, 1, 1, 0), "B", ("F", (0, 0, 1), 0)), ("F", (0, 1, 1, 1), "B", None), ("radd2", (0, 1, 1)),
    ("F", (0, 1, 1, 2), "B", None), ("y_store", (0, 1, 0)), ("F", (0, 1, 1, 3), "B", None),
    ("y_store", (0, 1, 1)), ("load_res", (0, 1, 1)),
]

SECOND = [
    ("picks", ()), ("load_res", (1, 0, 0)), ("F", (1, 0, 0, 0), "A", ("F", (0, 1, 0), -1)),
    ("F", (1, 0, 0, 1), "A", None), ("load_res", (1, 0, 1)), ("pick_a", (), "C", ("T", (1, 1, 1), -1)),
    ("F", (1, 0, 0, 2), "A", None), ("load_w2t", (0,)), ("load_w2t", (1,)), ("load_x", (0, 0)),
    ("pick_b", (), "C", ("pick_a", (), 0)), ("radd2", (1, 0, 0)), ("stats", (0, 0)), ("cur", ()),
    ("norm", (0, 0)), ("F", (1, 0, 0, 3), "A", None), ("F", (1, 0, 1, 0), "D", ("W", (7,), -1)),
    ("load_res", (1, 1, 0)), ("radd2", (1, 0, 1)), ("T", (0, 0, 0), "C", ("pick_b", (), 0)),
    ("load_x", (0, 1)), ("F", (1, 0, 1, 1), "D", None), ("T", (0, 0, 1), "A", ("F", (1, 0, 0), 0)),
    ("load_res", (1, 1, 1)), ("F", (1, 0, 1, 2), "D", None), ("load_w2t", (2,)),
    ("F", (1, 0, 1, 3), "D", None), ("radd2", (1, 1, 0)), ("W", (0,), "B", ("F", (0, 1, 1), -1)),
    ("F", (1, 1, 0, 0), "A", ("T", (0, 0, 1), 0)), ("load_w2t", (3,)),
    ("W", (1,), "D", ("F", (1, 0, 1), 0)), ("load_w2t", (4,)), ("load_res", (0, 0, 0)),
    ("load_res", (0, 0, 1)), ("F", (1, 1, 0, 1), "A", None), ("stats", (0, 1)), ("y_store", (1, 0, 0)),
    ("radd2", (1, 1, 1)), ("W_lo", (0,)), ("F", (1, 1, 0, 2), "A", None), ("norm", (0, 1)),
    ("W", (2,), "B", ("W", (0,), 0)), ("load_x", (1, 0)), ("W_lo", (1,)), ("F", (1, 1, 0, 3), "A", None),
    ("y_store", (1, 0, 1)), ("W_lo", (2,)), ("W", (3,), "C", ("T", (0, 0, 0), 0)),
    ("F", (1, 1, 1, 0), "D", ("W", (1,), 0)), ("W_lo", (3,)), ("gates2", ()), ("load_w2t", (5,)),
    ("T", (0, 1, 0), "B", ("W", (2,), 0)), ("y_store", (1, 1, 0)), ("F", (1, 1, 1, 1), "D", None),
    ("T", (0, 1, 1), "A", ("F", (1, 1, 0), 0)), ("F", (1, 1, 1, 2), "D", None),
    ("F", (1, 1, 1, 3), "D", None), ("y_store", (1, 1, 1)), ("stats", (1, 0)), ("load_res", (0, 1, 0)),
    ("gate2", (), "B", ("T", (0, 1, 0), 0)), ("F", (0, 0, 0, 0), "C", ("W", (3,), 0)), ("norm", (1, 0)),
    ("F", (0, 0, 0, 1), "C", None), ("load_w2t", (6,)), ("W", (4,), "B", ("gate2", (), 0)),
    ("row2", (), "D", ("F", (1, 1, 1), 0)), ("F", (0, 0, 0, 2), "C", None), ("radd2", (0, 0, 0)),
    ("W", (5,), "A", ("T", (0, 1, 1), 0)), ("radd2", (0, 0, 1)), ("W_lo", (4,)),
    ("F", (0, 0, 0, 3), "C", None), ("W_lo", (5,)), ("load_res", (0, 1, 1)),
    ("W", (6,), "A", ("W", (5,), 0)), ("F", (0, 0, 1, 0), "B", ("W", (4,), 0)), ("W_lo", (6,)),
    ("y_store", (0, 0, 0)), ("load_w2t", (7,)), ("radd2", (0, 1, 0)), ("F", (0, 0, 1, 1), "B", None),
    ("W", (7,), "D", ("row2", (), 0)), ("W_lo", (7,)), ("F", (0, 0, 1, 2), "B", None),
    ("T", (1, 0, 0), "C", ("F", (0, 0, 0), 0)), ("F", (0, 0, 1, 3), "B", None), ("load_x", (1, 1)),
    ("F", (0, 1, 0, 0), "A", ("W", (6,), 0)), ("T", (1, 0, 1), "B", ("F", (0, 0, 1), 0)),
    ("F", (0, 1, 0, 1), "A", None), ("radd2", (0, 1, 1)), ("stats", (1, 1)), ("norm", (1, 1)),
    ("F", (0, 1, 0, 2), "A", None), ("y_store", (0, 0, 1)), ("F", (0, 1, 0, 3), "A", None),
    ("F", (0, 1, 1, 0), "B", ("T", (1, 0, 1), 0)), ("y_store", (0, 1, 0)), ("F", (0, 1, 1, 1), "B", None),
    ("T", (1, 1, 0), "C", ("T", (1, 0, 0), 0)), ("F", (0, 1, 1, 2), "B", None),
    ("T", (1, 1, 1), "C", ("T", (1, 1, 0), 0)), ("F", (0, 1, 1, 3), "B", None), ("y_store", (0, 1, 1)),
]

END = [
    ("load_res", (1, 0, 0)), ("load_res", (1, 0, 1)), ("load_res", (1, 1, 0)), ("load_res", (1, 1, 1)),
    ("radd2", (1, 0, 0)), ("F", (1, 0, 0, 0), "A", ("F", (0, 1, 0), -1)), ("F", (1, 0, 0, 1), "A", None),
    ("F", (1, 0, 0, 2), "A", None), ("F", (1, 0, 0, 3), "A", None), ("y_store", (1, 0, 0)),
    ("radd2", (1, 0, 1)), ("F", (1, 0, 1, 0), "B", ("F", (0, 1, 1), -1)), ("F", (1, 0, 1, 1), "B", None),
    ("F", (1, 0, 1, 2), "B", None), ("F", (1, 0, 1, 3), "B", None), ("y_store", (1, 0, 1)),
    ("radd2", (1, 1, 0)), ("F", (1, 1, 0, 0), "A", ("F", (1, 0, 0), 0)), ("F", (1, 1, 0, 1), "A", None),
    ("F", (1, 1, 0, 2), "A", None), ("F", (1, 1, 0, 3), "A", None), ("y_store", (1, 1, 0)),
    ("radd2", (1, 1, 1)), ("F", (1, 1, 1, 0), "B", ("F", (1, 0, 1), 0)), ("F", (1, 1, 1, 1), "B", None),
    ("F", (1, 1, 1, 2), "B", None), ("F", (1, 1, 1, 3), "B", None), ("y_store", (1, 1, 1)),
]

OF_SECOND = ("picks", "pick_a", "pick_b", "gates2", "gate2", "row2", "turn_w", "W", "W_lo", "F",
             "radd2", "y_store", "zero_lora", "load_lora", "turn_lora", "load_rows", "store_w2t", "load_w2t",
             "load_res", "load_pick")


def build_block(nc, x, wqkv, bqkv, wo, bo, w2, bias, lora_a, lora_b, starts, c, wmod,
                k_ident, k_sel, k_pick, k_which, y):
    with ExitStack() as ctx:
        def sb(name, shape, dt=F32, at=ctx):
            return at.enter_context(nc.sbuf_tensor(name, shape, dt))

        def sem(name):
            return ctx.enter_context(nc.semaphore(name))

        x1_dram = nc.dram_tensor("x1_dram", [B * S, H], F32, kind="Internal").ap()
        w2t_dram = nc.dram_tensor("w2t_dram", [2 * CT // 2, P, 2 * BANK], F32, kind="Internal").ap()

        pair = {n: ctx.enter_context(nc.psum_tensor(f"pair{n}", [P, 2 * BANK], F32)) for n in "ABCD"}

        ident = sb("ident", [P, P])
        modT = sb("modT", [P, MODS, CT, B])
        boT = sb("boT", [P, CT])
        biasT = sb("biasT", [P, CT])
        bqkvT = sb("bqkvT", [P, 3 * DT])
        picked = sb("picked", [P, B])
        cur = sb("cur", [P, 2, CT])
        gate_col = sb("gate_col", [P, CT])
        row_col = sb("row_col", [P, CT])
        bn = sb("bn", [P, 2, 2, 6])
        mv = sb("mv", [P, 2, 2])
        rstd = sb("rstd", [P, 2, 2])
        power = sb("power", [P, 2])
        eps = sb("eps", [P, 2])
        fence = sb("fence", [P, 1])
        neg_max = sb("neg_max", [P, QT])
        total = sb("total", [P, QT])
        r_total = sb("r_total", [P, QT])
        xs = sb("xs", [P, 2, H])
        h_hi, h_lo = [sb("h0_hi", [P, CT, CHUNK], F32R)], [sb("h0_lo", [P, CT, CHUNK], F32R)]
        c_rows = sb("c_rows", [B * CT, P])
        c_exp = sb("c_exp", [B * CT, P])
        start_i = sb("start_i", [P, B], I32)
        start_f = sb("start_f", [P, B])
        which = sb("which", [P, 1])
        le = sb("le", [P, B, B])
        s1 = sb("s1", [P, B])
        s2 = sb("s2", [P, B])
        s3 = sb("s3", [P, B])
        h_hi.append(sb("h1_hi", [P, CT, CHUNK], F32R))
        h_lo.append(sb("h1_lo", [P, CT, CHUNK], F32R))
        pt_hi, pt_lo = h_hi[1], h_lo[1]
        with ExitStack() as first:
            w_hi = sb("w_hi", [P, CT, 3 * D], F32R, at=first)
            w_lo = sb("w_lo", [P, CT, 3 * D], F32R, at=first)
            with ExitStack() as early:
                wm = sb("wm", [P, WM, H], at=early)
                scT = sb("scT", [P, CT, 32], at=early)
                sel = sb("sel", [P, B], at=early)
                sign = sb("sign", [P, CT * B], at=early)
                size = sb("size", [P, CT * B], at=early)
                mod_rows = sb("mod_rows", [P, H], at=early)
                w_raw = sb("w_raw", [P, CT, 3 * D], at=early)
            wo_hi = sb("wo_hi", [P, DT, H], F32R, at=first)
            wo_lo = sb("wo_lo", [P, DT, H], F32R, at=first)
            probs = sb("probs", [P, 2, S], at=first)
            xr = sb("xr", [P, 2, H], at=first)
            row_bc = sb("row_bc", [P, H], at=first)
            q_hi = sb("q_hi", [P, DT, S], F32R, at=first)
            q_lo = sb("q_lo", [P, DT, S], F32R, at=first)
            k_hi = sb("k_hi", [P, DT, S], F32R, at=first)
            k_lo = sb("k_lo", [P, DT, S], F32R, at=first)
            with ExitStack() as early:
                xs_ahead = sb("xs_ahead", [P, 2, 2, H], at=early)
            v_hi = sb("v_hi", [P, QT, D], F32R, at=first)
            v_lo = sb("v_lo", [P, QT, D], F32R, at=first)
        w2t = sb("w2t", [P, 2, 2 * BANK])
        w_sum = sb("w_sum", [P, 2, 2 * BANK])
        w2_rows = w_sum
        a_stack = sb("a_stack", [P, H], F32R)
        b_stack = sb("b_stack", [P, H], F32R)
        a_used = sb("a_used", [P, H], F32R)
        b_used = sb("b_used", [P, H], F32R)
        pick = sb("pick", [P, 2, P])
        pick_b = sb("pick_b", [P, 2, P], F32R)
        with ExitStack() as early:
            a_raw = sb("a_raw", [P, H], at=early)
            b_raw = sb("b_raw", [P, CT, P], at=early)
        gate_bc = sb("gate_bc", [P, H])
        row2_bc = sb("row2_bc", [P, H])
        res = sb("res", [P, 4, 2 * BANK])
        second_half = [sb("w2_hi1", [P, CT, BANK], F32R), sb("w2_lo1", [P, CT, BANK], F32R)]
        gated = sb("gated", [P, 2 * BANK])
        sb("spacer", [P, 6 * 256])
        w2_hi = [sb("w2_hi0", [P, CT, BANK], F32R), second_half[0]]
        w2_lo = [sb("w2_lo0", [P, CT, BANK], F32R), second_half[1]]

        ld_const = sem("ld_const")
        ld_c = sem("ld_c")
        ld_small = sem("ld_small")
        ld_lora = sem("ld_lora")
        ld_wm = [sem(f"ld_wm{i}") for i in range(WM)]
        ld_w = [sem(f"ld_w{i}") for i in range(4)]
        ld_xs = [sem(f"ld_xs{i}") for i in range(2)]
        ld_ahead = [sem(f"ld_ahead{i}") for i in range(2)]
        ld_xr = [sem(f"ld_xr{i}") for i in range(2)]
        ld_wo = sem("ld_wo")
        st_x1 = [sem(f"st_x1_{i}") for i in range(2)]
        ld_pick = sem("ld_pick")
        ld_rows = [sem(f"ld_rows{i}") for i in range(2)]
        st_w2t = [sem(f"st_w2t{i}") for i in range(2)]
        ld_w2t = [sem(f"ld_w2t{i}") for i in range(2)]
        ld_res = [sem(f"ld_res{i}") for i in range(4)]
        st_y = [sem(f"st_y{i}") for i in range(4)]
        v_step = sem("v_step")
        g_step = sem("g_step")
        zeroed = sem("zeroed")
        c_expd = sem("c_expd")
        c_silu = sem("c_silu")
        c_turned = sem("c_turned")
        c_ready = sem("c_ready")
        lora_turned = sem("lora_turned")
        lora_hi = sem("lora_hi")
        lora_lo = sem("lora_lo")
        mod_used = sem("mod_used")
        mod_copied = sem("mod_copied")
        mod_turned = sem("mod_turned")
        mod_made = sem("mod_made")
        w_hi_made = sem("w_hi_made")
        w_lo_made = sem("w_lo_made")
        wo_turned = sem("wo_turned")
        wo_row_made = sem("wo_row_made")
        bn_made = sem("bn_made")
        mv_made = sem("mv_made")
        var_eps = sem("var_eps")
        rstd_made = sem("rstd_made")
        x_normed = sem("x_normed")
        cur_made = sem("cur_made")
        h_turned = sem("h_turned")
        h_affine = sem("h_affine")
        h_hi_made = sem("h_hi_made")
        h_lo_made = sem("h_lo_made")
        q_done, k_done, v_done = sem("q_done"), sem("k_done"), sem("v_done")
        q_hi_made, k_hi_made, v_hi_made = sem("q_hi_made"), sem("k_hi_made"), sem("v_hi_made")
        q_lo_made, k_lo_made, v_lo_made = sem("q_lo_made"), sem("k_lo_made"), sem("v_lo_made")
        gates_made = sem("gates_made")
        gate_done = sem("gate_done")
        wo_gated = sem("wo_gated")
        wo_hi_made = sem("wo_hi_made")
        wo_lo_made = sem("wo_lo_made")
        row_done = sem("row_done")
        row_made = sem("row_made")
        s_done = sem("s_done")
        max_made = sem("max_made")
        exp_made = sem("exp_made")
        r_total_made = sem("r_total_made")
        pt_done = sem("pt_done")
        pt_hi_made = sem("pt_hi_made")
        pt_lo_made = sem("pt_lo_made")
        pv_done = sem("pv_done")
        o_hi_made = sem("o_hi_made")
        o_lo_made = sem("o_lo_made")
        o_done = sem("o_done")
        residual_made = sem("residual_made")
        x1_made = sem("x1_made")
        picks_made = sem("picks_made")
        pick_done = sem("pick_done")
        picked_made = sem("picked_made")
        gates2_made = sem("gates2_made")
        gate2_done = sem("gate2_done")
        gate2_made = sem("gate2_made")
        row2_done = sem("row2_done")
        row2_made = sem("row2_made")
        w2_turned = sem("w2_turned")
        w2t_made = sem("w2t_made")
        lora_done = sem("lora_done")
        w_sum_made = sem("w_sum_made")
        w2_hi_made = sem("w2_hi_made")
        w2_lo_made = sem("w2_lo_made")
        f_done = sem("f_done")
        residual2_made = sem("residual2_made")
        y_gated = sem("y_gated")
        y_made = sem("y_made")

        def round_no(stage, b, j, r):
            return 4 * (b + 1) + 2 * j + r + stage * 2 * 2 * B

        def turn_no(stage, b, j, r, half):
            return 2 * round_no(stage, b, j, r) + half

        def f_no(b, j, h, p):
            return QT * (b if j else b + 1) + 4 * j + 2 * h + p

        def v_no(b, j, p):
            return 4 * (b + 1) + p if j else 4 * b + 2 + p

        def wait(eng, s, value):
            if not isinstance(value, int) or value > 0:
                eng.wait_ge(s, value)

        def wait_emptied(eng, before, b, prep):
            if before is None:
                return
            what, i, turn = before
            stage, b = prep[0], (prep[1] if what in OF_SECOND or what == "T" else b) + turn
            s, value = {
                "turn_c": lambda: (c_ready, 1),
                "turn_lora": lambda: (lora_lo, 2),
                "mod": lambda: (mod_copied, i[0] + 1),
                "mod_turn": lambda: (mod_made, i[0] + 1),
                "turn_wo": lambda: (wo_row_made, 1),
                "T": lambda: (h_affine, 4 * turn_no(stage, b, *i) + 4),
                "Q": lambda: (q_lo_made, 2 * (2 * (b + 1) + i[0]) + 2),
                "K": lambda: (k_lo_made, 2 * (2 * (b + 1) + i[0]) + 2),
                "V": lambda: (v_lo_made, v_no(b, i[0], 1) + 1),
                "gate": lambda: (wo_gated, DT * (b + 1) + DT),
                "row": lambda: (row_made, b + 2),
                "S": lambda: (exp_made, QT * b + i[0] + 1),
                "PT": lambda: (pt_lo_made, QT * b + i[0] + 1),
                "PV": lambda: (o_lo_made, 4 * b + 2 * i[0] + 2),
                "O": lambda: (x1_made, QT * b + i[0] + 1),
                "pick_a": lambda: (picked_made, 2 * (b + 1) + 1),
                "pick_b": lambda: (picked_made, 2 * (b + 1) + 2),
                "gate2": lambda: (gate2_made, b + 2),
                "row2": lambda: (row2_made, b + 2),
                "turn_w": lambda: (w2t_made, i[0] + 1),
                "W": lambda: (w_sum_made, 8 * (b + 1) + i[0] + 1),
                "F": lambda: (y_gated, f_no(b, *i) + 1),
            }[what]()
            wait(eng, s, value)

        def ahead(prep, j, r):
            return j if isinstance(prep[1], int) and prep == (0, -1) and j != r else None

        def rows_of(prep, j, r):
            a = ahead(prep, j, r)
            return xs if a is None else xs_ahead[:, a]

        def h_parts(prep, j, r, ct):
            where = (slice(None), slice(ct, ct + 2), slice(2 * r * P, 2 * (r + 1) * P))
            return (rows_of(prep, j, r)[:, :, ct * P:(ct + 2) * P].rearrange("p k (c n) -> p c k n", c=2),
                    h_hi[j][where].rearrange("p c (k n) -> p c k n", k=2),
                    h_lo[j][where].rearrange("p c (k n) -> p c k n", k=2))

        block = ctx.enter_context(nc.Block())

        @block.sync
        def _(sp):
            def load_xs(stage, b, j, r):
                if stage == 0 and isinstance(b, int) and b < 0:
                    sp.wait_ge(h_lo_made, 4)
                else:
                    wait(sp, h_lo_made, 2 * turn_no(stage, b, j, r, 0))
                src = x if stage == 0 else x1_dram
                if stage == 1:
                    for i in range(2):
                        wait(sp, st_x1[i], 16 * QT // 2 * (b + 2))
                for i in range(2):
                    row = (b + 1) * S + j * CHUNK + (2 * r + i) * P
                    sp.dma_start(xs[:, i, :], src[bass.ds(row, P), :]).then_inc(ld_xs[i], 16)

            def load_first(j, r):
                for i in range(2):
                    row = j * CHUNK + (2 * r + i) * P
                    a = ahead((0, -1), j, r)
                    sp.dma_start(rows_of((0, -1), j, r)[:, i, :], x[row:row + P, :]).then_inc(
                        ld_xs[i] if a is None else ld_ahead[a], 16)

            def load_wm(n, q):
                slot, k = n % WM, n % CT
                wait(sp, mod_used, n - WM + 1)
                sp.dma_start(wm[:, slot, :], wmod[k * P:(k + 1) * P, q * H:(q + 1) * H]).then_inc(ld_wm[slot], 16)

            def load_residual(b, t):
                wait(sp, st_x1[t % 2], 16 * (QT // 2 * b + t // 2))
                sp.dma_start(xr[:, t % 2, :], x[bass.ds(b * S + t * P, P), :]).then_inc(ld_xr[t % 2], 16)

            def load_wo(b):
                wait(sp, pt_done, QT * (b + 1))
                sp.dma_start(probs[:, :, :], wo.rearrange("(d p) n -> p d n", p=P)).then_inc(ld_wo, 16)

            def load_rows(n):
                h, cp = n // 4, n % 4
                if n < 2:
                    sp.wait_ge(v_done, 4 * B)
                wait(sp, w2_turned, n - 1)
                src = w2[h * BANK:(h + 1) * BANK, cp * 2 * P:(cp + 1) * 2 * P]
                sp.dma_start(w2_rows[:, n % 2, :].rearrange("p (o c) -> p o c", o=4),
                             src.rearrange("(o p) c -> p o c", p=P)).then_inc(ld_rows[n % 2], 16)

            def store_w2t(n):
                sp.wait_ge(w2t_made, n + 1)
                sp.dma_start(w2t_dram[n], w2t[:, n % 2, :]).then_inc(st_w2t[n % 2], 16)

            def load_pick():
                sp.wait_ge(v_done, 4 * B)
                sp.dma_start(pick[:, :, :], k_pick.rearrange("s p n -> p s n")).then_inc(ld_pick, 16)

            def load_w2t(b, n):
                wait(sp, w_sum_made, 8 * (b + 1) + n - 1)
                sp.wait_ge(st_w2t[n % 2], 16 * 4)
                sp.dma_start(w2t[:, n % 2, :], w2t_dram[n]).then_inc(ld_w2t[n % 2], 16)

            def load_res(b, j, h, p):
                slot = 2 * h + p
                batch = b if j else b + 1
                if j == 0 and isinstance(b, int) and b < 0:
                    sp.wait_ge(o_done, QT * B)
                    for i in range(2):
                        sp.wait_ge(st_x1[i], 16 * QT // 2 * B)
                else:
                    sp.wait_ge(st_y[slot], 16 * (2 * batch + j))
                row = batch * S + j * CHUNK + p * 2 * P
                src = x1_dram[bass.ds(row, 2 * P), h * BANK:(h + 1) * BANK].rearrange("(t p) n -> p t n", p=P)
                sp.dma_start(res[:, slot, :].rearrange("p (t n) -> p t n", t=2), src).then_inc(ld_res[slot], 16)

            def step(entry, b, prep):
                what, i = entry[0], entry[1]
                if what in OF_SECOND:
                    b = prep[1]
                if what == "load_x":
                    load_xs(*prep, *i)
                elif what == "load_r":
                    load_residual(b, *i)
                elif what == "load_next":
                    load_residual(b + 1, *i)
                elif what == "load_wo":
                    load_wo(b)
                elif what == "load_rows":
                    load_rows(*i)
                elif what == "store_w2t":
                    store_w2t(*i)
                elif what == "load_pick":
                    load_pick()
                elif what == "load_w2t":
                    load_w2t(b, *i)
                elif what == "load_res":
                    load_res(b, *i)

            sp.dma_start(c_rows[:, :], c.rearrange("b (k n) -> (b k) n", n=P)).then_inc(ld_c, 16)
            sp.dma_start(ident[:, :], k_ident).then_inc(ld_const, 16)
            sp.dma_start(sel[:, :], k_sel).then_inc(ld_const, 16)
            for k in range(CT):
                if k == WM:
                    load_first(0, 0)
                load_wm(k, CA)
            for k in range(CT):
                load_wm(CT + k, SA)
            load_first(0, 1)
            for n in range(4):
                sp.dma_start(w_raw[:, 2 * n:2 * n + 2, :], wqkv[2 * n * P:(2 * n + 2) * P, :].rearrange(
                    "(c p) n -> p c n", p=P)).then_inc(ld_w[n], 16)
                if n == 2:
                    load_first(1, 0)
            for s, q in ((2, GA), (3, SB), (4, CB), (5, GB)):
                for k in range(CT):
                    if s == 2 and k == WM:
                        load_xs(0, -1, 1, 1)
                    load_wm(s * CT + k, q)
            sp.wait_ge(mod_used, MODS * CT)
            load_wo(-1)
            sp.wait_ge(mod_made, MODS)
            load_residual(0, 0)
            load_residual(0, 1)
            with sp.Fori(0, B - 1) as b:
                for entry in ATTENTION:
                    step(entry, b, (0, b))
            for entry in LAST_ATTENTION:
                step(entry, LAST, (1, -1))
            with sp.Fori(0, B - 1) as b:
                for entry in SECOND:
                    step(entry, b, (1, b))
            for entry in END:
                step(entry, LAST, (1, LAST))

        @block.gpsimd
        def _(pool):
            nc.gpsimd.memset(power[:, :], -0.5).then_inc(g_step, 1)
            nc.gpsimd.memset(eps[:, :], EPS).then_inc(g_step, 1)
            pool.dma_start(start_i[:, :], starts.partition_broadcast(P)).then_inc(ld_small, 16)
            pool.dma_start(which[:, :], k_which).then_inc(ld_small, 16)
            pool.dma_start(bqkvT[:, :], bqkv.rearrange("(f p) -> p f", p=P),
                               allow_slow_non_contiguous=True).then_inc(ld_small, 16)
            pool.dma_start(boT[:, :], bo.rearrange("(f p) -> p f", p=P),
                               allow_slow_non_contiguous=True).then_inc(ld_small, 16)
            pool.dma_start(biasT[:, :], bias.rearrange("(f p) -> p f", p=P),
                               allow_slow_non_contiguous=True).then_inc(ld_small, 16)

            def step(entry, b, stage, prep):
                what, i = entry[0], entry[1]
                if what in OF_SECOND:
                    b = prep[1]
                if what == "load_lora":
                    pool.wait_ge(zeroed, 3)
                    for at in (0, LO_ROW):
                        pool.dma_start(a_raw[at:at + NL * RANK, :], lora_a.rearrange("n r d -> (n r) d")).then_inc(ld_lora, 16)
                        for n in range(NL):
                            pool.dma_start(b_raw[:, :, at + n * RANK:at + (n + 1) * RANK],
                                           lora_b[n].rearrange("(t p) r -> p t r", p=P)).then_inc(ld_lora, 16)
                elif what == "stats":
                    n = round_no(*prep, *i)
                    pool.wait_ge(mv_made, 2 * n + 2)
                    nc.gpsimd.tensor_tensor(rstd[:, 0, :], mv[:, :, 1], eps[:, :], ALU.add).then_inc(var_eps, 1)
                    pool.wait_ge(var_eps, n + 1)
                    nc.gpsimd.tensor_tensor(rstd[:, 1, :], rstd[:, 0, :], power[:, :], ALU.pow).then_inc(rstd_made, 1)
                elif what == "radd":
                    t = i[0]
                    pool.wait_ge(ld_xr[t % 2], 16 * (QT // 2 * b + t // 2 + 1))
                    pool.wait_ge(row_made, b + 1)
                    xt = xr[:, t % 2, :]
                    nc.gpsimd.tensor_tensor(xt, xt, row_bc[:, :], ALU.add).then_inc(residual_made, 1)
                elif what == "store":
                    t = i[0]
                    pool.wait_ge(x1_made, QT * b + t + 1)
                    pool.dma_start(x1_dram[bass.ds(b * S + t * P, P), :], xr[:, t % 2, :]).then_inc(st_x1[t % 2], 16)
                elif what == "radd2":
                    j, h, p = i
                    n = f_no(b, j, h, p)
                    slot, batch = 2 * h + p, (b if j else b + 1)
                    pool.wait_ge(ld_res[slot], 16 * (2 * batch + j + 1))
                    pool.wait_ge(row2_made, batch + 1)
                    rt = res[:, slot, :].rearrange("p (t n) -> p t n", t=2)
                    row = row2_bc[:, h * BANK:(h + 1) * BANK].unsqueeze(1).to_broadcast([P, 2, BANK])
                    nc.gpsimd.tensor_tensor(rt, rt, row, ALU.add).then_inc(residual2_made, 1)
                elif what == "y_store":
                    j, h, p = i
                    n = f_no(b, j, h, p)
                    slot, batch = 2 * h + p, (b if j else b + 1)
                    pool.wait_ge(y_made, n + 1)
                    dst = y[bass.ds(batch * S + j * CHUNK + p * 2 * P, 2 * P), h * BANK:(h + 1) * BANK]
                    pool.dma_start(dst.rearrange("(t p) n -> p t n", p=P),
                                   res[:, slot, :].rearrange("p (t n) -> p t n", t=2)).then_inc(st_y[slot], 16)

            pool.wait_ge(g_step, 2)
            for entry in FIRST:
                step(entry, -1, 0, (0, -1))
            with pool.Fori(0, B - 1) as b:
                for entry in ATTENTION:
                    step(entry, b, 0, (0, b))
            for entry in LAST_ATTENTION:
                step(entry, LAST, 0, (1, -1))
            with pool.Fori(0, B - 1) as b:
                for entry in SECOND:
                    step(entry, b, 1, (1, b))
            for entry in END:
                step(entry, LAST, 1, (1, LAST))
            for slot in range(4):
                pool.wait_ge(st_y[slot], 16 * 2 * B)

        @block.scalar
        def _(act):
            def emptied_copy(dst, src, made):
                nc.scalar.activation(dst, src, ACT.Copy).then_inc(made, 1)

            def step(entry, b, stage, prep):
                what, i = entry[0], entry[1]
                if what in OF_SECOND:
                    b = prep[1]
                ps = pair[entry[2]] if len(entry) > 2 else None
                if what == "turn_lora":
                    act.wait_ge(ld_lora, 16 * 2 * (1 + NL))
                    nc.scalar.activation(a_stack[:, :], a_raw[:, :], ACT.Copy).then_inc(lora_hi, 1)
                    act.wait_ge(lora_turned, 1)
                    nc.scalar.activation(b_stack[:, :], ps[:, :], ACT.Copy).then_inc(lora_hi, 1)
                elif what == "mod":
                    if i[2] == 0:
                        return
                    act.wait_ge(mod_used, CT * (i[0] + 1))
                    wait(act, mod_turned, i[0])
                    emptied_copy(mod_rows[:, :], ps[:, :], mod_copied)
                elif what == "w_hi":
                    n = i[0]
                    act.wait_ge(ld_w[n], 16)
                    c2 = slice(2 * n, 2 * n + 2)
                    nc.scalar.activation(w_hi[:, c2, 0:D], w_raw[:, c2, 0:D], ACT.Copy, scale=SCALE).then_inc(w_hi_made, 1)
                    nc.scalar.activation(w_hi[:, c2, D:], w_raw[:, c2, D:], ACT.Copy).then_inc(w_hi_made, 1)
                elif what == "T":
                    j, r, half = i
                    n = turn_no(*prep, *i)
                    act.wait_ge(h_turned, n + 1)
                    if stage == 0 and i == (1, 0, 0) and not (isinstance(b, int) and b < 0):
                        act.wait_ge(pv_done, 4 * (b + 1))
                    if i == (0, 0, 0):
                        act.wait_ge(cur_made, 2 * (prep[0] * B + prep[1] + 2))
                    for sub in range(2):
                        for cc in range(2):
                            ct = 4 * half + 2 * sub + cc
                            nc.scalar.activation(rows_of(prep, j, r)[:, :, ct * P:(ct + 1) * P],
                                                 ps[:, (2 * sub + cc) * 2 * P:(2 * sub + cc + 1) * 2 * P].rearrange(
                                                     "p (k n) -> p k n", k=2),
                                                 ACT.Identity, bias=cur[:, 1, ct:ct + 1],
                                                 scale=cur[:, 0, ct:ct + 1]).then_inc(h_affine, 1)
                    for sub in range(2):
                        act.wait_ge(h_affine, 4 * n + 2 * sub + 2)
                        h, hi, _ = h_parts(prep, j, r, 4 * half + 2 * sub)
                        nc.scalar.activation(hi, h, ACT.Copy).then_inc(h_hi_made, 1)
                elif what in ("Q", "K"):
                    n = 2 * (b + 1) + i[0]
                    done, made, dst, col = ((q_done, q_hi_made, q_hi, 0) if what == "Q"
                                            else (k_done, k_hi_made, k_hi, DT))
                    m = i[1]
                    act.wait_ge(done, 2 * n + m + 1)
                    nc.scalar.activation(dst[:, m, i[0] * CHUNK:(i[0] + 1) * CHUNK], ps[:, m * BANK:(m + 1) * BANK],
                                         ACT.Identity, bias=bqkvT[:, col + m:col + m + 1]).then_inc(made, 1)
                elif what == "V":
                    p = i[1]
                    act.wait_ge(v_done, v_no(b, i[0], p) + 1)
                    emptied_copy(v_hi[:, 4 * i[0] + 2 * p:4 * i[0] + 2 * p + 2, :],
                                 ps[:, p * BANK:(p + 1) * BANK].rearrange("p (t n) -> p t n", t=2), v_hi_made)
                elif what == "gate":
                    for d in range(DT):
                        act.wait_ge(wo_gated, DT * (b + 1) + d + 1)
                        nc.scalar.activation(wo_hi[:, d, :], probs[:, d, :], ACT.Copy).then_inc(wo_hi_made, 1)
                elif what == "row":
                    act.wait_ge(row_done, b + 2)
                    wait(act, residual_made, QT * (b + 1))
                    emptied_copy(row_bc[:, :], ps[:, :], row_made)
                elif what == "S":
                    t = i[0]
                    act.wait_ge(max_made, QT * b + t + 1)
                    if t >= 2:
                        act.wait_ge(pt_done, QT * b + t - 1)
                    else:
                        act.wait_ge(wo_lo_made, DT * (b + 1))
                    nc.scalar.activation(probs[:, t % 2, :], ps[:, :], ACT.Exp, bias=neg_max[:, t:t + 1],
                                         accum_out=total[:, t:t + 1]).then_inc(exp_made, 1)
                elif what == "PT":
                    t = i[0]
                    act.wait_ge(pt_done, QT * b + t + 1)
                    if t == 4:
                        act.wait_ge(pv_done, 4 * b + 2)
                    nc.scalar.activation(pt_hi[:, :, (t % 4) * P:(t % 4 + 1) * P],
                                         ps[:, :].rearrange("p (k q) -> p k q", q=P), ACT.Copy).then_inc(pt_hi_made, 1)
                elif what == "PV":
                    m = i[1]
                    act.wait_ge(pv_done, 4 * b + 2 * i[0] + m + 1)
                    nc.scalar.activation(q_hi[:, m, i[0] * CHUNK:(i[0] + 1) * CHUNK], ps[:, m * BANK:(m + 1) * BANK],
                                         ACT.Copy).then_inc(o_hi_made, 1)
                elif what in ("pick_a", "pick_b"):
                    side = 0 if what == "pick_a" else 1
                    act.wait_ge(pick_done, 2 * (b + 1) + side + 1)
                    emptied_copy((a_used, b_used)[side][:, :], ps[:, :], picked_made)
                elif what == "gate2":
                    act.wait_ge(gate2_done, b + 2)
                    wait(act, y_gated, QT * (b + 1))
                    emptied_copy(gate_bc[:, :], ps[:, :], gate2_made)
                elif what == "row2":
                    act.wait_ge(row2_done, b + 2)
                    wait(act, residual2_made, QT * (b + 1))
                    emptied_copy(row2_bc[:, :], ps[:, :], row2_made)
                elif what == "turn_w":
                    n = i[0]
                    act.wait_ge(w2_turned, n + 1)
                    if n >= 2:
                        act.wait_ge(st_w2t[n % 2], 16 * (n // 2))
                    emptied_copy(w2t[:, n % 2, :], ps[:, :], w2t_made)
                elif what == "W":
                    n = 8 * (b + 1) + i[0]
                    h, cp = i[0] // 4, i[0] % 4
                    act.wait_ge(w_sum_made, n + 1)
                    if h == 1 and isinstance(b, int) and b < 0:
                        for k in range(2):
                            act.wait_ge(st_x1[k], 16 * QT // 2 * B)
                    nc.scalar.activation(w2_hi[h][:, 2 * cp:2 * cp + 2, :],
                                         w_sum[:, i[0] % 2, :].rearrange("p (c n) -> p c n", c=2),
                                         ACT.Copy).then_inc(w2_hi_made, 1)
                elif what == "turn_c":
                    act.wait_ge(ld_c, 16)
                    nc.scalar.activation(c_exp[:, :], c_rows[:, :], ACT.Exp, scale=-1.0).then_inc(c_expd, 1)

            for entry in FIRST:
                step(entry, -1, 0, (0, -1))
            with act.Fori(0, B - 1) as b:
                for entry in ATTENTION:
                    step(entry, b, 0, (0, b))
            for entry in LAST_ATTENTION:
                step(entry, LAST, 0, (1, -1))
            with act.Fori(0, B - 1) as b:
                for entry in SECOND:
                    step(entry, b, 1, (1, b))

        @block.vector
        def _(dve):
            chain = [0]

            def link(ins):
                chain[0] += 1
                ins.then_inc(v_step, 1)
                dve.wait_ge(v_step, chain[0])

            def step(entry, b, stage, prep):
                what, i = entry[0], entry[1]
                if what in OF_SECOND:
                    b = prep[1]
                ps = pair[entry[2]] if len(entry) > 2 else None
                if what == "turn_c":
                    dve.wait_ge(c_expd, 1)
                    link(nc.vector.tensor_scalar(c_exp[:, :], c_exp[:, :], 1.0, None, ALU.add))
                    link(nc.vector.reciprocal(c_exp[:, :], c_exp[:, :]))
                    nc.vector.tensor_tensor(c_rows[:, :], c_rows[:, :], c_exp[:, :], ALU.mult).then_inc(c_silu, 1)
                    dve.wait_ge(c_turned, 1)
                    dve.wait_ge(zeroed, 1)
                    nc.vector.tensor_copy(scT[:, :, 0:B], ps[:, 0:B * CT].rearrange("p (b k) -> p k b", b=B)).then_inc(c_ready, 1)
                elif what == "zero_lora":
                    dve.wait_ge(v_done, 4 * B)
                    nc.vector.memset(a_raw[:, :], 0.0).then_inc(zeroed, 1)
                    nc.vector.memset(b_raw[:, :, :], 0.0).then_inc(zeroed, 1)
                elif what == "turn_lora":
                    link(nc.vector.tensor_copy(start_f[:, :], start_i[:, :]))
                    for b0 in range(B):
                        ins = nc.vector.tensor_scalar(le[:, :, b0], start_f[:, :], float(b0), None, ALU.is_le)
                    link(ins)
                    link(nc.vector.tensor_tensor(s1[:, :], le[:, 0, :], le[:, 1, :], ALU.mult))
                    link(nc.vector.tensor_tensor(s1[:, :], le[:, 0, :], s1[:, :], ALU.subtract))
                    link(nc.vector.scalar_tensor_tensor(s1[:, :], le[:, 1, :], 2.0, s1[:, :], ALU.mult, ALU.add))
                    link(nc.vector.scalar_tensor_tensor(s2[:, :], le[:, 3, :], 3.0, s1[:, :], ALU.add, ALU.subtract))
                    link(nc.vector.tensor_tensor(s3[:, :], le[:, 2, :], s2[:, :], ALU.mult))
                    link(nc.vector.tensor_tensor(s3[:, :], s3[:, :], s1[:, :], ALU.add))
                    link(nc.vector.tensor_scalar(picked[:, :], s3[:, :], which[:, 0:1], None, ALU.is_equal))
                    dve.wait_ge(lora_hi, 1)
                    nc.vector.tensor_tensor(a_stack[LO_ROW:, :], a_raw[LO_ROW:, :], a_stack[LO_ROW:, :].bitcast(F32),
                                            ALU.subtract).then_inc(lora_lo, 1)
                    dve.wait_ge(lora_hi, 2)
                    nc.vector.tensor_tensor(b_stack[LO_ROW:, :], ps[LO_ROW:, :], b_stack[LO_ROW:, :].bitcast(F32),
                                            ALU.subtract).then_inc(lora_lo, 1)
                elif what == "mod_turn":
                    s, q = i
                    dve.wait_ge(mod_turned, s + 1)
                    src, dst = ps[:, 0:CT * B], modT[:, q, :, :].rearrange("p c b -> p (c b)")
                    if q in (CA, CB):
                        nc.vector.tensor_scalar(dst, src, 1.0, None, ALU.add).then_inc(mod_made, 1)
                    elif q in (SA, SB):
                        nc.vector.tensor_copy(dst, src).then_inc(mod_made, 1)
                    else:
                        link(nc.vector.tensor_copy(dst, src))
                        link(nc.vector.tensor_scalar(sign[:, :], dst, 0.0, 2.0, ALU.is_ge, ALU.mult))
                        link(nc.vector.scalar_tensor_tensor(size[:, :], dst, -1.0, dst, ALU.mult, ALU.max))
                        link(nc.vector.tensor_scalar(size[:, :], size[:, :], 0.25, None, ALU.max))
                        nc.vector.scalar_tensor_tensor(dst, sign[:, :], -1.0, size[:, :], ALU.add,
                                                       ALU.mult).then_inc(mod_made, 1)
                elif what == "w_lo":
                    n = i[0]
                    if n == 0:
                        dve.wait_ge(ld_small, 16 * 5)
                        link(nc.vector.tensor_scalar(bqkvT[:, 0:DT], bqkvT[:, 0:DT], SCALE, None, ALU.mult))
                    c2 = slice(2 * n, 2 * n + 2)
                    dve.wait_ge(w_hi_made, 2 * n + 2)
                    nc.vector.scalar_tensor_tensor(w_lo[:, c2, 0:D], w_raw[:, c2, 0:D], SCALE,
                                                   w_hi[:, c2, 0:D].bitcast(F32), ALU.mult, ALU.subtract).then_inc(w_lo_made, 1)
                    nc.vector.tensor_tensor(w_lo[:, c2, D:], w_raw[:, c2, D:], w_hi[:, c2, D:].bitcast(F32),
                                            ALU.subtract).then_inc(w_lo_made, 1)
                elif what == "turn_wo":
                    dve.wait_ge(wo_turned, 1)
                    nc.vector.tensor_tensor(boT[:, :], boT[:, :], ps[:, 0:CT], ALU.add).then_inc(wo_row_made, 1)
                elif what == "stats":
                    n = round_no(*prep, *i)
                    a, rows = ahead(prep, *i), rows_of(prep, *i)
                    for k in range(2):
                        if a is not None:
                            dve.wait_ge(ld_ahead[a], 32)
                        else:
                            dve.wait_ge(ld_xs[k], 16 if isinstance(n, int) and n == 0 else 16 * (n - 1))
                        for half in range(2):
                            nc.vector.bn_stats(bn[:, k, half, :], rows[:, k, half * BANK:(half + 1) * BANK]).then_inc(bn_made, 1)
                    dve.wait_ge(bn_made, 4 * n + 4)
                    nc.vector.memset(fence[:, :], 0.0)
                    for k in range(2):
                        nc.vector.bn_aggr(mv[:, k, :], bn[:, k, :, :].rearrange("p h n -> p (h n)")).then_inc(mv_made, 1)
                elif what == "cur":
                    pst, pb = prep
                    wait(dve, h_affine, 4 * turn_no(pst, pb, 0, 0, 0))
                    if stage == 0 and isinstance(b, int) and b < 0:
                        dve.wait_ge(mod_made, 2)
                    for k, q in enumerate((CA, SA) if pst == 0 else (CB, SB)):
                        src = modT[:, q, :, bass.ds(pb + 1, 1)].rearrange("p c b -> p (c b)")
                        nc.vector.tensor_copy(cur[:, k, :], src).then_inc(cur_made, 1)
                elif what == "norm":
                    n = round_no(*prep, *i)
                    dve.wait_ge(rstd_made, n + 1)
                    rows = rows_of(prep, *i)
                    for k in range(2):
                        nc.vector.tensor_scalar(rows[:, k, :], rows[:, k, :], mv[:, k, 0:1], rstd[:, 1, k:k + 1],
                                                ALU.subtract, ALU.mult).then_inc(x_normed, 1)
                elif what == "T":
                    j, r, half = i
                    n = turn_no(*prep, *i)
                    for sub in range(2):
                        h, hi, lo = h_parts(prep, j, r, 4 * half + 2 * sub)
                        dve.wait_ge(h_hi_made, 2 * n + sub + 1)
                        nc.vector.tensor_tensor(lo, h, hi.bitcast(F32), ALU.subtract).then_inc(h_lo_made, 1)
                elif what in ("Q", "K"):
                    n = 2 * (b + 1) + i[0]
                    hi_made, made, hi, lo, col = ((q_hi_made, q_lo_made, q_hi, q_lo, 0) if what == "Q"
                                                  else (k_hi_made, k_lo_made, k_hi, k_lo, DT))
                    m = i[1]
                    where = (slice(None), m, slice(i[0] * CHUNK, (i[0] + 1) * CHUNK))
                    dve.wait_ge(hi_made, 2 * n + m + 1)
                    nc.vector.scalar_tensor_tensor(lo[where], ps[:, m * BANK:(m + 1) * BANK],
                                                   bqkvT[:, col + m:col + m + 1], hi[where].bitcast(F32),
                                                   ALU.add, ALU.subtract).then_inc(made, 1)
                elif what == "V":
                    p = i[1]
                    dve.wait_ge(v_hi_made, v_no(b, i[0], p) + 1)
                    where = (slice(None), slice(4 * i[0] + 2 * p, 4 * i[0] + 2 * p + 2), slice(None))
                    nc.vector.tensor_tensor(v_lo[where], ps[:, p * BANK:(p + 1) * BANK].rearrange("p (t n) -> p t n", t=2),
                                            v_hi[where].bitcast(F32), ALU.subtract).then_inc(v_lo_made, 1)
                elif what == "gates":
                    wait(dve, row_done, b + 1)
                    src = modT[:, GA, :, bass.ds(b + 1, 1)].rearrange("p c b -> p (c b)")
                    nc.vector.tensor_copy(gate_col[:, :], src).then_inc(gates_made, 1)
                    dve.wait_ge(wo_row_made, 1)
                    nc.vector.tensor_tensor(row_col[:, :], src, boT[:, :], ALU.mult).then_inc(gates_made, 1)
                elif what == "gate":
                    dve.wait_ge(gate_done, b + 2)
                    dve.wait_ge(ld_wo, 16 * (b + 2))
                    for d in range(DT):
                        nc.vector.tensor_tensor(probs[:, d, :], probs[:, d, :], ps[:, :], ALU.mult).then_inc(wo_gated, 1)
                elif what == "wo_lo":
                    for d in range(DT):
                        dve.wait_ge(wo_hi_made, DT * (b + 1) + d + 1)
                        nc.vector.tensor_tensor(wo_lo[:, d, :], probs[:, d, :], wo_hi[:, d, :].bitcast(F32),
                                                ALU.subtract).then_inc(wo_lo_made, 1)
                elif what == "S":
                    t = i[0]
                    dve.wait_ge(s_done, QT * b + t + 1)
                    nc.vector.tensor_reduce(neg_max[:, t:t + 1], ps[:, :], AX_X, ALU.max, negate=True).then_inc(max_made, 1)
                elif what == "PT":
                    t = i[0]
                    dve.wait_ge(exp_made, QT * b + t + 1)
                    nc.vector.reciprocal(r_total[:, t:t + 1], total[:, t:t + 1]).then_inc(r_total_made, 1)
                    where = (slice(None), slice(None), slice((t % 4) * P, (t % 4 + 1) * P))
                    dve.wait_ge(pt_hi_made, QT * b + t + 1)
                    nc.vector.tensor_tensor(pt_lo[where], ps[:, :].rearrange("p (k q) -> p k q", q=P),
                                            pt_hi[where].bitcast(F32), ALU.subtract).then_inc(pt_lo_made, 1)
                elif what == "PV":
                    m = i[1]
                    dve.wait_ge(o_hi_made, 4 * b + 2 * i[0] + m + 1)
                    where = (slice(None), m, slice(i[0] * CHUNK, (i[0] + 1) * CHUNK))
                    nc.vector.tensor_tensor(q_lo[where], ps[:, m * BANK:(m + 1) * BANK],
                                            q_hi[where].bitcast(F32), ALU.subtract).then_inc(o_lo_made, 1)
                elif what == "O":
                    t = i[0]
                    dve.wait_ge(o_done, QT * b + t + 1)
                    dve.wait_ge(residual_made, QT * b + t + 1)
                    dve.wait_ge(r_total_made, QT * b + t + 1)
                    xt = xr[:, t % 2, :]
                    nc.vector.scalar_tensor_tensor(xt, ps[:, :], r_total[:, t:t + 1], xt, ALU.mult,
                                                   ALU.add).then_inc(x1_made, 1)
                elif what == "picks":
                    wait(dve, pick_done, 2 * (b + 1))
                    if isinstance(b, int) and b < 0:
                        dve.wait_ge(ld_pick, 16)
                    for side in range(2):
                        nc.vector.tensor_scalar(pick_b[:, side, :], pick[:, side, :], picked[:, bass.ds(b + 1, 1)], None,
                                                ALU.mult).then_inc(picks_made, 1)
                elif what == "gates2":
                    wait(dve, row2_done, b + 1)
                    src = modT[:, GB, :, bass.ds(b + 1, 1)].rearrange("p c b -> p (c b)")
                    nc.vector.tensor_copy(gate_col[:, :], src).then_inc(gates2_made, 1)
                    nc.vector.tensor_tensor(row_col[:, :], src, biasT[:, :], ALU.mult).then_inc(gates2_made, 1)
                elif what == "W":
                    n = 8 * (b + 1) + i[0]
                    slot = i[0] % 2
                    dve.wait_ge(lora_done, n + 1)
                    wait(dve, w2_lo_made, n - 1)
                    dve.wait_ge(ld_w2t[slot], 16 * (4 * (b + 1) + i[0] // 2 + 1))
                    nc.vector.tensor_tensor(w_sum[:, slot, :], w2t[:, slot, :], ps[:, :], ALU.add).then_inc(w_sum_made, 1)
                elif what == "W_lo":
                    n = 8 * (b + 1) + i[0]
                    h, cp = i[0] // 4, i[0] % 4
                    where = (slice(None), slice(2 * cp, 2 * cp + 2), slice(None))
                    dve.wait_ge(w2_hi_made, n + 1)
                    nc.vector.tensor_tensor(w2_lo[h][where], w_sum[:, i[0] % 2, :].rearrange("p (c n) -> p c n", c=2),
                                            w2_hi[h][where].bitcast(F32), ALU.subtract).then_inc(w2_lo_made, 1)
                elif what == "F" and i[3] == 3:
                    j, h, p = i[:3]
                    n = f_no(b, j, h, p)
                    slot, batch = 2 * h + p, (b if j else b + 1)
                    dve.wait_ge(f_done, n + 1)
                    dve.wait_ge(gate2_made, batch + 1)
                    wait(dve, y_made, n)
                    gate = gate_bc[:, h * BANK:(h + 1) * BANK].unsqueeze(1).to_broadcast([P, 2, BANK])
                    nc.vector.tensor_tensor(gated[:, :].rearrange("p (t n) -> p t n", t=2),
                                            ps[:, :].rearrange("p (t n) -> p t n", t=2), gate, ALU.mult).then_inc(y_gated, 1)
                    dve.wait_ge(y_gated, n + 1)
                    dve.wait_ge(residual2_made, n + 1)
                    nc.vector.tensor_tensor(res[:, slot, :], res[:, slot, :], gated[:, :], ALU.add).then_inc(y_made, 1)

            nc.vector.memset(scT[:, :, :], 0.0).then_inc(zeroed, 1)
            for entry in FIRST:
                step(entry, -1, 0, (0, -1))
            with dve.Fori(0, B - 1) as b:
                for entry in ATTENTION:
                    step(entry, b, 0, (0, b))
            for entry in LAST_ATTENTION:
                step(entry, LAST, 0, (1, -1))
            with dve.Fori(0, B - 1) as b:
                for entry in SECOND:
                    step(entry, b, 1, (1, b))
            for entry in END:
                step(entry, LAST, 1, (1, LAST))

        @block.tensor
        def _(pe):
            def product3(out, left, right, first, last):
                nc.tensor.matmul(out, left[0], right[0], start=first, stop=False)
                nc.tensor.matmul(out, left[0], right[1], start=False, stop=False)
                return nc.tensor.matmul(out, left[1], right[0], start=False, stop=last)

            def both(hi, lo, *where):
                return hi[(slice(None),) + where], lo[(slice(None),) + where]

            def spread(ps, col, done):
                for ct in range(CT):
                    last = nc.tensor.transpose(ps[:, ct * P:(ct + 1) * P], col[:, ct:ct + 1].to_broadcast([P, P]), ident[:, :])
                last.then_inc(done, 1)

            def step(entry, b, stage, prep):
                if len(entry) < 3:
                    return
                what, i, _, before = entry
                ps = pair[entry[2]]
                wait_emptied(pe, before, b, prep)
                if what in OF_SECOND:
                    b = prep[1]
                if what == "turn_c":
                    pe.wait_ge(ld_const, 32)
                    pe.wait_ge(c_silu, 1)
                    nc.tensor.transpose(ps[:, 0:B * CT], c_rows[:, :], ident[0:B * CT, 0:B * CT]).then_inc(c_turned, 1)
                elif what == "turn_lora":
                    pe.wait_ge(ld_lora, 16 * 2 * (1 + NL))
                    for k in range(CT):
                        last = nc.tensor.transpose(ps[:, k * P:(k + 1) * P], b_raw[:, k, :], ident[:, :])
                    last.then_inc(lora_turned, 1)
                elif what == "mod":
                    if i[0] == 0:
                        pe.wait_ge(c_ready, 1)
                    for k in range(4 * i[2], 4 * i[2] + 4):
                        n = CT * i[0] + k
                        q = 32 * (k % 4)
                        pe.wait_ge(ld_wm[n % WM], 16 * (n // WM + 1))
                        for half in range(2):
                            cols = slice(half * BANK, (half + 1) * BANK)
                            last = nc.tensor.matmul(ps[q:q + 32, cols], scT[:, k, :], wm[:, n % WM, cols],
                                                    start=(k < 4), stop=(k >= 4))
                        last.then_inc(mod_used, 1)
                elif what == "mod_turn":
                    pe.wait_ge(mod_copied, i[0] + 1)
                    for k in range(CT):
                        last = nc.tensor.matmul(ps[:, k * B:(k + 1) * B], mod_rows[:, k * P:(k + 1) * P], sel[:, :],
                                                start=True, stop=True)
                    last.then_inc(mod_turned, 1)
                elif what == "T":
                    j, r, half = i
                    n = turn_no(*prep, *i)
                    pe.wait_ge(x_normed, 2 * round_no(*prep, j, r) + 2)
                    for cc in range(4):
                        for k in range(2):
                            ct = 4 * half + cc
                            last = nc.tensor.transpose(ps[:, (2 * cc + k) * P:(2 * cc + k + 1) * P],
                                                       rows_of(prep, j, r)[:, k, ct * P:(ct + 1) * P], ident[:, :])
                    last.then_inc(h_turned, 1)
                elif what in ("Q", "K", "V"):
                    j = i[0]
                    if what != "V" or j == 1:
                        pe.wait_ge(h_lo_made, 2 * turn_no(0, b, j, 1, 1) + 2)
                    if stage == 0 and isinstance(b, int):
                        pe.wait_ge(w_lo_made, 8)
                    if what == "V":
                        for t in range(2 * i[1], 2 * i[1] + 2):
                            for ct in range(CT):
                                last = product3(ps[:, t * D:(t + 1) * D], both(h_hi[j], h_lo[j], ct, slice(t * P, (t + 1) * P)),
                                                both(w_hi, w_lo, ct, slice(2 * D, 3 * D)), ct == 0, ct == CT - 1)
                        last.then_inc(v_done, 1)
                    else:
                        m = i[1]
                        at = (0 if what == "Q" else D) + m * P
                        for ct in range(CT):
                            last = product3(ps[:, m * BANK:(m + 1) * BANK], both(w_hi, w_lo, ct, slice(at, at + P)),
                                            both(h_hi[j], h_lo[j], ct, slice(None)), ct == 0, ct == CT - 1)
                        last.then_inc(q_done if what == "Q" else k_done, 1)
                elif what == "turn_wo":
                    pe.wait_ge(ld_wo, 16)
                    for ct in range(CT):
                        for d in range(DT):
                            last = nc.tensor.matmul(ps[:, ct:ct + 1], probs[:, d, ct * P:(ct + 1) * P],
                                                    bqkvT[:, 2 * DT + d:2 * DT + d + 1], start=(d == 0), stop=(d == DT - 1))
                    last.then_inc(wo_turned, 1)
                elif what == "gate":
                    pe.wait_ge(gates_made, 2 * (b + 1) + 1)
                    spread(ps, gate_col, gate_done)
                elif what == "row":
                    pe.wait_ge(gates_made, 2 * (b + 1) + 2)
                    spread(ps, row_col, row_done)
                elif what == "S":
                    t = i[0]
                    pe.wait_ge(q_lo_made, 4 * (b + 1))
                    pe.wait_ge(k_lo_made, 4 * (b + 1))
                    for half in range(2):
                        for d in range(DT):
                            last = product3(ps[:, half * BANK:(half + 1) * BANK], both(q_hi, q_lo, d, slice(t * P, (t + 1) * P)),
                                            both(k_hi, k_lo, d, slice(half * BANK, (half + 1) * BANK)), d == 0, d == DT - 1)
                    last.then_inc(s_done, 1)
                elif what == "PT":
                    t = i[0]
                    pe.wait_ge(exp_made, QT * b + t + 1)
                    for k in range(QT):
                        last = nc.tensor.transpose(ps[:, k * P:(k + 1) * P], probs[:, t % 2, k * P:(k + 1) * P], ident[:, :])
                    last.then_inc(pt_done, 1)
                elif what == "PV":
                    pe.wait_ge(v_lo_made, 4 * (b + 1))
                    pe.wait_ge(pt_lo_made, QT * b + 4 * i[0] + 4)
                    m = i[1]
                    for k in range(QT):
                        last = product3(ps[:, m * BANK:(m + 1) * BANK], both(v_hi, v_lo, k, slice(m * P, (m + 1) * P)),
                                        both(pt_hi, pt_lo, k, slice(None)), k == 0, k == QT - 1)
                    last.then_inc(pv_done, 1)
                elif what == "O":
                    t = i[0]
                    pe.wait_ge(o_lo_made, 4 * b + 2 * (t // 4) + 2)
                    pe.wait_ge(wo_lo_made, DT * (b + 1))
                    for half in range(2):
                        cols = slice(half * BANK, (half + 1) * BANK)
                        for d in range(DT):
                            last = product3(ps[:, cols], both(q_hi, q_lo, d, slice(t * P, (t + 1) * P)),
                                            both(wo_hi, wo_lo, d, cols), d == 0, d == DT - 1)
                    last.then_inc(o_done, 1)
                elif what in ("pick_a", "pick_b"):
                    side = 0 if what == "pick_a" else 1
                    pe.wait_ge(picks_made, 2 * (b + 1) + side + 1)
                    for half in range(2):
                        cols = slice(half * BANK, (half + 1) * BANK)
                        last = nc.tensor.matmul(ps[:, cols], pick_b[:, side, :], (a_stack, b_stack)[side][:, cols],
                                                start=True, stop=True)
                    last.then_inc(pick_done, 1)
                elif what == "gate2":
                    pe.wait_ge(gates2_made, 2 * (b + 1) + 1)
                    spread(ps, gate_col, gate2_done)
                elif what == "row2":
                    pe.wait_ge(gates2_made, 2 * (b + 1) + 2)
                    spread(ps, row_col, row2_done)
                elif what == "turn_w":
                    n = i[0]
                    pe.wait_ge(ld_rows[n % 2], 16 * (n // 2 + 1))
                    for cc in range(2):
                        for o in range(4):
                            last = nc.tensor.transpose(ps[:, (4 * cc + o) * P:(4 * cc + o + 1) * P],
                                                       w2_rows[:, n % 2, (2 * o + cc) * P:(2 * o + cc + 1) * P], ident[:, :])
                    last.then_inc(w2_turned, 1)
                elif what == "W":
                    h, cp = i[0] // 4, i[0] % 4
                    pe.wait_ge(picked_made, 2 * (b + 2))
                    for cc in range(2):
                        ct = 2 * cp + cc
                        last = nc.tensor.matmul(ps[:, cc * BANK:(cc + 1) * BANK], a_used[:, ct * P:(ct + 1) * P],
                                                b_used[:, h * BANK:(h + 1) * BANK], start=True, stop=True)
                    last.then_inc(lora_done, 1)
                elif what == "F":
                    j, h, p, s = i
                    batch = b if j else b + 1
                    if s == 0:
                        pe.wait_ge(w2_lo_made, 8 * batch + 4 * h + 4)
                        pe.wait_ge(h_lo_made, 2 * turn_no(1, batch - 1, j, 1, 1) + 2)
                    t = s // 2
                    for ct in range(4 * (s % 2), 4 * (s % 2) + 4):
                        last = product3(ps[:, t * BANK:(t + 1) * BANK],
                                        both(h_hi[j], h_lo[j], ct, slice((2 * p + t) * P, (2 * p + t + 1) * P)),
                                        both(w2_hi[h], w2_lo[h], ct, slice(None)), ct == 0, ct == CT - 1)
                    if s == 3:
                        last.then_inc(f_done, 1)

            for entry in FIRST:
                step(entry, -1, 0, (0, -1))
            with pe.Fori(0, B - 1) as b:
                for entry in ATTENTION:
                    step(entry, b, 0, (0, b))
            for entry in LAST_ATTENTION:
                step(entry, LAST, 0, (1, -1))
            with pe.Fori(0, B - 1) as b:
                for entry in SECOND:
                    step(entry, b, 1, (1, b))
            for entry in END:
                step(entry, LAST, 1, (1, LAST))


_INS = [
    "L0_attn_x", "L0_attn_Wqkv", "L0_attn_bqkv", "L0_attn_Wo", "L0_attn_bo", "L0_ffn_weight", "L0_ffn_bias",
    "L0_ffn_lora_A", "L0_ffn_lora_B", "L0_ffn_lora_start_indices", "L0_c", "L0_wmod",
]


def kernel(**inputs):
    import concourse.bacc as bacc
    from concourse.bass_utils import run_bass_kernel_spmd

    nc = bacc.Bacc("TRN2", target_bir_lowering=False, num_devices=1)
    arrays, args = {}, []

    def give(name, a):
        arrays[f"in_{name}"] = a
        args.append(nc.dram_tensor(f"in_{name}", a.shape, mybir.dt.from_np(a.dtype), kind="ExternalInput").ap())

    for name in _INS:
        a = np.ascontiguousarray(inputs[name])
        if name == "L0_attn_x":
            a = a.reshape(B * S, H)
        elif name == "L0_ffn_lora_start_indices":
            a = a.reshape(1, B)
        give(name, a)
    for name, a in host_constants().items():
        give(name, a)
    out = nc.dram_tensor("out_y", (B * S, H), F32, kind="ExternalOutput").ap()
    build_block(nc, *args, out)
    r = run_bass_kernel_spmd(nc, [arrays], core_ids=[0])
    return r.results[0]["out_y"].reshape(B, S, H)
```
